# Optimizing a Trainium2 kernel written in Bass

```python
import numpy as np
import jax
import jax.numpy as jnp

def _softmax(x, axis=-1):
    return jax.nn.softmax(x, axis=axis)

def _gelu(x):
    return jax.nn.gelu(x, approximate=True)

def _silu(x):
    return jax.nn.silu(x)

def _sigmoid(x):
    return jax.nn.sigmoid(x)

def _layernorm(x, axis=-1, eps=1e-05):
    m = jnp.mean(x, axis=axis, keepdims=True)
    v = jnp.var(x, axis=axis, keepdims=True)
    return (x - m) / jnp.sqrt(v + eps)

def _scatter_add(tgt, idx, src, axis=0):
    return tgt.at[idx].add(src)

def _segment_sum(src, seg, n):
    return jax.ops.segment_sum(src, seg, n)
kernel_name = 'mk_perceiver_d2_seqx_r8_713976'

def setup_inputs(seed: int=0):
    np.random.seed(seed)
    _w = jnp.asarray

    def _rec_inputs():
        import jax
        import jax.numpy as jnp
        _rk = jax.random.key(seed)
        x = -0.0003929 + 0.9999 * jax.random.normal(jax.random.fold_in(_rk, 1), (64, 32, 128), jnp.float32)
        _lenS = 32 - jax.random.randint(jax.random.fold_in(_rk, 7), (64,), 0, max(1, 32 // 4) + 1, jnp.int32)
        _lenS2 = 257 - jax.random.randint(jax.random.fold_in(_rk, 8), (64,), 0, max(1, 257 // 4) + 1, jnp.int32)
        _ctx_512P = jax.random.normal(jax.random.fold_in(_rk, 11), (64, 16, 64), jnp.float32)
        _ctx_512c = jax.random.dirichlet(jax.random.fold_in(_rk, 511), 0.3 * jnp.ones((16,), jnp.float32), (64, 257))
        _ctx_512t = jnp.einsum('bsk,bkd->bsd', _ctx_512c, _ctx_512P)
        _ctx_512t = _ctx_512t * jax.lax.rsqrt(jnp.mean(jnp.square(_ctx_512t)) + 1e-12) * 0.953939
        ctx_512 = -1.39393e-06 + 0.999914 * (_ctx_512t + 0.3 * jax.random.normal(jax.random.fold_in(_rk, 611), (64, 257, 64), jnp.float32))
        return (x, ctx_512)
    x, ctx_512 = _rec_inputs()

    def _L0_xattn_setup():
        import jax, jax.numpy as jnp
        import numpy as np
        HEADS = 16
        D_MODEL = 128
        IMG_MODEL = 64
        D_K = D_MODEL // HEADS
        key = jax.random.key(seed)
        ks = jax.random.split(key, 12)
        B, LQ, LKV = (8, 256, 128)
        s_dm = 1.0 / np.sqrt(D_MODEL)
        s_im = 1.0 / np.sqrt(IMG_MODEL)
        return {'q': jax.random.normal(ks[0], (B, LQ, D_MODEL), jnp.float32), 'k': jax.random.normal(ks[1], (B, LKV, IMG_MODEL), jnp.float32), 'v': jax.random.normal(ks[2], (B, LKV, IMG_MODEL), jnp.float32), 'Wq': jax.random.normal(ks[3], (D_MODEL, D_MODEL), jnp.float32) * s_dm, 'bq': jnp.zeros((D_MODEL,), jnp.float32), 'Wk': jax.random.normal(ks[4], (IMG_MODEL, D_MODEL), jnp.float32) * s_im, 'bk': jnp.zeros((D_MODEL,), jnp.float32), 'Wv': jax.random.normal(ks[5], (IMG_MODEL, D_MODEL), jnp.float32) * s_im, 'bv': jnp.zeros((D_MODEL,), jnp.float32), 'Wo': jax.random.normal(ks[6], (D_MODEL, D_MODEL), jnp.float32) * s_dm, 'bo': jnp.zeros((D_MODEL,), jnp.float32)}
    _L0_xattn_all = _L0_xattn_setup()
    _L0_xattn_in = {k: v for k, v in _L0_xattn_all.items() if k in ('Wq', 'bq', 'Wk', 'bk', 'Wv', 'bv', 'Wo', 'bo')}
    del _L0_xattn_all

    def _L0_attn_setup():
        import jax, jax.numpy as jnp
        import numpy as np
        D_MODEL = 128
        N_HEADS = 16
        D_HEAD = 64
        VAR_EPS = 1e-05
        INIT_RANGE = 0.02
        B, S = (2, 256)

        def _layernorm(x, w, b):
            mean = jnp.mean(x, axis=-1, keepdims=True)
            var = jnp.var(x, axis=-1, keepdims=True)
            norm = (x - mean) / jnp.sqrt(var + VAR_EPS)
            return norm * w + b
        key = jax.random.key(seed)
        ks = jax.random.split(key, 6)
        resid_stream = jax.random.normal(ks[0], (B, S, D_MODEL), dtype=jnp.float32)
        attn_mask = jnp.ones((B, S), dtype=jnp.int32)
        W_q = jax.random.normal(ks[1], (N_HEADS, D_MODEL, D_HEAD), dtype=jnp.float32) * INIT_RANGE
        W_k = jax.random.normal(ks[2], (N_HEADS, D_MODEL, D_HEAD), dtype=jnp.float32) * INIT_RANGE
        W_v = jax.random.normal(ks[3], (N_HEADS, D_MODEL, D_HEAD), dtype=jnp.float32) * INIT_RANGE
        W_o = jax.random.normal(ks[4], (N_HEADS, D_HEAD, D_MODEL), dtype=jnp.float32) * INIT_RANGE
        b_q = jnp.zeros((N_HEADS, D_HEAD), dtype=jnp.float32)
        b_k = jnp.zeros((N_HEADS, D_HEAD), dtype=jnp.float32)
        b_v = jnp.zeros((N_HEADS, D_HEAD), dtype=jnp.float32)
        b_o = jnp.zeros((D_MODEL,), dtype=jnp.float32)
        ln_w = jnp.ones((D_MODEL,), dtype=jnp.float32)
        ln_b = jnp.zeros((D_MODEL,), dtype=jnp.float32)
        return dict(resid_stream=resid_stream, attn_mask=attn_mask, W_q=W_q, W_k=W_k, W_v=W_v, W_o=W_o, b_q=b_q, b_k=b_k, b_v=b_v, b_o=b_o, ln_w=ln_w, ln_b=ln_b)
    _L0_attn_all = _L0_attn_setup()
    _L0_attn_in = {k: v for k, v in _L0_attn_all.items() if k in ('attn_mask', 'W_q', 'W_k', 'W_v', 'W_o', 'b_q', 'b_k', 'b_v', 'b_o', 'ln_w', 'ln_b')}
    del _L0_attn_all

    def _L0_ffn_setup():
        import jax, jax.numpy as jnp
        import numpy as np
        B, T, C, I, E = (4, 256, 128, 352, 7)

        def _swiglu(h, w1, w2, w3):
            return jax.nn.silu(h @ w1.T) * (h @ w3.T) @ w2.T
        key = jax.random.key(seed)
        ks = jax.random.split(key, 9)
        sc_c = 1.0 / np.sqrt(C)
        sc_i = 1.0 / np.sqrt(I)
        return {'x': jax.random.normal(ks[0], (B, T, C), jnp.float32), 'router_w': jax.random.normal(ks[1], (E, C), jnp.float32) * sc_c, 'routing_bias': jnp.zeros((E,), jnp.float32), 'sw1': jax.random.normal(ks[2], (I, C), jnp.float32) * sc_c, 'sw2': jax.random.normal(ks[3], (C, I), jnp.float32) * sc_i, 'sw3': jax.random.normal(ks[4], (I, C), jnp.float32) * sc_c, 'ew1': jax.random.normal(ks[5], (E, I, C), jnp.float32) * sc_c, 'ew2': jax.random.normal(ks[6], (E, C, I), jnp.float32) * sc_i, 'ew3': jax.random.normal(ks[7], (E, I, C), jnp.float32) * sc_c}
    _L0_ffn_all = _L0_ffn_setup()
    _L0_ffn_in = {k: v for k, v in _L0_ffn_all.items() if k in ('router_w', 'routing_bias', 'sw1', 'sw2', 'sw3', 'ew1', 'ew2', 'ew3')}
    del _L0_ffn_all

    def _L1_xattn_setup():
        import jax, jax.numpy as jnp
        import numpy as np
        DIM = 128
        LATENT_DIM = 64
        NUM_HEADS = 16
        HEAD_DIM = DIM // NUM_HEADS
        SCALE = HEAD_DIM ** (-0.5)
        key = jax.random.key(seed)
        k1, k2, k3, k4, k5 = jax.random.split(key, 5)
        B, xN, zN = (2, 256, 256)
        x = jax.random.normal(k1, (B, xN, DIM), dtype=jnp.float32)
        z = jax.random.normal(k2, (B, zN, LATENT_DIM), dtype=jnp.float32)
        Wq = jax.random.normal(k3, (DIM, DIM), dtype=jnp.float32) * DIM ** (-0.5)
        Wkv = jax.random.normal(k4, (2 * DIM, LATENT_DIM), dtype=jnp.float32) * LATENT_DIM ** (-0.5)
        Wo = jax.random.normal(k5, (DIM, DIM), dtype=jnp.float32) * DIM ** (-0.5)
        return {'x': x, 'z': z, 'Wq': Wq, 'Wkv': Wkv, 'Wo': Wo}
    _L1_xattn_all = _L1_xattn_setup()
    _L1_xattn_in = {k: v for k, v in _L1_xattn_all.items() if k in ('Wq', 'Wkv', 'Wo')}
    del _L1_xattn_all

    def _L1_attn_setup():
        import jax, jax.numpy as jnp
        import numpy as np
        D_MODEL = 128
        IDX_HEADS = 4
        IDX_DIM = 64
        TOP_K = 32

        def _rope(x):
            B, S, D = x.shape
            half = D // 2
            inv_freq = 1.0 / 10000.0 ** (jnp.arange(half, dtype=jnp.float32) / half)
            ang = jnp.arange(S, dtype=jnp.float32)[:, None] * inv_freq[None, :]
            cos, sin = (jnp.cos(ang), jnp.sin(ang))
            x1, x2 = (x[..., :half], x[..., half:])
            return jnp.concatenate([x1 * cos - x2 * sin, x1 * sin + x2 * cos], axis=-1)
        key = jax.random.key(seed)
        ks = jax.random.split(key, 11)
        B, S, D = (2, 512, D_MODEL)
        s = 0.02
        return {'x': jax.random.normal(ks[0], (B, S, D), dtype=jnp.float32), 'w_qkv': jax.random.normal(ks[1], (3 * D, D), dtype=jnp.float32) * s, 'b_qkv': jnp.zeros((3 * D,), dtype=jnp.float32), 'w_o': jax.random.normal(ks[2], (D, D), dtype=jnp.float32) * s, 'b_o': jnp.zeros((D,), dtype=jnp.float32), 'w_iq': jax.random.normal(ks[3], (IDX_HEADS * IDX_DIM, D), dtype=jnp.float32) * s, 'b_iq': jnp.zeros((IDX_HEADS * IDX_DIM,), dtype=jnp.float32), 'w_ik': jax.random.normal(ks[4], (IDX_DIM, D), dtype=jnp.float32) * s, 'b_ik': jnp.zeros((IDX_DIM,), dtype=jnp.float32), 'w_iw': jax.random.normal(ks[5], (IDX_HEADS, D), dtype=jnp.float32) * s, 'b_iw': jnp.zeros((IDX_HEADS,), dtype=jnp.float32)}
    _L1_attn_all = _L1_attn_setup()
    _L1_attn_in = {k: v for k, v in _L1_attn_all.items() if k in ('w_qkv', 'b_qkv', 'w_o', 'b_o', 'w_iq', 'b_iq', 'w_ik', 'b_ik', 'w_iw', 'b_iw')}
    del _L1_attn_all

    def _L1_ffn_setup():
        import jax, jax.numpy as jnp
        import numpy as np
        TOP_K = 2
        ROUTE_SCALE = 1.0
        EPS = 1e-20
        key = jax.random.key(seed)
        ks = jax.random.split(key, 8)
        dim, hid, E, X = (128, 352, 8, 1)
        std = 0.02
        x = jax.random.normal(ks[0], (2, 256, dim), dtype=jnp.float32)
        w1 = jax.random.normal(ks[1], (E, hid, dim), dtype=jnp.float32) * std
        w2 = jax.random.normal(ks[2], (E, dim, hid), dtype=jnp.float32) * std
        w3 = jax.random.normal(ks[3], (E, hid, dim), dtype=jnp.float32) * std
        new_w1 = jax.random.normal(ks[4], (X, hid, dim), dtype=jnp.float32) * std
        new_w2 = jnp.zeros((X, dim, hid), dtype=jnp.float32)
        new_w3 = jax.random.normal(ks[5], (X, hid, dim), dtype=jnp.float32) * std
        gate_weight = jax.random.normal(ks[6], (E, dim), dtype=jnp.float32) * std
        new_gate_weight = jax.random.normal(ks[7], (X, dim), dtype=jnp.float32) * std
        gate_bias = jnp.zeros((X,), dtype=jnp.float32)
        return dict(x=x, w1=w1, w2=w2, w3=w3, new_w1=new_w1, new_w2=new_w2, new_w3=new_w3, gate_weight=gate_weight, new_gate_weight=new_gate_weight, gate_bias=gate_bias)
    _L1_ffn_all = _L1_ffn_setup()
    _L1_ffn_in = {k: v for k, v in _L1_ffn_all.items() if k in ('w1', 'w2', 'w3', 'new_w1', 'new_w2', 'new_w3', 'gate_weight', 'new_gate_weight', 'gate_bias')}
    del _L1_ffn_all
    return {'x': x, 'ctx_512': ctx_512, 'L0_xattn_Wq': _L0_xattn_in['Wq'], 'L0_xattn_bq': _L0_xattn_in['bq'], 'L0_xattn_Wk': _L0_xattn_in['Wk'], 'L0_xattn_bk': _L0_xattn_in['bk'], 'L0_xattn_Wv': _L0_xattn_in['Wv'], 'L0_xattn_bv': _L0_xattn_in['bv'], 'L0_xattn_Wo': _L0_xattn_in['Wo'], 'L0_xattn_bo': _L0_xattn_in['bo'], 'L0_attn_attn_mask': _L0_attn_in['attn_mask'], 'L0_attn_W_q': _L0_attn_in['W_q'], 'L0_attn_W_k': _L0_attn_in['W_k'], 'L0_attn_W_v': _L0_attn_in['W_v'], 'L0_attn_W_o': _L0_attn_in['W_o'], 'L0_attn_b_q': _L0_attn_in['b_q'], 'L0_attn_b_k': _L0_attn_in['b_k'], 'L0_attn_b_v': _L0_attn_in['b_v'], 'L0_attn_b_o': _L0_attn_in['b_o'], 'L0_attn_ln_w': _L0_attn_in['ln_w'], 'L0_attn_ln_b': _L0_attn_in['ln_b'], 'L0_ffn_router_w': _L0_ffn_in['router_w'], 'L0_ffn_routing_bias': _L0_ffn_in['routing_bias'], 'L0_ffn_sw1': _L0_ffn_in['sw1'], 'L0_ffn_sw2': _L0_ffn_in['sw2'], 'L0_ffn_sw3': _L0_ffn_in['sw3'], 'L0_ffn_ew1': _L0_ffn_in['ew1'], 'L0_ffn_ew2': _L0_ffn_in['ew2'], 'L0_ffn_ew3': _L0_ffn_in['ew3'], 'L1_xattn_Wq': _L1_xattn_in['Wq'], 'L1_xattn_Wkv': _L1_xattn_in['Wkv'], 'L1_xattn_Wo': _L1_xattn_in['Wo'], 'L1_attn_w_qkv': _L1_attn_in['w_qkv'], 'L1_attn_b_qkv': _L1_attn_in['b_qkv'], 'L1_attn_w_o': _L1_attn_in['w_o'], 'L1_attn_b_o': _L1_attn_in['b_o'], 'L1_attn_w_iq': _L1_attn_in['w_iq'], 'L1_attn_b_iq': _L1_attn_in['b_iq'], 'L1_attn_w_ik': _L1_attn_in['w_ik'], 'L1_attn_b_ik': _L1_attn_in['b_ik'], 'L1_attn_w_iw': _L1_attn_in['w_iw'], 'L1_attn_b_iw': _L1_attn_in['b_iw'], 'L1_ffn_w1': _L1_ffn_in['w1'], 'L1_ffn_w2': _L1_ffn_in['w2'], 'L1_ffn_w3': _L1_ffn_in['w3'], 'L1_ffn_new_w1': _L1_ffn_in['new_w1'], 'L1_ffn_new_w2': _L1_ffn_in['new_w2'], 'L1_ffn_new_w3': _L1_ffn_in['new_w3'], 'L1_ffn_gate_weight': _L1_ffn_in['gate_weight'], 'L1_ffn_new_gate_weight': _L1_ffn_in['new_gate_weight'], 'L1_ffn_gate_bias': _L1_ffn_in['gate_bias']}

def reference(x, ctx_512, L0_xattn_Wq, L0_xattn_bq, L0_xattn_Wk, L0_xattn_bk, L0_xattn_Wv, L0_xattn_bv, L0_xattn_Wo, L0_xattn_bo, L0_attn_attn_mask, L0_attn_W_q, L0_attn_W_k, L0_attn_W_v, L0_attn_W_o, L0_attn_b_q, L0_attn_b_k, L0_attn_b_v, L0_attn_b_o, L0_attn_ln_w, L0_attn_ln_b, L0_ffn_router_w, L0_ffn_routing_bias, L0_ffn_sw1, L0_ffn_sw2, L0_ffn_sw3, L0_ffn_ew1, L0_ffn_ew2, L0_ffn_ew3, L1_xattn_Wq, L1_xattn_Wkv, L1_xattn_Wo, L1_attn_w_qkv, L1_attn_b_qkv, L1_attn_w_o, L1_attn_b_o, L1_attn_w_iq, L1_attn_b_iq, L1_attn_w_ik, L1_attn_b_ik, L1_attn_w_iw, L1_attn_b_iw, L1_ffn_w1, L1_ffn_w2, L1_ffn_w3, L1_ffn_new_w1, L1_ffn_new_w2, L1_ffn_new_w3, L1_ffn_gate_weight, L1_ffn_new_gate_weight, L1_ffn_gate_bias):
    import jax
    import jax.numpy as jnp

    def _L0_xattn_ref(q, k, v, Wq, bq, Wk, bk, Wv, bv, Wo, bo):
        import jax, jax.numpy as jnp
        import numpy as np
        HEADS = 16
        D_MODEL = 128
        IMG_MODEL = 64
        D_K = D_MODEL // HEADS
        B, LQ, _ = q.shape
        LKV = k.shape[1]
        qh = (q @ Wq + bq).reshape(B, LQ, HEADS, D_K).transpose(0, 2, 1, 3)
        kh = (k @ Wk + bk).reshape(B, LKV, HEADS, D_K).transpose(0, 2, 1, 3)
        vh = (v @ Wv + bv).reshape(B, LKV, HEADS, D_K).transpose(0, 2, 1, 3)
        scale = 1.0 / np.sqrt(D_K)
        scores = jnp.einsum('bhqd,bhkd->bhqk', qh, kh) * scale
        attn = jax.nn.softmax(scores, axis=-1)
        out = jnp.einsum('bhqk,bhkd->bhqd', attn, vh)
        concat = out.transpose(0, 2, 1, 3).reshape(B, LQ, D_MODEL)
        return concat @ Wo + bo

    def _L0_attn_ref(resid_stream, attn_mask, W_q, W_k, W_v, W_o, b_q, b_k, b_v, b_o, ln_w, ln_b):
        import jax, jax.numpy as jnp
        import numpy as np
        D_MODEL = 128
        N_HEADS = 16
        D_HEAD = 64
        VAR_EPS = 1e-05
        INIT_RANGE = 0.02
        B, S = (2, 256)

        def _layernorm(x, w, b):
            mean = jnp.mean(x, axis=-1, keepdims=True)
            var = jnp.var(x, axis=-1, keepdims=True)
            norm = (x - mean) / jnp.sqrt(var + VAR_EPS)
            return norm * w + b
        x = _layernorm(resid_stream, ln_w, ln_b)
        q = jnp.einsum('bsd,hde->bshe', x, W_q) + b_q
        k = jnp.einsum('bsd,hde->bshe', x, W_k) + b_k
        v = jnp.einsum('bsd,hde->bshe', x, W_v) + b_v
        scale = D_HEAD ** (-0.5)
        scores = jnp.einsum('bqhe,bkhe->bhqk', q, k) * scale
        sq, sk = (scores.shape[-2], scores.shape[-1])
        causal = jnp.tril(jnp.ones((sq, sk), dtype=bool))
        scores = jnp.where(causal, scores, -jnp.inf)
        pattern = jax.nn.softmax(scores, axis=-1)
        z = jnp.einsum('bhqk,bkhe->bqhe', pattern, v)
        attn_out = jnp.einsum('bqhe,hed->bqd', z, W_o) + b_o
        return attn_out

    def _L0_ffn_ref(x, router_w, routing_bias, sw1, sw2, sw3, ew1, ew2, ew3):
        import jax, jax.numpy as jnp
        import numpy as np
        B, T, C, I, E = (4, 256, 128, 352, 7)

        def _swiglu(h, w1, w2, w3):
            return jax.nn.silu(h @ w1.T) * (h @ w3.T) @ w2.T
        b, t, c = x.shape
        shared_out = _swiglu(x, sw1, sw2, sw3)
        logits = jnp.clip(x @ router_w.T + routing_bias, -50.0, 50.0)
        probs = jax.nn.sigmoid(logits)
        num_switched = 1
        topk_probs, topk_idx = jax.lax.top_k(probs, num_switched)
        topk_probs = jnp.clip(topk_probs, 1e-08, 1.0 - 1e-08)
        xf = x.reshape(-1, c)
        sel = topk_idx.reshape(-1)
        p = topk_probs.reshape(-1)
        switched = jnp.zeros_like(xf)
        n_experts = ew1.shape[0]
        for e in range(n_experts):
            y = _swiglu(xf, ew1[e], ew2[e], ew3[e])
            w = jnp.where(sel == e, p, 0.0)
            switched = switched + w[:, None] * y
        switched = switched.reshape(b, t, c)
        total_weight = 0.5 + topk_probs.sum(axis=-1)
        total_weight = jnp.clip(total_weight[..., None] + 1e-08, 0.5, 2.0)
        return 0.5 / total_weight * shared_out + switched / total_weight

    def _L1_xattn_ref(x, z, Wq, Wkv, Wo):
        import jax, jax.numpy as jnp
        import numpy as np
        DIM = 128
        LATENT_DIM = 64
        NUM_HEADS = 16
        HEAD_DIM = DIM // NUM_HEADS
        SCALE = HEAD_DIM ** (-0.5)
        B, xN, _ = x.shape
        _, zN, _ = z.shape
        Q = (x @ Wq.T).reshape(B, xN, NUM_HEADS, HEAD_DIM)
        KV = (z @ Wkv.T).reshape(B, zN, 2, NUM_HEADS, HEAD_DIM)
        K = KV[:, :, 0]
        V = KV[:, :, 1]
        attn = jnp.einsum('bqhd,bkhd->bhqk', Q, K) * SCALE
        attn = jax.nn.softmax(attn, axis=-1)
        O = jnp.einsum('bhqk,bkhd->bqhd', attn, V).reshape(B, xN, DIM)
        return O @ Wo.T

    def _L1_attn_ref(x, w_qkv, b_qkv, w_o, b_o, w_iq, b_iq, w_ik, b_ik, w_iw, b_iw):
        import jax, jax.numpy as jnp
        import numpy as np
        D_MODEL = 128
        IDX_HEADS = 4
        IDX_DIM = 64
        TOP_K = 32

        def _rope(x):
            B, S, D = x.shape
            half = D // 2
            inv_freq = 1.0 / 10000.0 ** (jnp.arange(half, dtype=jnp.float32) / half)
            ang = jnp.arange(S, dtype=jnp.float32)[:, None] * inv_freq[None, :]
            cos, sin = (jnp.cos(ang), jnp.sin(ang))
            x1, x2 = (x[..., :half], x[..., half:])
            return jnp.concatenate([x1 * cos - x2 * sin, x1 * sin + x2 * cos], axis=-1)
        B, S, D = x.shape
        qkv = x @ w_qkv.T + b_qkv
        Q, K, V = jnp.split(qkv, 3, axis=-1)
        Q, K = (_rope(Q), _rope(K))
        iq = (x @ w_iq.T + b_iq).reshape(B, S, IDX_HEADS, IDX_DIM)
        ik = x @ w_ik.T + b_ik
        iw = x @ w_iw.T + b_iw
        head_scores = jax.nn.relu(jnp.einsum('bqhd,bkd->bhqk', iq, ik))
        index_scores = jnp.einsum('bhqk,bqh->bqk', head_scores, iw)
        k = min(TOP_K, S)
        _, top_idx = jax.lax.top_k(index_scores, k)
        mask = jnp.zeros((B, S, S), dtype=bool)
        mask = mask.at[jnp.arange(B)[:, None, None], jnp.arange(S)[None, :, None], top_idx].set(True)
        attn_bias = jnp.where(mask, 0.0, -jnp.inf)
        scale = 1.0 / np.sqrt(D).astype(np.float32)
        logits = jnp.einsum('bqd,bkd->bqk', Q, K) * scale + attn_bias
        attn = jax.nn.softmax(logits, axis=-1)
        attn_out = jnp.einsum('bqk,bkd->bqd', attn, V)
        return attn_out @ w_o.T + b_o

    def _L1_ffn_ref(x, w1, w2, w3, new_w1, new_w2, new_w3, gate_weight, new_gate_weight, gate_bias):
        import jax, jax.numpy as jnp
        import numpy as np
        TOP_K = 2
        ROUTE_SCALE = 1.0
        EPS = 1e-20
        bs, slen, dim = x.shape
        x_flat = x.reshape(-1, dim)
        ew1 = jnp.concatenate([w1, new_w1], axis=0)
        ew2 = jnp.concatenate([w2, new_w2], axis=0)
        ew3 = jnp.concatenate([w3, new_w3], axis=0)
        gate = jnp.concatenate([gate_weight, new_gate_weight], axis=0)
        e_orig = w1.shape[0]
        e_tot = gate.shape[0]
        bias = jnp.concatenate([jnp.zeros((e_orig,), x.dtype), gate_bias])
        scores = jax.nn.sigmoid((x_flat @ gate.T + bias).astype(jnp.float32))
        top_scores, selected = jax.lax.top_k(scores, TOP_K)
        top_scores = top_scores / (jnp.sum(top_scores, axis=-1, keepdims=True) + EPS)
        top_scores = top_scores * ROUTE_SCALE
        onehot = jax.nn.one_hot(selected, e_tot, dtype=jnp.float32)
        cw = jnp.einsum('tk,tke->te', top_scores, onehot)
        out = jnp.zeros_like(x_flat)
        for e in range(e_tot):
            h = jax.nn.silu(x_flat @ ew1[e].T) * (x_flat @ ew3[e].T)
            out = out + cw[:, e:e + 1] * (h @ ew2[e].T)
        return out.reshape(bs, slen, dim)
    x = x + _L0_xattn_ref(_layernorm(x, axis=-1), ctx_512, ctx_512, L0_xattn_Wq, L0_xattn_bq, L0_xattn_Wk, L0_xattn_bk, L0_xattn_Wv, L0_xattn_bv, L0_xattn_Wo, L0_xattn_bo)
    x = x + _L0_attn_ref(_layernorm(x, axis=-1), L0_attn_attn_mask, L0_attn_W_q, L0_attn_W_k, L0_attn_W_v, L0_attn_W_o, L0_attn_b_q, L0_attn_b_k, L0_attn_b_v, L0_attn_b_o, L0_attn_ln_w, L0_attn_ln_b)
    x = x + _L0_ffn_ref(_layernorm(x, axis=-1), L0_ffn_router_w, L0_ffn_routing_bias, L0_ffn_sw1, L0_ffn_sw2, L0_ffn_sw3, L0_ffn_ew1, L0_ffn_ew2, L0_ffn_ew3)
    x = x + _L1_xattn_ref(_layernorm(x, axis=-1), ctx_512, L1_xattn_Wq, L1_xattn_Wkv, L1_xattn_Wo)
    x = x + _L1_attn_ref(_layernorm(x, axis=-1), L1_attn_w_qkv, L1_attn_b_qkv, L1_attn_w_o, L1_attn_b_o, L1_attn_w_iq, L1_attn_b_iq, L1_attn_w_ik, L1_attn_b_ik, L1_attn_w_iw, L1_attn_b_iw)
    x = x + _L1_ffn_ref(_layernorm(x, axis=-1), L1_ffn_w1, L1_ffn_w2, L1_ffn_w3, L1_ffn_new_w1, L1_ffn_new_w2, L1_ffn_new_w3, L1_ffn_gate_weight, L1_ffn_new_gate_weight, L1_ffn_gate_bias)
    return x

_drawn_inputs = setup_inputs


def setup_inputs(seed=0):
    import zlib

    import numpy as np

    out = dict(_drawn_inputs(seed))
    spreads = {'L0_xattn_bq': (0.0, 0.1),
     'L0_xattn_bk': (0.0, 0.8),
     'L0_xattn_bv': (0.0, 0.1),
     'L0_xattn_bo': (0.0, 0.1),
     'L0_attn_b_q': (0.0, 0.547),
     'L0_attn_b_k': (0.0, 0.8),
     'L0_attn_b_v': (0.0, 0.1),
     'L0_attn_b_o': (0.0, 0.1),
     'L0_attn_ln_w': (1.0, 0.2),
     'L0_attn_ln_b': (0.0, 0.1),
     'L0_ffn_routing_bias': (0.0, 0.1),
     'L1_attn_b_qkv': (0.0, 0.454),
     'L1_attn_b_o': (0.0, 0.1),
     'L1_attn_b_iq': (0.0, 0.1),
     'L1_attn_b_ik': (0.0, 0.1),
     'L1_attn_b_iw': (0.0, 0.1),
     'L1_ffn_new_w2': (0.0, 0.8)}
    factors = {'L0_attn_W_q': 3.095,
     'L0_attn_W_k': 4.352,
     'L1_ffn_w1': 8.0,
     'L1_ffn_w2': 8.0,
     'L1_ffn_w3': 8.0,
     'L1_ffn_new_w1': 8.0,
     'L1_ffn_new_w3': 8.0,
     'L1_ffn_gate_weight': 8.0,
     'L1_ffn_new_gate_weight': 8.0}
    for name, (base, spread) in spreads.items():
        noise = np.random.default_rng([zlib.crc32(name.encode()), seed]).standard_normal(out[name].shape)
        drawn = base * np.exp(spread * noise) if base else spread * noise
        out[name] = jnp.asarray(drawn.astype(out[name].dtype))
    for name, factor in factors.items():
        out[name] = (out[name] * factor).astype(out[name].dtype)
    return out
```

```python
import concourse.bass as bass
from concourse import mybir
from contextlib import ExitStack

F32 = mybir.dt.float32
F32R = mybir.dt.float32r
ALU = mybir.AluOpType
ACT = mybir.ActivationFunctionType
AX = mybir.AxisListType

P = 128
D = 128
B, S = 64, 32
T = B * S // P
BT = P // S
KV = 257
KVP = 258
CW = 64
H, DH = 16, 8
G, J = 4, 4
EPS = 1e-5


def wait(eng, sem, value):
    if not isinstance(value, int) or value > 0:
        eng.wait_ge(sem, value)


class Chain:

    def __init__(self, eng, sem, base=0):
        self.eng, self.sem, self.base, self.n = eng, sem, base, 0

    def then(self, ins):
        self.n += 1
        ins.then_inc(self.sem, 1)
        self.eng.wait_ge(self.sem, self.base + self.n)


def layernorm_stage(nc, cx, name, X, XNT, ident, twice=None):
    sem = lambda n: cx.enter_context(nc.semaphore(f"{name}_{n}"))
    var_ready, rstd_ready, xn_ready, xt_ready, xt_copied, step = (
        sem(n) for n in ("var_ready", "rstd_ready", "xn_ready", "xt_ready", "xt_copied", "step"))
    NB = 4
    rounds = 2 if twice else 1
    with ExitStack() as mem:
        sb = lambda n, s, d=F32: mem.enter_context(nc.sbuf_tensor(f"{name}_{n}", s, d))
        stats = sb("stats", [P, T, 6])
        mv = sb("mv", [P, T, 2])
        rvar = sb("rvar", [P, T])
        rstd = sb("rstd", [P, T])
        XN = sb("xn", [P, T, D])
        xt_ps = [mem.enter_context(nc.psum_tensor(f"{name}_xt{n}", [P, NB * P], F32)) for n in range(T // NB)]
        block = mem.enter_context(nc.Block())

        @block.vector
        def _(dve):
            chain = Chain(dve, step)
            for r in range(rounds):
                src = X if r == 0 else XN
                for t in range(T):
                    last = nc.vector.bn_stats(stats[:, t, :], src[:, t, :])
                chain.then(last)
                for t in range(T):
                    last = nc.vector.bn_aggr(mv[:, t, :], stats[:, t, :])
                chain.then(last)
                chain.then(nc.vector.tensor_scalar_add(rvar[:, :], mv[:, :, 1], EPS))
                nc.vector.reciprocal(rvar[:, :], rvar[:, :]).then_inc(var_ready, 1)
                dve.wait_ge(rstd_ready, r + 1)
                for t in range(T):
                    last = nc.vector.tensor_scalar(XN[:, t, :], src[:, t, :], mv[:, t, 0:1], rstd[:, t:t + 1],
                                                   ALU.subtract, ALU.mult)
                    if r < rounds - 1:
                        if t == T - 1:
                            chain.then(last)
                    elif t % NB == NB - 1:
                        last.then_inc(xn_ready, 1)

        @block.scalar
        def _(act):
            for r in range(rounds):
                act.wait_ge(var_ready, r + 1)
                nc.scalar.activation(rstd[:, :], rvar[:, :], ACT.Sqrt).then_inc(rstd_ready, 1)
            for n in range(T // NB):
                act.wait_ge(xt_ready, n + 1)
                w, b = twice or (1.0, 0.0)
                nc.scalar.activation(XNT[:, n * NB * P:(n + 1) * NB * P], xt_ps[n][:, :], ACT.Identity,
                                     bias=b, scale=w).then_inc(xt_copied, 1)

        @block.tensor
        def _(pe):
            for n in range(T // NB):
                pe.wait_ge(xn_ready, n + 1)
                for k in range(NB):
                    last = nc.tensor.transpose(xt_ps[n][:, k * P:(k + 1) * P], XN[:, n * NB + k, :], ident[:, :])
                last.then_inc(xt_ready, 1)


def cross_attention(nc, cx, name, X, XNT, con, W):
    ds = bass.ds
    sem = lambda n: cx.enter_context(nc.semaphore(f"{name}_{n}"))
    names = ("w_loaded", "ctx_loaded", "w_split", "ctx_split", "q_mm", "q_ready", "qbd_ready", "pair_scored",
             "max_ready", "exp_done", "p_transposed", "rsum_ready", "spread_ready", "rl_done", "concat_step",
             "concat_ready", "out_mm", "x_updated", "k_mm", "k_ready", "v_mm", "v_copied", "v256_ready",
             "v_ready", "xb_ready", "zeroed")
    s = {n: sem(n) for n in names}
    SCALE = DH ** -0.5
    biased = W["bias"] is not None
    KB = 256 // 32
    with ExitStack() as mem:
        sb = lambda n, sh, d=F32: mem.enter_context(nc.sbuf_tensor(f"{name}_{n}", sh, d))
        ps = lambda n, sh: mem.enter_context(nc.psum_tensor(f"{name}_{n}", sh, F32))
        wq, wo = sb("wq", [P, D]), sb("wo", [P, D])
        wraw = sb("wraw", [P, 3, D])
        whi, wlo = sb("whi", [P, 3, D], F32R), sb("wlo", [P, 3, D], F32R)
        bias = sb("bias", [P, 4])
        bo = sb("bo", [P, D])
        ctx_raw = sb("ctx_raw", [P, BT, KVP])
        ctx_hl = sb("ctx_hl", [P, BT, KVP], F32R)
        zero = sb("zero", [P, 1])
        QT = sb("qt", [P, T * P])
        qbd = [sb(f"qbd{n}", [P, BT, J * G, S]) for n in range(2)]
        KT = [sb(f"kt{n}", [P, BT, KVP]) for n in range(2)]
        VT = sb("vt", [P, BT, 256])
        VB = [sb(f"vb{n}", [P, BT * KB, J, G, DH]) for n in range(2)]
        v256 = [sb(f"v256{n}", [P, BT]) for n in range(2)]
        probs = [sb(f"probs{n}", [P, J, KV]) for n in range(2)]
        probsT = [sb(f"probsT{n}", [P, J, 256]) for n in range(2)]
        nmax = [sb(f"nmax{n}", [P, J]) for n in range(2)]
        sums = [sb(f"sums{n}", [P, J]) for n in range(2)]
        rsum = [sb(f"rsum{n}", [P, J]) for n in range(2)]
        spread = [sb(f"spread{n}", [P, 2, J, G, DH]) for n in range(2)]
        cc = sb("cc", [P, 3, P])
        sc = [ps(f"sc{n}", [P, 2, 512]) for n in range(2)]
        pj = [ps(f"pj{n}", [P, 512]) for n in range(2)]
        oacc = ps("oacc", [P, 512])
        oacc_v = oacc[:, 0:128]
        oacc_last = oacc[:, 128:256]
        oacc_rsum = oacc[:, 256:384]
        xo = ps("xo", [P, 512])
        block = mem.enter_context(nc.Block())

        def tiles(eng, tile):
            tile(0, 0, True, False)
            tile(1, 1, False, False)
            with eng.Fori(1, T // 2 - 1) as i:
                tile(2 * i, 0, False, False)
                tile(2 * i + 1, 1, False, False)
            tile(T - 2, 0, False, False)
            tile(T - 1, 1, False, True)

        @block.sync
        def _(sp):
            n = 0
            for dst, src in ((wq[:, :], W["wq"]), (wo[:, :], W["wo"]), (wraw[:, :, :], W["wkvv"]),
                             (bias[:, :], W["bias"]), (bo[:, :], W["bo"])):
                if src is not None:
                    sp.dma_start(dst, src).then_inc(s["w_loaded"], 16)

            def load(t):
                wait(sp, s["ctx_split"], 2 * t)
                for half in range(2):
                    sp.dma_start(ctx_raw[half * CW:(half + 1) * CW, :, :],
                                 W["ctx"][:, ds(BT * t, BT), :]).then_inc(s["ctx_loaded"], 16)
            load(0)
            load(1)
            with sp.Fori(2, T) as t:
                load(t)
        nw = 16 * (5 if biased else 3)

        @block.gpsimd
        def _(pool):
            for n in range(2):
                nc.gpsimd.memset(VB[n][:, :, :, :, :], 0.0).then_inc(s["zeroed"], 1)
            nc.gpsimd.memset(zero[:, :], 0.0).then_inc(s["zeroed"], 1)
            pool.wait_ge(s["w_loaded"], nw)
            pool.wait_ge(s["zeroed"], 3)
            nc.gpsimd.tensor_copy(whi[:, :, :], wraw[:, :, :]).then_inc(s["w_split"], 1)
            pool.wait_ge(s["w_split"], 1)
            nc.gpsimd.tensor_tensor(wlo[:, :, :], wraw[:, :, :], whi[:, :, :].bitcast(F32),
                                    ALU.subtract).then_inc(s["w_split"], 1)

            def split(t):
                pool.wait_ge(s["ctx_loaded"], 32 * t + 32)
                wait(pool, s["v_mm"], 4 * t)
                nc.gpsimd.tensor_tensor(ctx_hl[:, :, :], ctx_raw[:, :, :],
                                        zero[:, :].unsqueeze(2).broadcast_to([P, BT, KVP]), ALU.add).then_inc(s["ctx_split"], 1)
                pool.wait_ge(s["ctx_split"], 2 * t + 1)
                nc.gpsimd.tensor_tensor(ctx_hl[CW:P, :, :], ctx_raw[CW:P, :, :],
                                        ctx_hl[CW:P, :, :].bitcast(F32), ALU.subtract).then_inc(s["ctx_split"], 1)

            def queries(t, p):
                wait(pool, s["pair_scored"], 8 * (t - 1))
                nc.gpsimd.tensor_tensor(
                    qbd[p][:, :, :, :],
                    QT[:, ds(P * t, P)].rearrange("p (b q) -> p b q", b=BT).unsqueeze(2).broadcast_to([P, BT, J * G, S]),
                    con["qmask"].unsqueeze(1).unsqueeze(3).broadcast_to([P, BT, J * G, S]),
                    ALU.mult).then_inc(s["qbd_ready"], 1)

            pool.wait_ge(s["w_split"], 2)
            split(0)
            pool.wait_ge(s["ctx_split"], 2)
            pool.wait_ge(s["q_ready"], 4)
            queries(0, 0)

            def tile(t, p, first, last):
                for b in range(BT):
                    n = 4 * t + b
                    q = b % 2
                    wait(pool, s["rl_done"], n - 1)
                    if b == 1 and not last:
                        pool.wait_ge(s["ctx_split"], 2 * t + 4)
                    elif b == 2 and not last:
                        pool.wait_ge(s["qbd_ready"], t + 2)
                    elif b == 0 and first:
                        pool.wait_ge(s["qbd_ready"], 1)
                    else:
                        pool.wait_ge(s["spread_ready"], 2 * n)
                    pool.wait_ge(s["exp_done"], 4 * n + 4)
                    nc.gpsimd.tensor_tensor(
                        spread[q][:, 0], con["rowmask"].rearrange("p (j g d) -> p j (g d)", j=J, g=G),
                        probs[q][:, :, KV - 1:KV].broadcast_to([P, J, G * DH]), ALU.mult).then_inc(s["spread_ready"], 1)
                    pool.wait_ge(s["rsum_ready"], n + 1)
                    pool.wait_ge(s["spread_ready"], 2 * n + 1)
                    nc.gpsimd.tensor_tensor(
                        spread[q][:, 1], con["rowmask"].rearrange("p (j g d) -> p j (g d)", j=J, g=G),
                        rsum[q][:, :].unsqueeze(2).broadcast_to([P, J, G * DH]), ALU.mult).then_inc(s["spread_ready"], 1)
                    if b < 2 and not last:
                        pool.wait_ge(s["spread_ready"], 2 * n + 2)
                    if b == 0 and not last:
                        split(t + 1)
                    if b == 1 and not last:
                        queries(t + 1, 1 - p)
            tiles(pool, tile)

        @block.scalar
        def _(act):
            act.wait_ge(s["w_loaded"], nw)

            def key_copies(t, p):
                wait(act, s["pair_scored"], 8 * (t - 1))
                for c in range(BT):
                    act.wait_ge(s["k_mm"], 4 * t + c + 1)
                    nc.scalar.activation(KT[p][:, c, :], pj[c % 2][:, 0:KVP], ACT.Identity,
                                         bias=bias[:, 1:2] if biased else 0.0).then_inc(s["k_ready"], 1)

            def value_copies(t, p):
                wait(act, s["v_ready"], 4 * t)
                for c in range(BT):
                    act.wait_ge(s["v_mm"], 4 * t + c + 1)
                    nc.scalar.activation(VT[:, c, :], pj[c % 2][:, 0:256], ACT.Identity,
                                         bias=bias[:, 2:3] if biased else 0.0).then_inc(s["v_copied"], 1)
                wait(act, s["concat_ready"], t - 1)
                nc.scalar.activation(v256[p][:, :], pj[1][:, 300:300 + BT], ACT.Identity,
                                     bias=bias[:, 3:4] if biased else 0.0).then_inc(s["v256_ready"], 1)

            key_copies(0, 0)
            value_copies(0, 0)

            def tile(t, p, first, last):
                for b in range(BT):
                    n = 4 * t + b
                    q = b % 2
                    wait(act, s["p_transposed"], 2 * (n - 1))
                    wait(act, s["spread_ready"], 2 * (n - 1))
                    for j in range(J):
                        act.wait_ge(s["max_ready"], 2 * n + j // 2 + 1)
                        nc.scalar.activation(probs[q][:, j, :], sc[j // 2][:, j % 2, 0:KV], ACT.Exp,
                                             bias=nmax[q][:, j:j + 1],
                                             accum_out=sums[q][:, j:j + 1]).then_inc(s["exp_done"], 1)
                    if b == 2 and not last:
                        key_copies(t + 1, 1 - p)
                if not last:
                    value_copies(t + 1, 1 - p)
            tiles(act, tile)

        @block.vector
        def _(dve):
            for c in range(4):
                dve.wait_ge(s["q_mm"], c + 1)
                if c == 0:
                    dve.wait_ge(s["w_loaded"], nw)
                src = [sc[0][:, 0, :], sc[0][:, 1, :], sc[1][:, 0, :], sc[1][:, 1, :]][c]
                if biased:
                    nc.vector.tensor_scalar(QT[:, 512 * c:512 * (c + 1)], src, bias[:, 0:1], SCALE,
                                            ALU.add, ALU.mult).then_inc(s["q_ready"], 1)
                else:
                    nc.vector.tensor_scalar(QT[:, 512 * c:512 * (c + 1)], src, SCALE, None,
                                            ALU.mult).then_inc(s["q_ready"], 1)
            if biased:
                nc.vector.tensor_tensor(X[:, :, :], X[:, :, :], bo[:, :].unsqueeze(1).broadcast_to([P, T, D]),
                                        ALU.add).then_inc(s["xb_ready"], 1)

            def values(t, p):
                dve.wait_ge(s["zeroed"], 3)
                dve.wait_ge(s["v_copied"], 4 * t + 4)
                wait(dve, s["rl_done"], 4 * (t - 1))
                for g in range(G):
                    r = slice(32 * g, 32 * g + 32)
                    nc.vector.transpose(VB[p][r, :, :, g, :], VT[r, :, :]).then_inc(s["v_ready"], 1)

            def finish(t, p):
                dve.wait_ge(s["rl_done"], 4 * t + 4)
                dve.wait_ge(s["v256_ready"], t + 1)
                wait(dve, s["out_mm"], t)
                base = 3 * t if biased else 3 * t
                chain = Chain(dve, s["concat_step"], 2 * t)
                chain.then(nc.vector.tensor_tensor(
                    cc[:, 0, :].rearrange("p (b q) -> p b q", b=BT), oacc_last.rearrange("p (b q) -> p b q", b=BT),
                    v256[p][:, :].unsqueeze(2).broadcast_to([P, BT, S]), ALU.mult))
                chain.then(nc.vector.tensor_tensor(cc[:, 1, :], oacc_v, cc[:, 0, :], ALU.add))
                nc.vector.tensor_tensor(cc[:, 2, :], oacc_rsum, cc[:, 1, :], ALU.mult).then_inc(s["concat_ready"], 1)

            def update(t):
                dve.wait_ge(s["out_mm"], t + 1)
                if biased:
                    dve.wait_ge(s["xb_ready"], 1)
                nc.vector.tensor_tensor(X[:, ds(t, 1), :].rearrange("p o d -> p (o d)") if not isinstance(t, int) else X[:, t, :],
                                        xo[:, 0:D],
                                        X[:, ds(t, 1), :].rearrange("p o d -> p (o d)") if not isinstance(t, int) else X[:, t, :],
                                        ALU.add).then_inc(s["x_updated"], 1)

            values(0, 0)

            def tile(t, p, first, last):
                for b in range(BT):
                    n = 4 * t + b
                    q = b % 2
                    for h in range(2):
                        dve.wait_ge(s["pair_scored"], 2 * n + h + 1)
                        wait(dve, s["exp_done"], 4 * (n - 1))
                        nc.vector.tensor_reduce(nmax[q][:, 2 * h:2 * h + 2], sc[h][:, :, 0:KV], AX.X, ALU.max,
                                                negate=True).then_inc(s["max_ready"], 1)
                    wait(dve, s["rl_done"], n - 1)
                    for h in range(2):
                        dve.wait_ge(s["exp_done"], 4 * n + 2 * h + 2)
                        nc.vector.transpose(probsT[q][:, 2 * h:2 * h + 2, :],
                                            probs[q][:, 2 * h:2 * h + 2, 0:256]).then_inc(s["p_transposed"], 1)
                    wait(dve, s["spread_ready"], 2 * (n - 1))
                    nc.vector.reciprocal(rsum[q][:, :], sums[q][:, :]).then_inc(s["rsum_ready"], 1)
                    if b == 0 and not first:
                        finish(t - 1, 1 - p)
                    if b == 1 and not first:
                        update(t - 1)
                if not last:
                    values(t + 1, 1 - p)
            tiles(dve, tile)
            finish(T - 1, 1)
            update(T - 1)

        @block.tensor
        def _(pe):
            pe.wait_ge(s["w_loaded"], nw)
            for c in range(4):
                nc.tensor.matmul([sc[0][:, 0, :], sc[0][:, 1, :], sc[1][:, 0, :], sc[1][:, 1, :]][c],
                                 wq[:, :], XNT[:, 512 * c:512 * (c + 1)], start=True, stop=True).then_inc(s["q_mm"], 1)
            pe.wait_ge(s["w_split"], 2)

            def project(t, what):
                pe.wait_ge(s["ctx_split"], 2 * t + 2)
                for c in range(BT):
                    if what == 0:
                        if c < 2:
                            wait(pe, s["v_copied"], 4 * (t - 1) + c + 3)
                            wait(pe, s["v256_ready"], t)
                        else:
                            pe.wait_ge(s["k_ready"], 4 * t + c - 1)
                    elif c < 2:
                        pe.wait_ge(s["k_ready"], 4 * t + c + 3)
                    else:
                        pe.wait_ge(s["v_copied"], 4 * t + c - 1)
                    nc.tensor.matmul(pj[c % 2][:, 0:KVP], whi[:, what, :], ctx_hl[:, c, :], start=True, stop=False)
                    last = nc.tensor.matmul(pj[c % 2][:, 0:KVP], wlo[:, what, :], ctx_hl[:, c, :], start=False, stop=True)
                    if what == 1 and c == BT - 1:
                        lk = ctx_hl[:, :, KV - 1]
                        nc.tensor.matmul(pj[1][:, 300:300 + BT], whi[:, 2, :], lk, start=True, stop=False)
                        last = nc.tensor.matmul(pj[1][:, 300:300 + BT], wlo[:, 2, :], lk, start=False, stop=True)
                    last.then_inc(s["v_mm"] if what else s["k_mm"], 1)

            def score(t, p, b):
                n = 4 * t + b
                for j in range(J):
                    wait(pe, s["exp_done"], 4 * (n - 1) + j + 1)
                    last = nc.tensor.matmul(sc[j // 2][:, j % 2, 0:KV],
                                            qbd[p][:, b, G * j:G * (j + 1), :], KT[p][:, b, 0:KV],
                                            start=True, stop=True)
                    if j % 2:
                        last.then_inc(s["pair_scored"], 1)

            def weigh(t, p, b):
                n = 4 * t + b
                q = b % 2
                pe.wait_ge(s["p_transposed"], 2 * n + 2)
                if b == 0:
                    pe.wait_ge(s["v_ready"], 4 * t + 4)
                    wait(pe, s["concat_ready"], t)
                cols = slice(S * b, S * (b + 1))
                for kb in range(KB):
                    for j in range(J):
                        nc.tensor.matmul(oacc_v[32 * j:32 * j + 32, cols], VB[p][:, KB * b + kb, j, :, :],
                                         probsT[q][:, j, 32 * kb:32 * kb + 32], start=(kb == 0), stop=(kb == KB - 1))
                pe.wait_ge(s["spread_ready"], 2 * n + 2)
                nc.tensor.matmul(oacc_last[:, cols], spread[q][:, 0], con["eye4"], start=True, stop=True)
                nc.tensor.matmul(oacc_rsum[:, cols], spread[q][:, 1], con["eye4"], start=True,
                                 stop=True).then_inc(s["rl_done"], 1)

            def output(t):
                pe.wait_ge(s["concat_ready"], t + 1)
                wait(pe, s["x_updated"], t)
                nc.tensor.matmul(xo[:, 0:D], cc[:, 2, :], wo[:, :], start=True, stop=True).then_inc(s["out_mm"], 1)

            project(0, 0)
            project(0, 1)
            pe.wait_ge(s["q_ready"], 4)

            def tile(t, p, first, last):
                pe.wait_ge(s["qbd_ready"], t + 1)
                pe.wait_ge(s["k_ready"], 4 * t + 4)
                score(t, p, 0)
                if not first:
                    weigh(t - 1, 1 - p, BT - 1)
                score(t, p, 1)
                weigh(t, p, 0)
                if not first:
                    output(t - 1)
                score(t, p, 2)
                weigh(t, p, 1)
                if not last:
                    project(t + 1, 0)
                score(t, p, 3)
                weigh(t, p, 2)
                if not last:
                    project(t + 1, 1)
            tiles(pe, tile)
            weigh(T - 1, 1, BT - 1)
            output(T - 1)


E_H, E_D = 16, 64


def at_tile(ap3, t):
    if isinstance(t, int):
        return ap3[:, t, :]
    return ap3[:, bass.ds(t, 1), :].rearrange("p o n -> p (o n)")


def at_cols(ap2, t, n):
    return ap2[:, t * n:(t + 1) * n] if isinstance(t, int) else ap2[:, bass.ds(t * n, n)]


def self_attention(nc, cx, name, X, XNT, con, W):
    sem = lambda n: cx.enter_context(nc.semaphore(f"{name}_{n}"))
    names = ("w_loaded", "xb_ready", "proj_mm", "proj_copied", "scored", "masked", "max_ready", "shifted",
             "exp_done", "rsum_ready", "probs_ready", "p_transposed", "z_mm", "z_copied", "out_mm", "x_updated",
             "sum_ready", "xts_ready")
    s = {n: sem(n) for n in names}
    HC = E_H // 2
    HE = E_H * E_D
    NPR = 6
    with ExitStack() as mem:
        sb = lambda n, sh, d=F32: mem.enter_context(nc.sbuf_tensor(f"{name}_{n}", sh, d))
        ps = lambda n, sh: mem.enter_context(nc.psum_tensor(f"{name}_{n}", sh, F32))
        wqkv = sb("wqkv", [P, 3, HE])
        wo = sb("wo", [P, HC, D])
        bqk = sb("bqk", [P, 2, HC])
        bv = sb("bv", [P, HE])
        bo = sb("bo", [P, D])
        QK = [sb(f"qk{n}", [P, 2, HC, P]) for n in range(2)]
        V = [sb(f"v{n}", [P, HE]) for n in range(2)]
        sm = sb("sm", [P, 2, HC, S])
        pr = sb("pr", [P, 2, HC, S])
        prT = sb("prT", [P, 2, HC, S])
        nmax, sums, rsum = sb("nmax", [P, 2 * HC]), sb("sums", [P, 2 * HC]), sb("rsum", [P, 2 * HC])
        zT = sb("zT", [P, HC, BT, S])
        xts = sb("xts", [P, P])
        pj = [ps(f"pj{n}", [P, 512]) for n in range(2)]
        sc = ps("sc", [P, 2, 512])
        z = ps("z", [P, BT, 512])
        block = mem.enter_context(nc.Block())
        nw = 16 * 5

        def heads(a):
            return a[:, :].unsqueeze(2).broadcast_to([P, 2 * HC, S])
        flat = lambda a: a[:, :, :, :].rearrange("p r c k -> p (r c) k")

        @block.sync
        def _(sp):
            for dst, src in ((wqkv[:, :, :], W["wqkv"]), (wo[:, :, :], W["wo"]), (bqk[:, :, :], W["bqk"]),
                             (bv[:, :], W["bv"]), (bo[:, :], W["bo"])):
                sp.dma_start(dst, src).then_inc(s["w_loaded"], 16)

        def tiles(eng, tile):
            tile(0, 0, True, False)
            tile(1, 1, False, False)
            with eng.Fori(1, T // 2 - 1) as i:
                tile(2 * i, 0, False, False)
                tile(2 * i + 1, 1, False, False)
            tile(T - 2, 0, False, False)
            tile(T - 1, 1, False, True)

        @block.tensor
        def _(pe):
            pe.wait_ge(s["w_loaded"], nw)

            def project(t, m):
                wait(pe, s["proj_copied"], NPR * t + m - 1)
                xt = at_cols(XNT, t, P)
                for c in range(4):
                    if m < 4:
                        w = 4 * (m % 2) + c
                        last = nc.tensor.matmul(pj[m % 2][:, c * P:(c + 1) * P], wqkv[:, m // 2, w * P:(w + 1) * P],
                                                xt, start=True, stop=True)
                    else:
                        w = (m - 4) * 512 + c * P
                        if c == 0:
                            last = nc.tensor.matmul(pj[m % 2][:, :], xts[:, :], wqkv[:, 2, w:w + 512],
                                                    start=True, stop=True)
                last.then_inc(s["proj_mm"], 1)

            def may_score(t):
                pe.wait_ge(s["proj_copied"], NPR * t + 4)
                wait(pe, s["masked"], t)

            def score(t, p):
                for b in range(BT):
                    for h in range(E_H):
                        r = slice(E_D * (h % 2), E_D * (h % 2) + E_D)
                        last = nc.tensor.matmul(sc[S * b:S * b + S, h % 2, S * (h // 2):S * (h // 2) + S],
                                                QK[p][r, 0, h // 2, S * b:S * b + S],
                                                QK[p][r, 1, h // 2, S * b:S * b + S], start=True, stop=True)
                last.then_inc(s["scored"], 1)

            def weigh(t, p):
                pe.wait_ge(s["p_transposed"], t + 1)
                pe.wait_ge(s["proj_copied"], NPR * t + 6)
                wait(pe, s["x_updated"], t)
                wait(pe, s["z_copied"], t)
                for h in range(E_H):
                    for b in range(BT):
                        r = slice(S * b, S * b + S)
                        last = nc.tensor.matmul(z[E_D * (h % 2):E_D * (h % 2) + E_D, b, S * (h // 2):S * (h // 2) + S],
                                                V[p][r, E_D * h:E_D * h + E_D], prT[r, h % 2, h // 2, :],
                                                start=True, stop=True)
                last.then_inc(s["z_mm"], 1)

            def output(t):
                pe.wait_ge(s["z_copied"], t + 1)
                for c in range(HC):
                    last = nc.tensor.matmul(z[:, 0, 256:256 + D], zT[:, c, :, :], wo[:, c, :],
                                            start=(c == 0), stop=(c == HC - 1))
                last.then_inc(s["out_mm"], 1)

            def stage_x(t):
                pe.wait_ge(s["xts_ready"], t + 1)

            def tile(t, p, first, last):
                may_score(t)
                if not last:
                    project(t + 1, 0)
                score(t, p)
                if not first:
                    output(t - 1)
                if not last:
                    for m in range(1, NPR):
                        if m == 4:
                            stage_x(t + 1)
                        project(t + 1, m)
                weigh(t, p)
            for m in range(NPR):
                if m == 4:
                    stage_x(0)
                project(0, m)
            tiles(pe, tile)
            output(T - 1)

        @block.vector
        def _(dve):
            dve.wait_ge(s["w_loaded"], nw)
            nc.vector.tensor_tensor(X[:, :, :], X[:, :, :], bo[:, :].unsqueeze(1).broadcast_to([P, T, D]),
                                    ALU.add).then_inc(s["xb_ready"], 1)

            def copy(t, p, m):
                dve.wait_ge(s["proj_mm"], NPR * t + m + 1)
                if m < 4:
                    if m == 0:
                        wait(dve, s["scored"], t - 1)
                    o = QK[p][:, m // 2, 4 * (m % 2):4 * (m % 2) + 4, :]
                    a = pj[m % 2][:, :].rearrange("p (c n) -> p c n", c=4)
                    bb = bqk[:, m // 2, 4 * (m % 2):4 * (m % 2) + 4].unsqueeze(2).broadcast_to([P, 4, P])
                else:
                    if m == 4:
                        wait(dve, s["z_mm"], t - 1)
                    w = (m - 4) * 512
                    o, a, bb = V[p][:, w:w + 512], pj[m % 2][:, :], bv[:, w:w + 512]
                nc.vector.tensor_tensor(o, a, bb, ALU.add).then_inc(s["proj_copied"], 1)

            def update(t):
                dve.wait_ge(s["out_mm"], t + 1)
                dve.wait_ge(s["xb_ready"], 1)
                nc.vector.tensor_tensor(at_tile(X, t), z[:, 0, 256:256 + D], at_tile(X, t),
                                        ALU.add).then_inc(s["x_updated"], 1)

            for m in range(NPR):
                copy(0, 0, m)

            def tile(t, p, first, last):
                nxt = lambda m: None if last else copy(t + 1, 1 - p, m)
                dve.wait_ge(s["scored"], t + 1)
                wait(dve, s["exp_done"], t)
                nc.vector.scalar_tensor_tensor(
                    flat(sm), sc[:, :, 0:HC * S].rearrange("p r (c k) -> p r c k", k=S), E_D ** -0.5,
                    con["causal"],
                    ALU.mult, ALU.add).then_inc(s["masked"], 1)
                dve.wait_ge(s["masked"], t + 1)
                nc.vector.tensor_reduce(nmax[:, :], flat(sm), AX.X, ALU.max).then_inc(s["max_ready"], 1)
                if not first:
                    update(t - 1)
                nxt(0)
                nxt(1)
                dve.wait_ge(s["exp_done"], t + 1)
                nc.vector.reduce_sum(sums[:, :], flat(pr), AX.X).then_inc(s["sum_ready"], 1)
                nxt(2)
                dve.wait_ge(s["sum_ready"], t + 1)
                wait(dve, s["probs_ready"], t)
                nc.vector.reciprocal(rsum[:, :], sums[:, :]).then_inc(s["rsum_ready"], 1)
                nxt(3)
                nxt(4)
                dve.wait_ge(s["probs_ready"], t + 1)
                wait(dve, s["z_mm"], t)
                nc.vector.transpose(prT[:, :, :, :].rearrange("p r c k -> p (r c k)"),
                                    pr[:, :, :, :].rearrange("p r c k -> p (r c k)")).then_inc(s["p_transposed"], 1)
                nxt(5)
            tiles(dve, tile)
            update(T - 1)

        @block.gpsimd
        def _(pool):
            def tile(t, p, first, last):
                pool.wait_ge(s["max_ready"], t + 1)
                wait(pool, s["probs_ready"], t)
                nc.gpsimd.tensor_tensor(flat(sm), flat(sm), heads(nmax), ALU.subtract).then_inc(s["shifted"], 1)
                pool.wait_ge(s["rsum_ready"], t + 1)
                pool.wait_ge(s["shifted"], t + 1)
                nc.gpsimd.tensor_tensor(flat(pr), flat(pr), heads(rsum), ALU.mult).then_inc(s["probs_ready"], 1)
            tiles(pool, tile)

        @block.scalar
        def _(act):
            def stage(t):
                wait(act, s["proj_mm"], NPR * t)
                nc.scalar.copy(xts[:, :], at_cols(XNT, t, P)).then_inc(s["xts_ready"], 1)
            stage(0)

            def tile(t, p, first, last):
                act.wait_ge(s["shifted"], t + 1)
                wait(act, s["p_transposed"], t)
                nc.scalar.activation(flat(pr), flat(sm), ACT.Exp).then_inc(s["exp_done"], 1)
                if not last:
                    stage(t + 1)
                act.wait_ge(s["z_mm"], t + 1)
                wait(act, s["out_mm"], t)
                nc.scalar.copy(zT[:, :, :, :].rearrange("p c b k -> p b c k"),
                               z[:, :, 0:HC * S].rearrange("p b (c k) -> p b c k", k=S)).then_inc(s["z_copied"], 1)
            tiles(act, tile)


I_FF = 352
CH = (128, 128, 96)


def router(nc, cx, name, XNT, CW, con, W, n_exp, top2, shared):
    sem = lambda n: cx.enter_context(nc.semaphore(f"{name}_{n}"))
    w_loaded, logits_mm, neg_ready, exp_done, step = (
        sem(n) for n in ("w_loaded", "logits_mm", "neg_ready", "exp_done", "step"))
    with ExitStack() as mem:
        sb = lambda n, sh, d=F32: mem.enter_context(nc.sbuf_tensor(f"{name}_{n}", sh, d))
        rw = sb("rw", [P, n_exp])
        rb = sb("rb", [P, n_exp])
        pr, eq, pr2, hot = (sb(n, [P, T, n_exp]) for n in ("pr", "eq", "pr2", "hot"))
        best, first, total, second = (sb(n, [P, T]) for n in ("best", "first", "total", "second"))
        lg = mem.enter_context(nc.psum_tensor(f"{name}_lg", [P, 512], F32))
        lgv = lg[:, 0:T * n_exp].rearrange("p (t e) -> p t e", e=n_exp)
        block = mem.enter_context(nc.Block())
        wide = lambda a: a[:, :].unsqueeze(2).broadcast_to([P, T, n_exp])
        experts = lambda a: a.unsqueeze(1).broadcast_to([P, T, n_exp])

        @block.sync
        def _(sp):
            sp.dma_start(rw[:, :], W["rw"]).then_inc(w_loaded, 16)
            sp.dma_start(rb[:, :], W["rb"]).then_inc(w_loaded, 16)

        @block.tensor
        def _(pe):
            pe.wait_ge(w_loaded, 32)
            for t in range(T):
                last = nc.tensor.matmul(lgv[:, t, :], XNT[:, t * P:(t + 1) * P], rw[:, :], start=True, stop=True)
            last.then_inc(logits_mm, 1)

        @block.scalar
        def _(act):
            act.wait_ge(neg_ready, 1)
            nc.scalar.activation(pr[:, :, :], pr[:, :, :], ACT.Exp, scale=-1.0).then_inc(exp_done, 1)

        @block.vector
        def _(dve):
            chain = Chain(dve, step)
            v = nc.vector
            dve.wait_ge(logits_mm, 1)
            if shared:
                chain.then(v.tensor_tensor(pr[:, :, :], lgv, experts(rb[:, :]), ALU.add))
                v.tensor_scalar(pr[:, :, :], pr[:, :, :], 50.0, -50.0, ALU.min, ALU.max).then_inc(neg_ready, 1)
            else:
                v.tensor_tensor(pr[:, :, :], lgv, experts(rb[:, :]), ALU.add).then_inc(neg_ready, 1)
            dve.wait_ge(exp_done, 1)
            chain.then(v.tensor_scalar_add(pr[:, :, :], pr[:, :, :], 1.0))
            chain.then(v.reciprocal(pr[:, :, :], pr[:, :, :]))

            def pick(src, best):
                chain.then(v.tensor_reduce(best[:, :], src[:, :, :], AX.X, ALU.max))
                chain.then(v.tensor_tensor(eq[:, :, :], src[:, :, :], wide(best), ALU.is_equal))
                chain.then(v.tensor_tensor(eq[:, :, :], eq[:, :, :], experts(con["rank"][:, 0:n_exp]), ALU.mult))
                chain.then(v.tensor_reduce(first[:, :], eq[:, :, :], AX.X, ALU.max))
                chain.then(v.tensor_tensor(hot[:, :, :], eq[:, :, :], wide(first), ALU.is_equal))

            pick(pr, best)
            if not top2:
                chain.then(v.tensor_scalar(best[:, :], best[:, :], 1e-8, 1.0 - 1e-8, ALU.max, ALU.min))
                chain.then(v.tensor_scalar(total[:, :], best[:, :], 0.5, 1e-8, ALU.add, ALU.add))
                chain.then(v.tensor_scalar(total[:, :], total[:, :], 0.5, 2.0, ALU.max, ALU.min))
                chain.then(v.reciprocal(total[:, :], total[:, :]))
                chain.then(v.tensor_scalar(CW[:, :, 0], total[:, :], 0.5, None, ALU.mult))
                chain.then(v.tensor_tensor(best[:, :], best[:, :], total[:, :], ALU.mult))
                chain.then(v.tensor_tensor(CW[:, :, 1:1 + n_exp], hot[:, :, :], wide(best), ALU.mult))
            else:
                chain.then(v.tensor_tensor(CW[:, :, 0:n_exp], hot[:, :, :], wide(best), ALU.mult))
                chain.then(v.scalar_tensor_tensor(pr2[:, :, :], hot[:, :, :], -2.0, pr[:, :, :], ALU.mult, ALU.add))
                pick(pr2, second)
                chain.then(v.tensor_tensor(hot[:, :, :], hot[:, :, :], wide(second), ALU.mult))
                chain.then(v.tensor_tensor(CW[:, :, 0:n_exp], CW[:, :, 0:n_exp], hot[:, :, :], ALU.add))
                chain.then(v.tensor_tensor(total[:, :], best[:, :], second[:, :], ALU.add))
                chain.then(v.tensor_scalar_add(total[:, :], total[:, :], 1e-20))
                chain.then(v.reciprocal(total[:, :], total[:, :]))
                chain.then(v.tensor_tensor(CW[:, :, 0:n_exp], CW[:, :, 0:n_exp], wide(total), ALU.mult))


def dense_experts(nc, cx, name, X, XNT, CW, W, n):
    ds = bass.ds
    sem = lambda k: cx.enter_context(nc.semaphore(f"{name}_{k}"))
    w_loaded = [sem(f"w_loaded{p}") for p in range(2)]
    names = ("up_mm", "silu_done", "h_ready", "down_mm", "x_updated")
    s = {k: sem(k) for k in names}
    NBLK = T * P // 512
    NC = len(CH)
    with ExitStack() as mem:
        sb = lambda k, sh, d=F32: mem.enter_context(nc.sbuf_tensor(f"{name}_{k}", sh, d))
        ps = lambda k, sh: mem.enter_context(nc.psum_tensor(f"{name}_{k}", sh, F32))
        w13 = [sb(f"w13{k}", [P, 2, I_FF]) for k in range(2)]
        w2 = [sb(f"w2{k}", [P, NC, D]) for k in range(2)]
        g = [sb(f"g{k}", [P, 512]) for k in range(NC)]
        h = [[sb(f"h{q}{k}", [P, 512]) for k in range(NC)] for q in range(2)]
        u1 = [ps(f"u1{k}", [P, 512]) for k in range(NC)]
        u3 = [ps(f"u3{k}", [P, 512]) for k in range(NC)]
        y = [ps(f"y{k}", [P, 4, P]) for k in range(2)]
        block = mem.enter_context(nc.Block())
        NL = n // 2 * 2

        def experts(eng, work):
            work(0, 0, True, 0)
            work(1, 1, False, 0)
            with eng.Fori(1, NL // 2) as i:
                work(2 * i, 0, False, i)
                work(2 * i + 1, 1, False, i)
            if n % 2:
                work(n - 1, 0, False, n // 2)

        @block.sync
        def _(sp):
            def work(e, p, first, turn):
                wait(sp, s["down_mm"], NBLK * (e - 1))
                sp.dma_start(w13[p][:, :, :], W["w13"][ds(e, 1), :, :, :].rearrange("o p m i -> p (o m) i")
                             ).then_inc(w_loaded[p], 16)
                sp.dma_start(w2[p][:, :, :], W["w2"][ds(e, 1), :, :, :].rearrange("o p m i -> p (o m) i")
                             ).then_inc(w_loaded[p], 16)
            experts(sp, work)

        @block.tensor
        def _(pe):
            def down(e, p, k):
                m = NBLK * e + k
                wait(pe, s["x_updated"], 4 * (m - 1))
                pe.wait_ge(s["h_ready"], NC * m + NC)
                for t in range(4):
                    for c in range(NC):
                        last = nc.tensor.matmul(y[k % 2][:, t, :], h[k % 2][c][0:CH[c], t * P:(t + 1) * P],
                                                w2[p][0:CH[c], c, :], start=(c == 0), stop=(c == NC - 1))
                last.then_inc(s["down_mm"], 1)

            def work(e, p, first, turn):
                for k in range(NBLK):
                    m = NBLK * e + k
                    for c in range(NC):
                        if c == 0 and k == 0:
                            pe.wait_ge(w_loaded[p], 32 * turn + 32)
                        if not (first and k == 0):
                            pe.wait_ge(s["h_ready"], NC * (m - 1) + c + 1)
                        for j, u in ((0, u1), (1, u3)):
                            last = nc.tensor.matmul(u[c][0:CH[c], :], w13[p][:, j, c * P:c * P + CH[c]],
                                                    XNT[:, k * 512:(k + 1) * 512], start=True, stop=True)
                        last.then_inc(s["up_mm"], 1)
                    if k:
                        down(e, p, k - 1)
                    elif not first:
                        down(e - 1, 1 - p, NBLK - 1)
            experts(pe, work)
            down(n - 1, (n - 1) % 2, NBLK - 1)

        @block.scalar
        def _(act):
            def work(e, p, first, turn):
                for k in range(NBLK):
                    m = NBLK * e + k
                    for c in range(NC):
                        act.wait_ge(s["up_mm"], NC * m + c + 1)
                        if not (first and k == 0):
                            act.wait_ge(s["h_ready"], NC * (m - 1) + c + 1)
                        nc.scalar.activation(g[c][0:CH[c], :], u1[c][0:CH[c], :], ACT.Silu).then_inc(s["silu_done"], 1)
            experts(act, work)

        @block.vector
        def _(dve):
            def update(e, k):
                m = NBLK * e + k
                dve.wait_ge(s["down_mm"], m + 1)
                for t in range(4):
                    tt = 4 * k + t
                    if not (isinstance(e, int) and e == 0):
                        dve.wait_ge(s["x_updated"], 4 * (m - NBLK) + t + 1)
                    nc.vector.scalar_tensor_tensor(X[:, tt, :], y[k % 2][:, t, :], at_cw(CW, tt, e), X[:, tt, :],
                                                   ALU.mult, ALU.add).then_inc(s["x_updated"], 1)

            def work(e, p, first, turn):
                for k in range(NBLK):
                    m = NBLK * e + k
                    if not (first and k < 2):
                        dve.wait_ge(s["down_mm"], m - 1)
                    for c in range(NC):
                        dve.wait_ge(s["silu_done"], NC * m + c + 1)
                        nc.vector.tensor_tensor(h[k % 2][c][0:CH[c], :], g[c][0:CH[c], :], u3[c][0:CH[c], :],
                                                ALU.mult).then_inc(s["h_ready"], 1)
                    if k:
                        update(e, k - 1)
                    elif not first:
                        update(e - 1, NBLK - 1)
            experts(dve, work)
            update(n - 1, NBLK - 1)


def at_cw(CW, t, e):
    return CW[:, t, e:e + 1] if isinstance(e, int) else CW[:, t, bass.ds(e, 1)]


def rope_attention(nc, cx, name, X, XNT, con, W):
    sem = lambda n: cx.enter_context(nc.semaphore(f"{name}_{n}"))
    names = ("w_loaded", "xb_ready", "xs_ready", "qkv_mm", "qk_ready", "v_ready", "cos_done", "swap_done", "roped",
             "qkT_mm", "qkT_copied", "scored", "max_ready", "bias_ready", "exp_done", "rsum_ready", "probs_ready",
             "pT_ready", "spread", "o_mm", "o_copied", "out_mm", "x_updated")
    s = {n: sem(n) for n in names}
    TB = 4
    NBLK = T // TB
    HALF = D // 2
    with ExitStack() as mem:
        sb = lambda n, sh, d=F32: mem.enter_context(nc.sbuf_tensor(f"{name}_{n}", sh, d))
        ps = lambda n, sh: mem.enter_context(nc.psum_tensor(f"{name}_{n}", sh, F32))
        wqkv = sb("wqkv", [P, 3 * D])
        wo = sb("wo", [P, D])
        bqkv = sb("bqkv", [P, 3 * D])
        bo = sb("bo", [P, D])
        xs = sb("xs", [P, TB * P])
        qk = sb("qk", [P, TB * 2, 2, HALF])
        v = sb("v", [P, TB, D])
        qc, qs, qr = sb("qc", [P, TB * 2, 2, HALF]), sb("qs", [P, TB * 2, 2, HALF]), sb("qr", [P, TB * 2, 2, HALF])
        qkT = sb("qkT", [P, TB * 2, P])
        nmax, sums, rsum = sb("nmax", [P, TB]), sb("sums", [P, TB]), sb("rsum", [P, TB])
        pr, prn, prT = sb("pr", [P, TB, S]), sb("prn", [P, TB, S]), sb("prT", [P, TB, S])
        pbd = sb("pbd", [P, TB, BT, S])
        oT = sb("oT", [P, TB, P])
        qkv_ps = ps("qkv_ps", [P, TB, 512])
        tr_ps = ps("tr_ps", [P, 2, 4, P])
        sc_ps = ps("sc_ps", [P, 512])
        o_ps = ps("o_ps", [P, TB, P])
        block = mem.enter_context(nc.Block())
        nw = 64

        def blocks(eng, work):
            work(0)
            with eng.Fori(1, NBLK) as i:
                work(i)

        @block.sync
        def _(sp):
            for dst, src in ((wqkv[:, :], W["wqkv"]), (wo[:, :], W["wo"]), (bqkv[:, :], W["bqkv"]), (bo[:, :], W["bo"])):
                sp.dma_start(dst, src).then_inc(s["w_loaded"], 16)

        @block.tensor
        def _(pe):
            pe.wait_ge(s["w_loaded"], nw)
            def work(i):
                pe.wait_ge(s["xs_ready"], i + 1)
                wait(pe, s["x_updated"], i)
                for t in range(TB):
                    last = nc.tensor.matmul(qkv_ps[:, t, 0:3 * D], xs[:, t * P:(t + 1) * P], wqkv[:, :],
                                            start=True, stop=True)
                last.then_inc(s["qkv_mm"], 1)
                pe.wait_ge(s["roped"], i + 1)
                for m in range(2 * TB):
                    last = nc.tensor.transpose(tr_ps[:, m // 4, m % 4, :],
                                               qr[:, m, :, :].rearrange("p h d -> p (h d)"), con["ident"])
                last.then_inc(s["qkT_mm"], 1)
                pe.wait_ge(s["qkT_copied"], i + 1)
                for t in range(TB):
                    for b in range(BT):
                        r = slice(S * b, S * b + S)
                        last = nc.tensor.matmul(sc_ps[r, S * t:S * t + S], qkT[:, 2 * t, r], qkT[:, 2 * t + 1, r],
                                                start=True, stop=True)
                last.then_inc(s["scored"], 1)
                pe.wait_ge(s["spread"], i + 1)
                for t in range(TB):
                    last = nc.tensor.matmul(o_ps[:, t, :], v[:, t, :], pbd[:, t, :, :], start=True, stop=True)
                last.then_inc(s["o_mm"], 1)
                pe.wait_ge(s["o_copied"], i + 1)
                for t in range(TB):
                    last = nc.tensor.matmul(qkv_ps[:, 0, t * P:(t + 1) * P], oT[:, t, :], wo[:, :], start=True, stop=True)
                last.then_inc(s["out_mm"], 1)
            blocks(pe, work)

        @block.scalar
        def _(act):
            def work(i):
                wait(act, s["qkv_mm"], i)
                nc.scalar.copy(xs[:, :], at_cols(XNT, i, TB * P)).then_inc(s["xs_ready"], 1)
                act.wait_ge(s["qkT_mm"], i + 1)
                nc.scalar.copy(qkT[:, :, :].rearrange("p m n -> p (m n)"),
                               tr_ps[:, :, :, :].rearrange("p a m n -> p (a m n)")).then_inc(s["qkT_copied"], 1)
                act.wait_ge(s["bias_ready"], i + 1)
                wait(act, s["probs_ready"], i)
                for t in range(TB):
                    nc.scalar.activation(pr[:, t, :], sc_ps[:, S * t:S * t + S], ACT.Exp, bias=nmax[:, t:t + 1],
                                         scale=D ** -0.5, accum_out=sums[:, t:t + 1]).then_inc(s["exp_done"], 1)
                act.wait_ge(s["o_mm"], i + 1)
                nc.scalar.copy(oT[:, :, :], o_ps[:, :, :]).then_inc(s["o_copied"], 1)
            blocks(act, work)

        @block.gpsimd
        def _(pool):
            def work(i):
                pool.wait_ge(s["qk_ready"], i + 1)
                wait(pool, s["spread"], i)
                nc.gpsimd.tensor_tensor(qc[:, :, :, :].rearrange("p m h d -> p m (h d)"),
                                        qk[:, :, :, :].rearrange("p m h d -> p m (h d)"),
                                        con["cos"].unsqueeze(1).broadcast_to([P, 2 * TB, D]), ALU.mult
                                        ).then_inc(s["cos_done"], 1)
                pool.wait_ge(s["pT_ready"], i + 1)
                pool.wait_ge(s["cos_done"], i + 1)
                nc.gpsimd.tensor_tensor(pbd[:, :, :, :], prT[:, :, :].unsqueeze(2).broadcast_to([P, TB, BT, S]),
                                        con["seqmask"].unsqueeze(1).unsqueeze(3).broadcast_to([P, TB, BT, S]),
                                        ALU.mult).then_inc(s["spread"], 1)
            blocks(pool, work)

        @block.vector
        def _(dve):
            dve.wait_ge(s["w_loaded"], nw)
            nc.vector.tensor_tensor(X[:, :, :], X[:, :, :], bo[:, :].unsqueeze(1).broadcast_to([P, T, D]),
                                    ALU.add).then_inc(s["xb_ready"], 1)
            dve.wait_ge(s["xb_ready"], 1)
            def work(i):
                dve.wait_ge(s["qkv_mm"], i + 1)
                nc.vector.tensor_tensor(
                    qk[:, :, :, :].rearrange("p (t m) h d -> p t (m h d)", t=TB), qkv_ps[:, :, 0:2 * D],
                    bqkv[:, 0:2 * D].unsqueeze(1).broadcast_to([P, TB, 2 * D]), ALU.add).then_inc(s["qk_ready"], 1)
                dve.wait_ge(s["qk_ready"], i + 1)
                for h in range(2):
                    nc.vector.tensor_tensor(qs[:, :, h, :], qk[:, :, 1 - h, :],
                                            con["sin"][:, h * HALF:(h + 1) * HALF].unsqueeze(1)
                                            .broadcast_to([P, 2 * TB, HALF]), ALU.mult).then_inc(s["swap_done"], 1)
                dve.wait_ge(s["cos_done"], i + 1)
                dve.wait_ge(s["swap_done"], 2 * i + 2)
                nc.vector.tensor_tensor(qr[:, :, :, :], qc[:, :, :, :], qs[:, :, :, :], ALU.add).then_inc(s["roped"], 1)
                nc.vector.tensor_tensor(v[:, :, :], qkv_ps[:, :, 2 * D:3 * D],
                                        bqkv[:, 2 * D:3 * D].unsqueeze(1).broadcast_to([P, TB, D]),
                                        ALU.add).then_inc(s["v_ready"], 1)
                dve.wait_ge(s["scored"], i + 1)
                wait(dve, s["exp_done"], 4 * i)
                nc.vector.tensor_reduce(nmax[:, :], sc_ps[:, 0:TB * S].rearrange("p (t k) -> p t k", k=S), AX.X,
                                        ALU.max, negate=True).then_inc(s["max_ready"], 1)
                dve.wait_ge(s["max_ready"], i + 1)
                nc.vector.tensor_scalar(nmax[:, :], nmax[:, :], D ** -0.5, None, ALU.mult).then_inc(s["bias_ready"], 1)
                dve.wait_ge(s["exp_done"], 4 * i + 4)
                nc.vector.reciprocal(rsum[:, :], sums[:, :]).then_inc(s["rsum_ready"], 1)
                dve.wait_ge(s["rsum_ready"], i + 1)
                nc.vector.tensor_tensor(prn[:, :, :], pr[:, :, :], rsum[:, :].unsqueeze(2).broadcast_to([P, TB, S]),
                                        ALU.mult).then_inc(s["probs_ready"], 1)
                dve.wait_ge(s["probs_ready"], i + 1)
                nc.vector.transpose(prT[:, :, :].rearrange("p t k -> p (t k)"),
                                    prn[:, :, :].rearrange("p t k -> p (t k)")).then_inc(s["pT_ready"], 1)
                dve.wait_ge(s["out_mm"], i + 1)
                xb = X[:, slice(0, TB) if isinstance(i, int) else bass.ds(i * TB, TB), :].rearrange("p t d -> p (t d)")
                nc.vector.tensor_tensor(xb, qkv_ps[:, 0, :], xb, ALU.add).then_inc(s["x_updated"], 1)
            blocks(dve, work)

CONSTS = (("ident", P), ("qmask", J * G), ("rowmask", P), ("eye4", S), ("causal", E_H * S), ("rank", 9),
          ("cos", D), ("sin", D), ("seqmask", BT))


def perceiver(nc, a, out):
    with ExitStack() as cx:
        sb = lambda n, s: cx.enter_context(nc.sbuf_tensor(n, s, F32))
        sem = lambda n: cx.enter_context(nc.semaphore(n))
        X = sb("x", [P, T, D])
        XNT = sb("xnt", [P, T * P])
        CW = sb("cw", [P, T, 9])
        cs = sb("consts", [P, sum(w for _, w in CONSTS)])
        con, at = {}, 0
        for n, w in CONSTS:
            con[n] = cs[:, at:at + w]
            at += w
        con["causal"] = con["causal"].rearrange("p (h k) -> p h k", k=S)
        loaded, stored = sem("loaded"), sem("stored")

        with nc.Block() as block:
            @block.sync
            def _(sp):
                sp.dma_start(X[:, :, :], a["x"]).then_inc(loaded, 16)
                sp.dma_start(cs[:, :], a["consts"]).then_inc(loaded, 16)
                sp.wait_ge(loaded, 32)

        def weights(pre, names):
            return {n: a.get(pre + n) for n in names}

        xa_names = ("wq", "wo", "wkvv", "bias", "bo")
        layernorm_stage(nc, cx, "n0", X, XNT, con["ident"])
        cross_attention(nc, cx, "x0", X, XNT, con, dict(weights("x0_", xa_names), ctx=a["ctx"]))

        lnwb = sb("lnwb", [P, 2])
        lnwb_loaded = sem("lnwb_loaded")
        with nc.Block() as block:
            @block.sync
            def _(sp):
                sp.dma_start(lnwb[:, :], a["a0_lnwb"]).then_inc(lnwb_loaded, 16)
                sp.wait_ge(lnwb_loaded, 16)
        layernorm_stage(nc, cx, "n1", X, XNT, con["ident"], twice=(lnwb[:, 0:1], lnwb[:, 1:2]))
        self_attention(nc, cx, "a0", X, XNT, con, weights("a0_", ("wqkv", "wo", "bqk", "bv", "bo")))

        layernorm_stage(nc, cx, "n2", X, XNT, con["ident"])
        router(nc, cx, "r0", XNT, CW, con, weights("f0_", ("rw", "rb")), 7, top2=False, shared=True)
        dense_experts(nc, cx, "f0", X, XNT, CW, weights("f0_", ("w13", "w2")), 8)

        layernorm_stage(nc, cx, "n3", X, XNT, con["ident"])
        cross_attention(nc, cx, "x1", X, XNT, con, dict(weights("x1_", xa_names), ctx=a["ctx"]))

        layernorm_stage(nc, cx, "n4", X, XNT, con["ident"])
        rope_attention(nc, cx, "a1", X, XNT, con, weights("a1_", ("wqkv", "wo", "bqkv", "bo")))

        layernorm_stage(nc, cx, "n5", X, XNT, con["ident"])
        router(nc, cx, "r1", XNT, CW, con, weights("f1_", ("rw", "rb")), 9, top2=True, shared=False)
        dense_experts(nc, cx, "f1", X, XNT, CW, weights("f1_", ("w13", "w2")), 9)

        with nc.Block() as block:
            @block.sync
            def _(sp):
                sp.dma_start(out, X[:, :, :]).then_inc(stored, 16)
                sp.wait_ge(stored, 16)


def kernel(**inputs):
    import numpy as np
    import concourse.bacc as bacc
    from concourse.bass_utils import run_bass_kernel_spmd

    i = {k: np.asarray(v) for k, v in inputs.items()}
    f32 = np.float32
    tile = lambda a: np.broadcast_to(a, (P, a.shape[-1]))
    twice = lambda w: np.concatenate([w, w], 0)
    r = np.arange(P)

    qmask = np.zeros((P, J * G), f32)
    qmask[r, G * (r // DH % J) + r // (J * DH)] = 1
    rowmask = (r[None, :] // DH % G == r[:, None] // S).astype(f32)
    causal = np.where(np.tril(np.ones((S, S))) > 0, 0, -3e38).astype(f32)
    half = D // 2
    inv = (1.0 / 10000.0 ** (np.arange(half, dtype=f32) / f32(half))).astype(f32)
    ang = np.arange(S, dtype=f32)[:, None] * inv[None]
    seqmask = (r[:, None] // S == np.arange(BT)[None]).astype(f32)
    consts = {
        "ident": np.eye(P, dtype=f32), "qmask": qmask, "rowmask": rowmask,
        "eye4": np.tile(np.eye(S, dtype=f32), (BT, 1)), "causal": np.tile(causal, (BT, E_H)),
        "rank": tile(np.arange(9, 0, -1).astype(f32)), "cos": np.tile(np.cos(ang), (BT, 2)),
        "sin": np.tile(np.concatenate([-np.sin(ang), np.sin(ang)], 1), (BT, 1)), "seqmask": seqmask,
    }

    rows = np.array([(J * g + j) * DH + d for j in range(J) for g in range(G) for d in range(DH)])
    arrays = {
        "x": i["x"].reshape(T, P, D).transpose(1, 0, 2),
        "consts": np.concatenate([consts[n] for n, _ in CONSTS], 1),
        "ctx": np.pad(i["ctx_512"].transpose(2, 0, 1), ((0, 0), (0, 0), (0, KVP - KV))),
    }

    def cross(pre, wq, wk, wv, wo):
        arrays[pre + "wq"], arrays[pre + "wo"] = wq, wo[rows]
        arrays[pre + "wkvv"] = np.stack([twice(wk), twice(wv), twice(wv[:, rows])], 1)

    cross("x0_", *(i[f"L0_xattn_W{c}"] for c in "qkvo"))
    bq, bk, bv, bo = (i[f"L0_xattn_b{c}"] for c in "qkvo")
    arrays["x0_bias"], arrays["x0_bo"] = np.stack([bq, bk, bv, bv[rows]], 1), tile(bo)
    wkv = i["L1_xattn_Wkv"]
    cross("x1_", i["L1_xattn_Wq"].T, wkv[:D].T, wkv[D:].T, i["L1_xattn_Wo"].T)

    heads = lambda w: w.transpose(1, 0, 2).reshape(D, E_H * E_D)
    arrays["a0_lnwb"] = np.stack([i["L0_attn_ln_w"], i["L0_attn_ln_b"]], 1)
    arrays["a0_wqkv"] = np.stack([heads(i[f"L0_attn_W_{c}"]) for c in "qkv"], 1)
    arrays["a0_wo"] = i["L0_attn_W_o"].reshape(E_H // 2, P, D).transpose(1, 0, 2)
    arrays["a0_bqk"] = np.stack([i[f"L0_attn_b_{c}"].reshape(E_H // 2, P).T for c in "qk"], 1)
    arrays["a0_bv"] = tile(i["L0_attn_b_v"].reshape(-1))
    arrays["a0_bo"] = tile(i["L0_attn_b_o"])

    arrays["a1_wqkv"], arrays["a1_wo"] = i["L1_attn_w_qkv"].T, i["L1_attn_w_o"].T
    arrays["a1_bqkv"], arrays["a1_bo"] = tile(i["L1_attn_b_qkv"]), tile(i["L1_attn_b_o"])

    def experts(pre, w1, w2, w3, rw, rb):
        n, pad = len(w1), P * len(CH) - I_FF
        arrays[pre + "w13"] = np.stack([w1.transpose(0, 2, 1), w3.transpose(0, 2, 1)], 2)
        w2t = np.pad(w2.transpose(0, 2, 1), ((0, 0), (0, pad), (0, 0))).reshape(n, len(CH), P, D)
        arrays[pre + "w2"] = w2t.transpose(0, 2, 1, 3)
        arrays[pre + "rw"], arrays[pre + "rb"] = rw.T, tile(rb)

    join = lambda *n: np.concatenate([i[k] if i[k].ndim != 2 or "gate" in k else i[k][None] for k in n])
    experts("f0_", *(join(f"L0_ffn_sw{m}", f"L0_ffn_ew{m}") for m in (1, 2, 3)),
            i["L0_ffn_router_w"], i["L0_ffn_routing_bias"])
    experts("f1_", *(join(f"L1_ffn_w{m}", f"L1_ffn_new_w{m}") for m in (1, 2, 3)),
            join("L1_ffn_gate_weight", "L1_ffn_new_gate_weight"), np.pad(i["L1_ffn_gate_bias"], (8, 0)))

    nc = bacc.Bacc("TRN2", target_bir_lowering=False, num_devices=1)
    arrays = {f"in_{n}": np.ascontiguousarray(v, dtype=f32) for n, v in arrays.items()}
    aps = {n[3:]: nc.dram_tensor(n, v.shape, F32, kind="ExternalInput").ap() for n, v in arrays.items()}
    out = nc.dram_tensor("out", (P, T, D), F32, kind="ExternalOutput").ap()
    perceiver(nc, aps, out)
    got = run_bass_kernel_spmd(nc, [arrays], core_ids=[0]).results[0]["out"]
    return got.transpose(1, 0, 2).reshape(B, S, D)
```

```python
import concourse.bass as bass
from concourse import mybir
from contextlib import ExitStack

F32 = mybir.dt.float32
F32R = mybir.dt.float32r
BF16 = mybir.dt.bfloat16
I32 = mybir.dt.int32
ALU = mybir.AluOpType
ACT = mybir.ActivationFunctionType
AX = mybir.AxisListType

P = 128
D = 128
B, S = 64, 32
T = B * S // P
BT = P // S
KV = 257
KVP = 258
CW = 64
H, DH = 16, 8
G, J = 4, 4
EPS = 1e-5
ACT_QUADS, POOL_QUADS = (0, 1, 2), (3,)


def wait(eng, sem, value):
    if not isinstance(value, int) or value > 0:
        eng.wait_ge(sem, value)


class Chain:

    def __init__(self, eng, sem, base=0):
        self.eng, self.sem, self.base, self.n = eng, sem, base, 0

    def then(self, ins):
        self.n += 1
        ins.then_inc(self.sem, 1)
        self.eng.wait_ge(self.sem, self.base + self.n)


class LayernormCount:

    def __init__(self, nc, cx):
        (self.stats_ready, self.mv_ready, self.var_ready, self.rstd_ready, self.shift_ready, self.xn_dve, self.xn_act,
         self.xt_ready) = (cx.enter_context(nc.semaphore("norm_" + n)) for n in (
            "stats_ready", "mv_ready", "var_ready", "rstd_ready", "shift_ready", "xn_dve", "xn_act", "xt_ready"))
        self.rounds = self.stages = 0


def layernorm_stage(nc, count, name, X, XNT, con, twice=None, wait_wb=None, rows=None,
                    loads=None, before=None, after=None, wait_x=None):
    NB = 4
    NG = T // NB
    rounds = 2 if twice else 1
    first_round, stages = count.rounds, count.stages
    count.rounds, count.stages = first_round + rounds, stages + 1
    with ExitStack() as mem:
        sb = lambda n, s, d=F32: mem.enter_context(nc.sbuf_tensor(f"{name}_{n}", s, d))
        stats = sb("stats", [P, T, 6])
        mv = sb("mv", [P, T, 2])
        rvar = sb("rvar", [P, T])
        rstd = sb("rstd", [P, T])
        shift = sb("shift", [P, T])
        XN = [sb(f"xn{n}", [P, T, D]) for n in range(rounds - 1)] + [rows or sb("rows", [P, T, D])]
        xt_ps = [mem.enter_context(nc.psum_tensor(f"{name}_xt{n}", [P, NB * P], F32)) for n in range(NG)]
        block = mem.enter_context(nc.Block())
        src = [X, XN[0]]
        w, b = twice or (1.0, 0.0)
        group = lambda n: slice(n * NB * P, (n + 1) * NB * P)

        @block.vector
        def _(dve):
            if wait_x:
                wait_x(dve)
            for r in range(rounds):
                for t in range(T):
                    if r and t % NB == 0:
                        dve.wait_ge(count.xn_dve, first_round * NG + t // NB + 1)
                    if r and t % NB == 2:
                        dve.wait_ge(count.xn_act, first_round * NG + t // NB + 1)
                    last = nc.vector.bn_stats(stats[:, t, :], src[r][:, t, :])
                last.then_inc(count.stats_ready, 1)
                dve.wait_ge(count.stats_ready, first_round + r + 1)
                for t in range(T):
                    last = nc.vector.bn_aggr(mv[:, t, :], stats[:, t, :])
                last.then_inc(count.mv_ready, 1)
                dve.wait_ge(count.rstd_ready, first_round + r + 1)
                nc.vector.scalar_tensor_tensor(shift[:, :], mv[:, :, 0], -1.0, rstd[:, :], ALU.mult,
                                               ALU.mult).then_inc(count.shift_ready, 1)
                for n in range(NG):
                    for t in (NB * n, NB * n + 1):
                        last = nc.vector.tensor_scalar(XN[r][:, t, :], src[r][:, t, :], mv[:, t, 0:1],
                                                       rstd[:, t:t + 1], ALU.subtract, ALU.mult)
                    last.then_inc(count.xn_dve, 1)
            if wait_wb:
                wait_wb(dve)
            for n in (1, 3):
                dve.wait_ge(count.xt_ready, stages * NG + n + 1)
                nc.vector.tensor_scalar(XNT[:, group(n)], xt_ps[n][:, :], w, b, ALU.mult, ALU.add)

        @block.sync
        def _(sp):
            if loads:
                loads(sp)

        @block.gpsimd
        def _(pool):
            if before:
                before(pool)
            if wait_x:
                wait_x(pool)
            for r in range(rounds):
                pool.wait_ge(count.mv_ready, first_round + r + 1)
                nc.gpsimd.tensor_tensor(rvar[:, :], mv[:, :, 1], con["eps"].broadcast_to([P, T]),
                                        ALU.add).then_inc(count.var_ready, 1)
                pool.wait_ge(count.var_ready, first_round + r + 1)
                nc.gpsimd.tensor_tensor(rstd[:, :], rvar[:, :], con["power"].broadcast_to([P, T]),
                                        ALU.pow).then_inc(count.rstd_ready, 1)
            if after:
                pool.wait_ge(count.rstd_ready, first_round + rounds)
                after(pool)

        @block.scalar
        def _(act):
            if wait_x:
                wait_x(act)
            for r in range(rounds):
                act.wait_ge(count.shift_ready, first_round + r + 1)
                for n in range(NG):
                    for t in (NB * n + 2, NB * n + 3):
                        last = nc.scalar.activation(XN[r][:, t, :], src[r][:, t, :], ACT.Identity,
                                                    bias=shift[:, t:t + 1], scale=rstd[:, t:t + 1])
                    last.then_inc(count.xn_act, 1)
            if wait_wb:
                wait_wb(act)
            for n in (0, 2):
                act.wait_ge(count.xt_ready, stages * NG + n + 1)
                nc.scalar.activation(XNT[:, group(n)], xt_ps[n][:, :], ACT.Identity,
                                     bias=b, scale=w)

        @block.tensor
        def _(pe):
            if wait_x:
                wait_x(pe)
            for n in range(NG):
                pe.wait_ge(count.xn_dve, (first_round + rounds - 1) * NG + n + 1)
                pe.wait_ge(count.xn_act, (first_round + rounds - 1) * NG + n + 1)
                for k in range(NB):
                    last = nc.tensor.transpose(xt_ps[n][:, k * P:(k + 1) * P], XN[-1][:, n * NB + k, :], con["ident"])
                last.then_inc(count.xt_ready, 1)


class CrossBuffers:

    def __init__(self, nc, cx):
        sb = lambda n, sh, d=F32: cx.enter_context(nc.sbuf_tensor(f"cross_{n}", sh, d))
        self.whi, self.wlo = sb("whi", [P, 3, D], F32R), sb("wlo", [P, 3, D], F32R)
        self.ctx_raw = sb("ctx_raw", [P, BT, KVP])
        self.ctx_hl = [sb(f"ctx_hl{n}", [P, BT, KVP], F32R) for n in range(2)]
        self.VB = [sb(f"vb{n}", [P, BT * 256 // 32, J, G, DH]) for n in range(2)]
        self.zero = sb("zero", [P, 1])


def cross_semaphores(nc, cx, name):
    names = ("ctx_loaded", "w_split", "ctx_split", "q_mm", "q_ready", "qbd_ready", "pair_scored",
             "max_ready", "exp_done", "p_transposed", "rsum_ready", "spread_ready", "pv_done", "rl_done", "concat_step",
             "concat_ready", "out_mm", "x_updated", "k_mm", "k_ready", "v_mm", "v_copied", "v256_ready",
             "v_turned", "v_act", "v_pool", "xb_ready")
    return {n: cx.enter_context(nc.semaphore(f"{name}_{n}")) for n in names}


def load_context(sp, s, B, W, t):
    wait(sp, s["ctx_split"], 2 * t)
    for half in range(2):
        sp.dma_start(B.ctx_raw[half * CW:(half + 1) * CW, :, :],
                     W["ctx"][:, bass.ds(BT * t, BT), :]).then_inc(s["ctx_loaded"], 16)


def split_high(nc, pool, s, B, t, p):
    pool.wait_ge(s["ctx_loaded"], 32 * t + 32)
    wait(pool, s["k_mm"], 4 * (t - 1))
    nc.gpsimd.tensor_tensor(B.ctx_hl[p][:, :, :], B.ctx_raw[:, :, :],
                            B.zero[:, :].unsqueeze(2).broadcast_to([P, BT, KVP]), ALU.add).then_inc(s["ctx_split"], 1)


def split_low(nc, pool, s, B, t, p):
    pool.wait_ge(s["ctx_split"], 2 * t + 1)
    nc.gpsimd.tensor_tensor(B.ctx_hl[p][CW:P, :, :], B.ctx_raw[CW:P, :, :],
                            B.ctx_hl[p][CW:P, :, :].bitcast(F32), ALU.subtract).then_inc(s["ctx_split"], 1)


def cross_start(nc, s, B, W, zeroed=None):

    def before(pool):
        if zeroed:
            nc.gpsimd.memset(B.zero[:, :], 0.0).then_inc(zeroed, 1)
            for n in range(2):
                pool.wait_ge(zeroed, n + 1)
                nc.gpsimd.memset(B.VB[n][:, :, :, :, :], 0.0).then_inc(zeroed, 1)
            pool.wait_ge(zeroed, 3)
        else:
            split_weights(pool)

    def split_weights(pool):
        W["wait"](pool)
        nc.gpsimd.tensor_copy(B.whi[:, :, :], W["wkvv"][:, :, :]).then_inc(s["w_split"], 1)
        pool.wait_ge(s["w_split"], 1)
        nc.gpsimd.tensor_tensor(B.wlo[:, :, :], W["wkvv"][:, :, :], B.whi[:, :, :].bitcast(F32),
                                ALU.subtract).then_inc(s["w_split"], 1)
        pool.wait_ge(s["w_split"], 2)

    def after(pool):
        if zeroed:
            split_weights(pool)
        split_high(nc, pool, s, B, 0, 0)
        split_low(nc, pool, s, B, 0, 0)

    return before, after, lambda sp: load_context(sp, s, B, W, 0)


def cross_attention(nc, cx, name, X, XNT, con, W, s, B):
    ds = bass.ds
    SCALE = DH ** -0.5
    biased = "bias" in W
    NA = len(ACT_QUADS)
    KB = 256 // 32
    with ExitStack() as mem:
        sb = lambda n, sh, d=F32: mem.enter_context(nc.sbuf_tensor(f"{name}_{n}", sh, d))
        ps = lambda n, sh: mem.enter_context(nc.psum_tensor(f"{name}_{n}", sh, F32))
        wq, wo, bo = (W.get(n) for n in ("wq", "wo", "bo"))
        bias = W.get("bias")
        whi, wlo, ctx_hl, VB, zero = B.whi, B.wlo, B.ctx_hl, B.VB, B.zero
        QT = sb("qt", [P, T * P])
        qbd = [sb(f"qbd{n}", [P, BT, J * G, S]) for n in range(2)]
        KT = [sb(f"kt{n}", [P, BT, KVP]) for n in range(2)]
        VT = sb("vt", [P, BT, 256])
        VS = sb("vs", [P, BT * KB, J * DH])
        v256 = [sb(f"v256{n}", [P, BT]) for n in range(2)]
        probs = [sb(f"probs{n}", [P, J, KV]) for n in range(2)]
        probsT = [sb(f"probsT{n}", [P, J, 256]) for n in range(2)]
        nmax = [sb(f"nmax{n}", [P, J]) for n in range(2)]
        sums = [sb(f"sums{n}", [P, J]) for n in range(2)]
        rsum = [sb(f"rsum{n}", [P, J]) for n in range(2)]
        spread = [sb(f"spread{n}", [P, 2, J, G, DH]) for n in range(2)]
        cc = sb("cc", [P, 3, P])
        sc = [ps(f"sc{n}", [P, 2, 512]) for n in range(2)]
        pj = [ps(f"pj{n}", [P, 512]) for n in range(2)]
        oacc = [ps(f"oacc{n}", [P, 512]) for n in range(2)]
        oacc_v, oacc_last, oacc_rsum, xo = ([o[:, k * P:(k + 1) * P] for o in oacc] for k in range(4))
        block = mem.enter_context(nc.Block())

        def tiles(eng, tile):
            tile(0, 0, True, False)
            tile(1, 1, False, False)
            with eng.Fori(1, T // 2 - 1) as i:
                tile(2 * i, 0, False, False)
                tile(2 * i + 1, 1, False, False)
            tile(T - 2, 0, False, False)
            tile(T - 1, 1, False, True)

        @block.sync
        def _(sp):
            load_context(sp, s, B, W, 1)
            with sp.Fori(2, T) as t:
                load_context(sp, s, B, W, t)

        @block.gpsimd
        def _(pool):
            def spread_values(t, p, h, quadrants=POOL_QUADS):
                wait(pool, s["pv_done"], 4 * (t - 1))
                for g in quadrants:
                    r = slice(32 * g, 32 * g + 32)
                    pool.wait_ge(s["v_turned"], 2 * t + h + 1)
                    nc.gpsimd.tensor_tensor(VB[p][r, 2 * h * KB:2 * (h + 1) * KB, :, g, :].rearrange("p k j d -> p (k j) d"),
                                            VS[r, 2 * h * KB:2 * (h + 1) * KB, :].rearrange("p k (j d) -> p (k j) d", j=J),
                                            zero[r, :].unsqueeze(2).broadcast_to([32, 2 * KB * J, DH]),
                                            ALU.add).then_inc(s["v_pool"], 1)

            def queries(t, p, b):
                wait(pool, s["pair_scored"], 8 * (t - 1))
                nc.gpsimd.tensor_tensor(
                    qbd[p][:, b, :, :],
                    QT[:, ds(P * t + S * b, S)].unsqueeze(1).broadcast_to([P, J * G, S]),
                    con["qmask"].unsqueeze(2).broadcast_to([P, J * G, S]), ALU.mult).then_inc(s["qbd_ready"], 1)

            pool.wait_ge(s["q_ready"], 4)
            for b in range(BT):
                wait(pool, s["qbd_ready"], b)
                queries(0, 0, b)
            pool.wait_ge(s["qbd_ready"], 4)
            split_high(nc, pool, s, B, 1, 1)
            split_low(nc, pool, s, B, 1, 1)
            pool.wait_ge(s["ctx_split"], 4)
            for h in range(2):
                wait(pool, s["v_pool"], h)
                spread_values(0, 0, h)

            def tile(t, p, first, last):
                splits = not (isinstance(t, int) and t + 2 >= T)
                for b in range(BT):
                    n = 4 * t + b
                    q = b % 2
                    wait(pool, s["rl_done"], n - 1)
                    if b == 0 and first:
                        pool.wait_ge(s["v_pool"], 2)
                    elif b == 0:
                        pool.wait_ge(s["qbd_ready"], 4 * t + 4)
                    elif b == 1 and not last:
                        pool.wait_ge(s["qbd_ready"], 4 * t + 6)
                    elif b == 1:
                        pool.wait_ge(s["v_pool"], 2 * t + 2)
                    elif b == 2 and splits:
                        pool.wait_ge(s["ctx_split"], 2 * t + 5)
                    elif b == 3 and not last:
                        pool.wait_ge(s["v_pool"], 2 * t + 3)
                    else:
                        pool.wait_ge(s["spread_ready"], 2 * n)
                    pool.wait_ge(s["exp_done"], 4 * n + 4)
                    nc.gpsimd.tensor_tensor(
                        spread[q][:, 0], con["rowmask"].rearrange("p (j g d) -> p j (g d)", j=J, g=G),
                        probs[q][:, :, KV - 1:KV].broadcast_to([P, J, G * DH]), ALU.mult).then_inc(s["spread_ready"], 1)
                    pool.wait_ge(s["rsum_ready"], n + 1)
                    pool.wait_ge(s["spread_ready"], 2 * n + 1)
                    nc.gpsimd.tensor_tensor(
                        spread[q][:, 1], con["rowmask"].rearrange("p (j g d) -> p j (g d)", j=J, g=G),
                        rsum[q][:, :].unsqueeze(2).broadcast_to([P, J, G * DH]), ALU.mult).then_inc(s["spread_ready"], 1)
                    if b == 0 and not first:
                        pool.wait_ge(s["spread_ready"], 2 * n + 2)
                        spread_values(t, p, 1)
                        if not last:
                            pool.wait_ge(s["v_pool"], 2 * t + 2)
                    if b in (0, 3) and not last:
                        c = 0 if b == 0 else 2
                        pool.wait_ge(s["spread_ready"], 2 * n + 2)
                        queries(t + 1, 1 - p, c)
                        pool.wait_ge(s["qbd_ready"], 4 * t + 5 + c)
                        queries(t + 1, 1 - p, c + 1)
                    if b in (1, 2) and splits:
                        pool.wait_ge(s["spread_ready"], 2 * n + 2)
                        if b == 1:
                            split_high(nc, pool, s, B, t + 2, p)
                        else:
                            split_low(nc, pool, s, B, t + 2, p)
                            pool.wait_ge(s["ctx_split"], 2 * t + 6)
                    if b == 2 and not last:
                        if not splits:
                            pool.wait_ge(s["spread_ready"], 2 * n + 2)
                        spread_values(t + 1, 1 - p, 0)
            tiles(pool, tile)

        @block.scalar
        def _(act):
            W["wait"](act)

            def key_copies(t, p, h):
                wait(act, s["pair_scored"], 8 * (t - 1))
                for c in (2 * h, 2 * h + 1):
                    act.wait_ge(s["k_mm"], 4 * t + c + 1)
                    nc.scalar.activation(KT[p][:, c, :], pj[c % 2][:, 0:KVP], ACT.Identity,
                                         bias=bias[:, 1:2] if biased else 0.0).then_inc(s["k_ready"], 1)

            def value_copies(t, p, h):
                wait(act, s["v_turned"], 2 * (t - 1) + h + 1)
                for c in (2 * h, 2 * h + 1):
                    act.wait_ge(s["v_mm"], 4 * t + c + 1)
                    nc.scalar.activation(VT[:, c, :], pj[c % 2][:, 0:256], ACT.Identity,
                                         bias=bias[:, 2:3] if biased else 0.0).then_inc(s["v_copied"], 1)
                if h == 1:
                    wait(act, s["concat_ready"], t - 1)
                    nc.scalar.activation(v256[p][:, :], pj[1][:, 300:300 + BT], ACT.Identity,
                                         bias=bias[:, 3:4] if biased else 0.0).then_inc(s["v256_ready"], 1)

            def spread_values(t, p, h, quadrants=ACT_QUADS):
                wait(act, s["pv_done"], 4 * (t - 1))
                act.wait_ge(s["v_turned"], 2 * t + h + 1)
                for g in quadrants:
                    r = slice(32 * g, 32 * g + 32)
                    nc.scalar.copy(VB[p][r, 2 * h * KB:2 * (h + 1) * KB, :, g, :].rearrange("p k j d -> p (k j) d"),
                                          VS[r, 2 * h * KB:2 * (h + 1) * KB, :].rearrange("p k (j d) -> p (k j) d", j=J)
                                   ).then_inc(s["v_act"], 1)

            for h in range(2):
                value_copies(0, 0, h)
                key_copies(0, 0, h)
            for h in range(2):
                spread_values(0, 0, h)

            def tile(t, p, first, last):
                for b in range(BT):
                    n = 4 * t + b
                    q = b % 2
                    wait(act, s["p_transposed"], 2 * (n - 1))
                    wait(act, s["spread_ready"], 2 * (n - 1))
                    for j in range(J):
                        act.wait_ge(s["max_ready"], 2 * n + j // 2 + 1)
                        nc.scalar.activation(probs[q][:, j, :], sc[j // 2][:, j % 2, 0:KV], ACT.Exp,
                                             bias=nmax[q][:, j:j + 1],
                                             accum_out=sums[q][:, j:j + 1]).then_inc(s["exp_done"], 1)
                    if not last:
                        (key_copies if b % 2 else value_copies)(t + 1, 1 - p, b // 2)
                    quadrants = ACT_QUADS[2:] if b % 2 else ACT_QUADS[:2]
                    if b >= 2 and not last:
                        spread_values(t + 1, 1 - p, 0, quadrants)
                    if b < 2 and not first:
                        spread_values(t, p, 1, quadrants)
            tiles(act, tile)

        @block.vector
        def _(dve):
            for c in range(4):
                dve.wait_ge(s["q_mm"], c + 1)
                if c == 0:
                    W["wait"](dve)
                src = [sc[0][:, 0, :], sc[0][:, 1, :], sc[1][:, 0, :], sc[1][:, 1, :]][c]
                if biased:
                    nc.vector.tensor_scalar(QT[:, 512 * c:512 * (c + 1)], src, bias[:, 0:1], SCALE,
                                            ALU.add, ALU.mult).then_inc(s["q_ready"], 1)
                else:
                    nc.vector.tensor_scalar(QT[:, 512 * c:512 * (c + 1)], src, SCALE, None,
                                            ALU.mult).then_inc(s["q_ready"], 1)
            if biased:
                nc.vector.tensor_tensor(X[:, :, :], X[:, :, :], bo[:, :].unsqueeze(1).broadcast_to([P, T, D]),
                                        ALU.add).then_inc(s["xb_ready"], 1)

            def values(t, h):
                dve.wait_ge(s["v_copied"], 4 * t + 2 * h + 2)
                wait(dve, s["v_act"], NA * (2 * (t - 1) + h + 1))
                wait(dve, s["v_pool"], 2 * (t - 1) + h + 1)
                nc.vector.transpose(VS[:, 2 * h * KB:2 * (h + 1) * KB, :].rearrange("p k d -> p (k d)"),
                                    VT[:, 2 * h:2 * h + 2, :].rearrange("p c k -> p (c k)")).then_inc(s["v_turned"], 1)

            def finish(t, p):
                dve.wait_ge(s["rl_done"], 4 * t + 4)
                dve.wait_ge(s["v256_ready"], t + 1)
                wait(dve, s["out_mm"], t)
                chain = Chain(dve, s["concat_step"], 2 * t)
                chain.then(nc.vector.tensor_tensor(
                    cc[:, 0, :].rearrange("p (b q) -> p b q", b=BT), oacc_last[p].rearrange("p (b q) -> p b q", b=BT),
                    v256[p][:, :].unsqueeze(2).broadcast_to([P, BT, S]), ALU.mult))
                chain.then(nc.vector.tensor_tensor(cc[:, 1, :], oacc_v[p], cc[:, 0, :], ALU.add))
                nc.vector.tensor_tensor(cc[:, 2, :], oacc_rsum[p], cc[:, 1, :], ALU.mult).then_inc(s["concat_ready"], 1)

            def update(t, p):
                dve.wait_ge(s["out_mm"], t + 1)
                if biased:
                    dve.wait_ge(s["xb_ready"], 1)
                row = X[:, ds(t, 1), :].rearrange("p o d -> p (o d)")
                nc.vector.tensor_tensor(row, xo[p], row, ALU.add).then_inc(s["x_updated"], 1)

            values(0, 0)
            values(0, 1)

            def maximum(n, q, h):
                dve.wait_ge(s["pair_scored"], 2 * n + h + 1)
                if h == 0:
                    wait(dve, s["exp_done"], 4 * (n - 1))
                nc.vector.tensor_reduce(nmax[q][:, 2 * h:2 * h + 2], sc[h][:, :, 0:KV], AX.X, ALU.max,
                                        negate=True).then_inc(s["max_ready"], 1)

            def turn(n, q, h):
                dve.wait_ge(s["exp_done"], 4 * n + 2 * h + 2)
                if h == 0:
                    wait(dve, s["pv_done"], n - 1)
                nc.vector.transpose(probsT[q][:, 2 * h:2 * h + 2, :],
                                    probs[q][:, 2 * h:2 * h + 2, 0:256]).then_inc(s["p_transposed"], 1)

            def second_half(n, q):
                turn(n, q, 1)
                wait(dve, s["spread_ready"], 2 * (n - 1))
                nc.vector.reciprocal(rsum[q][:, :], sums[q][:, :]).then_inc(s["rsum_ready"], 1)

            def tile(t, p, first, last):
                for b in range(BT):
                    n = 4 * t + b
                    if not (b == 0 and first):
                        second_half(n - 1, 1 - b % 2)
                    maximum(n, b % 2, 0)
                    maximum(n, b % 2, 1)
                    turn(n, b % 2, 0)
                    if b == 1 and not first:
                        finish(t - 1, 1 - p)
                    if b == 2 and not first:
                        update(t - 1, 1 - p)
                    if b == 1 and not last:
                        values(t + 1, 0)
                    if b == 3 and not last:
                        values(t + 1, 1)
            tiles(dve, tile)
            second_half(4 * T - 1, 1)
            finish(T - 1, 1)
            update(T - 1, 1)

        @block.tensor
        def _(pe):
            W["wait"](pe)
            for c in range(4):
                nc.tensor.matmul([sc[0][:, 0, :], sc[0][:, 1, :], sc[1][:, 0, :], sc[1][:, 1, :]][c],
                                 wq[:, :], XNT[:, 512 * c:512 * (c + 1)], start=True, stop=True).then_inc(s["q_mm"], 1)
            pe.wait_ge(s["w_split"], 2)

            def project(t, p, h, what):
                pe.wait_ge(s["ctx_split"], 2 * t + 2)
                for c in (2 * h, 2 * h + 1):
                    if what == 0:
                        pe.wait_ge(s["v_copied"], 4 * t + c + 1)
                        if c == 3:
                            pe.wait_ge(s["v256_ready"], t + 1)
                    else:
                        wait(pe, s["k_ready"], 4 * t + c - 1)
                    nc.tensor.matmul(pj[c % 2][:, 0:KVP], whi[:, what, :], ctx_hl[p][:, c, :], start=True, stop=False)
                    last = nc.tensor.matmul(pj[c % 2][:, 0:KVP], wlo[:, what, :], ctx_hl[p][:, c, :], start=False, stop=True)
                    if what == 1 and c == BT - 1:
                        lk = ctx_hl[p][:, :, KV - 1]
                        nc.tensor.matmul(pj[1][:, 300:300 + BT], whi[:, 2, :], lk, start=True, stop=False)
                        last = nc.tensor.matmul(pj[1][:, 300:300 + BT], wlo[:, 2, :], lk, start=False, stop=True)
                    last.then_inc(s["v_mm"] if what else s["k_mm"], 1)

            def score(t, p, b):
                n = 4 * t + b
                pe.wait_ge(s["qbd_ready"], n + 1)
                pe.wait_ge(s["k_ready"], n + 1)
                for j in range(J):
                    wait(pe, s["exp_done"], 4 * (n - 1) + j + 1)
                    last = nc.tensor.matmul(sc[j // 2][:, j % 2, 0:KV],
                                            qbd[p][:, b, G * j:G * (j + 1), :], KT[p][:, b, 0:KV],
                                            start=True, stop=True)
                    if j % 2:
                        last.then_inc(s["pair_scored"], 1)

            def weigh(t, p, b):
                n = 4 * t + b
                q = b % 2
                pe.wait_ge(s["p_transposed"], 2 * n + 2)
                pe.wait_ge(s["v_act"], NA * (2 * t + b // 2 + 1))
                pe.wait_ge(s["v_pool"], 2 * t + b // 2 + 1)
                if b == 0:
                    wait(pe, s["concat_ready"], t - 1)
                    wait(pe, s["x_updated"], t - 1)
                cols = slice(S * b, S * (b + 1))
                for kb in range(KB):
                    for j in range(J):
                        last = nc.tensor.matmul(oacc_v[p][32 * j:32 * j + 32, cols], VB[p][:, KB * b + kb, j, :, :],
                                         probsT[q][:, j, 32 * kb:32 * kb + 32], start=(kb == 0),
                                         stop=(kb == KB - 1))
                last.then_inc(s["pv_done"], 1)

            def spread_rows(t, p, b):
                n = 4 * t + b
                q = b % 2
                cols = slice(S * b, S * (b + 1))
                pe.wait_ge(s["spread_ready"], 2 * n + 2)
                nc.tensor.matmul(oacc_last[p][:, cols], spread[q][:, 0], con["eye4"], start=True, stop=True)
                nc.tensor.matmul(oacc_rsum[p][:, cols], spread[q][:, 1], con["eye4"], start=True,
                                 stop=True).then_inc(s["rl_done"], 1)

            def output(t, p):
                pe.wait_ge(s["concat_ready"], t + 1)
                nc.tensor.matmul(xo[p], cc[:, 2, :], wo[:, :], start=True, stop=True).then_inc(s["out_mm"], 1)

            for h in range(2):
                project(0, 0, h, 1)
                project(0, 0, h, 0)
            pe.wait_ge(s["q_ready"], 4)

            def tile(t, p, first, last):
                for b in range(BT):
                    score(t, p, b)
                    if b >= 2:
                        spread_rows(t, p, b - 2)
                    elif not first:
                        spread_rows(t - 1, 1 - p, b + 2)
                    if b == 2 and not first:
                        output(t - 1, 1 - p)
                    if b > 0:
                        weigh(t, p, b - 1)
                    elif not first:
                        weigh(t - 1, 1 - p, 3)
                    if not last:
                        project(t + 1, 1 - p, b // 2, 1 - b % 2)
            tiles(pe, tile)
            spread_rows(T - 1, 1, 2)
            weigh(T - 1, 1, 3)
            spread_rows(T - 1, 1, 3)
            output(T - 1, 1)


E_H, E_D = 16, 64


def at_tile(ap3, t):
    if isinstance(t, int):
        return ap3[:, t, :]
    return ap3[:, bass.ds(t, 1), :].rearrange("p o n -> p (o n)")


def at_cols(ap2, t, n):
    return ap2[:, t * n:(t + 1) * n] if isinstance(t, int) else ap2[:, bass.ds(t * n, n)]


def self_attention(nc, cx, name, X, XNT, con, W):
    sem = lambda n: cx.enter_context(nc.semaphore(f"{name}_{n}"))
    names = ("zeroed", "xb_ready", "proj_mm", "q_copied", "k_copied", "v_copied", "scored", "masked",
             "max_ready", "shifted", "exp_done", "sum_ready", "rsum_ready", "probs_ready", "p_transposed",
             "z_mm", "z_copied", "out_mm", "x_updated", "xts_ready")
    s = {n: sem(n) for n in names}
    HC = E_H // 2
    HE = E_H * E_D
    NPR = 6
    with ExitStack() as mem:
        sb = lambda n, sh, d=F32: mem.enter_context(nc.sbuf_tensor(f"{name}_{n}", sh, d))
        ps = lambda n, sh: mem.enter_context(nc.psum_tensor(f"{name}_{n}", sh, F32))
        wqkv, wo, bqk, bv, bo = (W[n] for n in ("wqkv", "wo", "bqk", "bv", "bo"))
        QT = [sb(f"q{n}", [P, HC, P]) for n in range(2)]
        KE = [sb(f"k{n}", [P, HC, 2, P]) for n in range(2)]
        V = [sb(f"v{n}", [P, HE]) for n in range(2)]
        sm = sb("sm", [P, E_H, S])
        pr = sb("pr", [P, E_H, S])
        PT = sb("pT", [P, E_H, P])
        nmax, sums, rsum = sb("nmax", [P, E_H]), sb("sums", [P, E_H]), sb("rsum", [P, E_H])
        zT = sb("zT", [P, HC, P])
        xts = sb("xts", [P, P])
        pj = [ps(f"pj{n}", [P, 512]) for n in range(2)]
        sc = ps("sc", [P, E_H, P])
        z = ps("z", [P, HC, P])
        block = mem.enter_context(nc.Block())
        heads = lambda a: a[:, :].unsqueeze(2).broadcast_to([P, E_H, S])
        quads = [slice(S * b, S * b + S) for b in range(BT)]

        def tiles(eng, tile):
            tile(0, 0, True, False)
            tile(1, 1, False, False)
            with eng.Fori(1, T // 2 - 1) as i:
                tile(2 * i, 0, False, False)
                tile(2 * i + 1, 1, False, False)
            tile(T - 2, 0, False, False)
            tile(T - 1, 1, False, True)

        @block.tensor
        def _(pe):
            W["wait"](pe)

            def project(t, m):
                if m < 2:
                    wait(pe, s["v_copied"], 2 * (t - 1) + m + 1)
                elif m < 4:
                    pe.wait_ge(s["q_copied"], HC * t + 4 * (m - 1))
                else:
                    pe.wait_ge(s["k_copied"], 4 * t + 2 * (m - 3))
                if m < 4:
                    xt = at_cols(XNT, t, P)
                    for c in range(4):
                        w = 4 * (m % 2) + c
                        last = nc.tensor.matmul(pj[m % 2][:, c * P:(c + 1) * P], wqkv[:, m // 2, w * P:(w + 1) * P],
                                                xt, start=True, stop=True)
                else:
                    if m == 4:
                        pe.wait_ge(s["xts_ready"], t + 1)
                    w = (m - 4) * 512
                    last = nc.tensor.matmul(pj[m % 2][:, :], xts[:, :], wqkv[:, 2, w:w + 512], start=True, stop=True)
                last.then_inc(s["proj_mm"], 1)

            def score(t, p):
                pe.wait_ge(s["q_copied"], HC * t + HC)
                pe.wait_ge(s["k_copied"], 4 * t + 4)
                wait(pe, s["masked"], BT * t)
                for c in range(HC):
                    last = nc.tensor.matmul(sc[:, 2 * c:2 * c + 2, :], QT[p][:, c, :], KE[p][:, c, :, :],
                                            start=True, stop=True)
                last.then_inc(s["scored"], 1)

            def weigh(t, p):
                pe.wait_ge(s["p_transposed"], BT * t + BT)
                pe.wait_ge(s["v_copied"], 2 * t + 2)
                wait(pe, s["x_updated"], t)
                for h in range(E_H):
                    r = slice(E_D * (h % 2), E_D * (h % 2) + E_D)
                    last = nc.tensor.matmul(z[r, h // 2, :], V[p][:, E_D * h:E_D * h + E_D], PT[:, h, :],
                                            start=True, stop=True)
                last.then_inc(s["z_mm"], 1)

            def output(t):
                pe.wait_ge(s["z_copied"], t + 1)
                for c in range(HC):
                    last = nc.tensor.matmul(z[:, 0, :], zT[:, c, :], wo[:, c, :], start=(c == 0), stop=(c == HC - 1))
                last.then_inc(s["out_mm"], 1)

            def tile(t, p, first, last):
                score(t, p)
                if not last:
                    for m in range(4):
                        project(t + 1, m)
                if not first:
                    weigh(t - 1, 1 - p)
                if not last:
                    project(t + 1, 4)
                    project(t + 1, 5)
                if not first:
                    output(t - 1)
            for m in range(NPR):
                project(0, m)
            tiles(pe, tile)
            weigh(T - 1, 1)
            output(T - 1)

        @block.vector
        def _(dve):
            W["wait"](dve)
            nc.vector.tensor_tensor(X[:, :, :], X[:, :, :], bo[:, :].unsqueeze(1).broadcast_to([P, T, D]),
                                    ALU.add).then_inc(s["xb_ready"], 1)

            def key_copies(t, p):
                if isinstance(t, int) and t < 2:
                    dve.wait_ge(s["zeroed"], 3)
                wait(dve, s["scored"], t - 1)
                for m in range(2):
                    dve.wait_ge(s["proj_mm"], NPR * t + m + 3)
                    for h in range(2):
                        r = slice(E_D * h, E_D * h + E_D)
                        nc.vector.tensor_tensor(
                            KE[p][r, 4 * m:4 * m + 4, h, :], pj[m][r, :].rearrange("p (c n) -> p c n", c=4),
                            bqk[r, 1, 4 * m:4 * m + 4].unsqueeze(2).broadcast_to([E_D, 4, P]),
                            ALU.add).then_inc(s["k_copied"], 1)

            def value_copies(t, p):
                wait(dve, s["z_mm"], t - 1)
                for m in range(2):
                    dve.wait_ge(s["proj_mm"], NPR * t + m + 5)
                    nc.vector.tensor_tensor(V[p][:, 512 * m:512 * (m + 1)], pj[m][:, :], bv[:, 512 * m:512 * (m + 1)],
                                            ALU.add).then_inc(s["v_copied"], 1)

            def update(t):
                dve.wait_ge(s["out_mm"], t + 1)
                dve.wait_ge(s["xb_ready"], 1)
                nc.vector.tensor_tensor(at_tile(X, t), z[:, 0, :], at_tile(X, t), ALU.add).then_inc(s["x_updated"], 1)

            key_copies(0, 0)
            value_copies(0, 0)

            def tile(t, p, first, last):
                dve.wait_ge(s["scored"], t + 1)
                wait(dve, s["exp_done"], t)
                for b, r in enumerate(quads):
                    nc.vector.scalar_tensor_tensor(sm[r, :, :], sc[r, :, S * b:S * b + S], E_D ** -0.5,
                                                   con["causal"][r, :, :], ALU.mult, ALU.add).then_inc(s["masked"], 1)
                dve.wait_ge(s["masked"], BT * t + BT)
                nc.vector.tensor_reduce(nmax[:, :], sm[:, :, :], AX.X, ALU.max).then_inc(s["max_ready"], 1)
                if not last:
                    key_copies(t + 1, 1 - p)
                dve.wait_ge(s["exp_done"], t + 1)
                nc.vector.reduce_sum(sums[:, :], pr[:, :, :], AX.X).then_inc(s["sum_ready"], 1)
                dve.wait_ge(s["sum_ready"], t + 1)
                nc.vector.reciprocal(rsum[:, :], sums[:, :]).then_inc(s["rsum_ready"], 1)
                if not last:
                    value_copies(t + 1, 1 - p)
                if isinstance(t, int) and t == 0:
                    dve.wait_ge(s["zeroed"], 3)
                dve.wait_ge(s["probs_ready"], t + 1)
                wait(dve, s["z_mm"], t)
                for b, r in enumerate(quads):
                    nc.vector.transpose(PT[r, :, S * b:S * b + S], pr[r, :, :]).then_inc(s["p_transposed"], 1)
                if not first:
                    update(t - 1)
            tiles(dve, tile)
            update(T - 1)

        @block.gpsimd
        def _(pool):
            for n, a in enumerate((KE[0], KE[1])):
                nc.gpsimd.memset(a[:, :, :, :], 0.0).then_inc(s["zeroed"], 1)
            nc.gpsimd.memset(PT[:, :, :], 0.0).then_inc(s["zeroed"], 1)
            pool.wait_ge(s["zeroed"], 3)

            def tile(t, p, first, last):
                pool.wait_ge(s["max_ready"], t + 1)
                wait(pool, s["probs_ready"], t)
                nc.gpsimd.tensor_tensor(sm[:, :, :], sm[:, :, :], heads(nmax), ALU.subtract).then_inc(s["shifted"], 1)
                pool.wait_ge(s["rsum_ready"], t + 1)
                pool.wait_ge(s["shifted"], t + 1)
                nc.gpsimd.tensor_tensor(pr[:, :, :], pr[:, :, :], heads(rsum), ALU.mult).then_inc(s["probs_ready"], 1)
            tiles(pool, tile)

        @block.scalar
        def _(act):
            W["wait"](act)

            def stage(t):
                wait(act, s["proj_mm"], NPR * t)
                nc.scalar.copy(xts[:, :], at_cols(XNT, t, P)).then_inc(s["xts_ready"], 1)

            def query_copies(t, p):
                wait(act, s["scored"], t - 1)
                for m in range(2):
                    act.wait_ge(s["proj_mm"], NPR * t + m + 1)
                    for c in range(4):
                        w = 4 * m + c
                        nc.scalar.activation(QT[p][:, w, :], pj[m][:, c * P:(c + 1) * P], ACT.Identity,
                                             bias=bqk[:, 0, w:w + 1]).then_inc(s["q_copied"], 1)
            stage(0)
            query_copies(0, 0)

            def heads_out(t):
                act.wait_ge(s["z_mm"], t + 1)
                wait(act, s["out_mm"], t)
                nc.scalar.copy(zT[:, :, :], z[:, :, :]).then_inc(s["z_copied"], 1)

            def tile(t, p, first, last):
                if not last:
                    stage(t + 1)
                    query_copies(t + 1, 1 - p)
                act.wait_ge(s["shifted"], t + 1)
                wait(act, s["p_transposed"], BT * t)
                nc.scalar.activation(pr[:, :, :], sm[:, :, :], ACT.Exp).then_inc(s["exp_done"], 1)
                if not first:
                    heads_out(t - 1)
            tiles(act, tile)
            heads_out(T - 1)


I_FF = 352
CH = (128, 128, 96)


class RouterCount:

    def __init__(self, nc, cx):
        (self.logits_mm, self.neg_ready, self.exp_done, self.mask_ready, self.counters_ready, self.ranks_mm,
         self.step) = (cx.enter_context(nc.semaphore("router_" + n)) for n in (
            "logits_mm", "neg_ready", "exp_done", "mask_ready", "counters_ready", "ranks_mm", "step"))
        self.calls = self.steps = 0


def router(nc, count_of, name, XNT, R, con, W, n_exp, top2, shared):
    call = count_of.calls
    count_of.calls = call + 1
    n_tiles = slot_tiles(n_exp, 2 if top2 else 1)
    with ExitStack() as mem:
        sb = lambda n, sh, d=F32: mem.enter_context(nc.sbuf_tensor(f"{name}_{n}", sh, d))
        rw, rb = W["rw"], W["rb"]
        pr, eq, pr2, slots = (sb(n, [P, T, n_exp]) for n in ("pr", "eq", "pr2", "slots"))
        hot = [sb(f"hot{c}", [P, T, n_exp]) for c in range(2 if top2 else 1)]
        mask = sb("mask", [P, T, n_exp], BF16)
        ones, before = sb("ones", [P, P], BF16), sb("before", [P, P], BF16)
        best, first, total, second, slot = (sb(n, [P, T]) for n in ("best", "first", "total", "second", "slot"))
        count, tiles, base = (sb(n, [P, n_exp]) for n in ("count", "tiles", "base"))
        over = sb("over", [P, n_exp, T])
        pairs = sb("pairs", [P, n_exp, n_exp])
        begun = sb("begun", [P, n_tiles, n_exp])
        owner = sb("owner", [P, n_tiles])
        banks = [mem.enter_context(nc.psum_tensor(f"{name}_{n}", [P, 512], F32)) for n in ("lg", "rank", "tot")]
        lgv, rank, tot = (k[:, 0:T * n_exp].rearrange("p (t e) -> p t e", e=n_exp) for k in banks)
        block = mem.enter_context(nc.Block())
        wide = lambda a: a[:, :].unsqueeze(2).broadcast_to([P, T, n_exp])
        experts = lambda a: a.unsqueeze(1).broadcast_to([P, T, n_exp])

        @block.tensor
        def _(pe):
            W["wait"](pe)
            for t in range(T):
                last = nc.tensor.matmul(lgv[:, t, :], XNT[:, t * P:(t + 1) * P], rw[:, :], start=True, stop=True)
            last.then_inc(count_of.logits_mm, 1)
            pe.wait_ge(count_of.counters_ready, 2 * call + 2)
            pe.wait_ge(count_of.mask_ready, call + 1)
            nc.tensor.matmul(tot, ones[:, :], mask[:, :, :], start=True, stop=True)
            nc.tensor.matmul(rank, before[:, :], mask[:, :, :], start=True, stop=False)
            for t in range(T - 1):
                last = nc.tensor.matmul(rank[:, t + 1:, :], ones[:, :],
                                        mask[:, t:t + 1, :].broadcast_to([P, T - 1 - t, n_exp]),
                                        start=False, stop=(t == T - 2))
            last.then_inc(count_of.ranks_mm, 1)

        @block.scalar
        def _(act):
            nc.scalar.copy(ones[:, :], con["ones"]).then_inc(count_of.counters_ready, 1)
            nc.scalar.copy(before[:, :], con["before"]).then_inc(count_of.counters_ready, 1)
            act.wait_ge(count_of.neg_ready, call + 1)
            nc.scalar.activation(pr[:, :, :], pr[:, :, :], ACT.Exp, scale=-1.0).then_inc(count_of.exp_done, 1)

        @block.vector
        def _(dve):
            chain = Chain(dve, count_of.step, count_of.steps)
            v = nc.vector
            W["wait"](dve)
            dve.wait_ge(count_of.logits_mm, call + 1)
            if shared:
                chain.then(v.tensor_tensor(pr[:, :, :], lgv, experts(rb[:, :]), ALU.add))
                v.tensor_scalar(pr[:, :, :], pr[:, :, :], 50.0, -50.0, ALU.min, ALU.max).then_inc(count_of.neg_ready, 1)
            else:
                v.tensor_tensor(pr[:, :, :], lgv, experts(rb[:, :]), ALU.add).then_inc(count_of.neg_ready, 1)
            dve.wait_ge(count_of.exp_done, call + 1)
            chain.then(v.tensor_scalar_add(pr[:, :, :], pr[:, :, :], 1.0))
            chain.then(v.reciprocal(pr[:, :, :], pr[:, :, :]))

            def pick(src, best, hot):
                chain.then(v.tensor_reduce(best[:, :], src[:, :, :], AX.X, ALU.max))
                chain.then(v.tensor_tensor(eq[:, :, :], src[:, :, :], wide(best), ALU.is_equal))
                chain.then(v.tensor_tensor(eq[:, :, :], eq[:, :, :], experts(con["rank"][:, 0:n_exp]), ALU.mult))
                chain.then(v.tensor_reduce(first[:, :], eq[:, :, :], AX.X, ALU.max))
                chain.then(v.tensor_tensor(hot[:, :, :], eq[:, :, :], wide(first), ALU.is_equal))

            pick(pr, best, hot[0])
            if top2:
                chain.then(v.scalar_tensor_tensor(pr2[:, :, :], hot[0][:, :, :], -2.0, pr[:, :, :], ALU.mult, ALU.add))
                pick(pr2, second, hot[1])
                v.tensor_tensor(mask[:, :, :], hot[0][:, :, :], hot[1][:, :, :], ALU.add).then_inc(count_of.mask_ready, 1)
            else:
                v.tensor_copy(mask[:, :, :], hot[0][:, :, :]).then_inc(count_of.mask_ready, 1)
            if not top2:
                chain.then(v.tensor_scalar(best[:, :], best[:, :], 1e-8, 1.0 - 1e-8, ALU.max, ALU.min))
                chain.then(v.tensor_scalar(total[:, :], best[:, :], 0.5, 1e-8, ALU.add, ALU.add))
                chain.then(v.tensor_scalar(total[:, :], total[:, :], 0.5, 2.0, ALU.max, ALU.min))
                chain.then(v.reciprocal(total[:, :], total[:, :]))
                chain.then(v.tensor_scalar(R.shared[:, :], total[:, :], 0.5, None, ALU.mult))
                chain.then(v.tensor_tensor(R.gate[:, 0, :], best[:, :], total[:, :], ALU.mult))
            else:
                chain.then(v.tensor_tensor(total[:, :], best[:, :], second[:, :], ALU.add))
                chain.then(v.tensor_scalar_add(total[:, :], total[:, :], 1e-20))
                chain.then(v.reciprocal(total[:, :], total[:, :]))
                chain.then(v.tensor_tensor(R.gate[:, 0, :], best[:, :], total[:, :], ALU.mult))
                chain.then(v.tensor_tensor(R.gate[:, 1, :], second[:, :], total[:, :], ALU.mult))

            dve.wait_ge(count_of.ranks_mm, call + 1)
            chain.then(v.tensor_reduce(count[:, :], tot.rearrange("p t e -> p e t"), AX.X, ALU.add))
            chain.then(v.tensor_scalar(count[:, :], count[:, :], 1.0 / P, None, ALU.mult))
            chain.then(v.tensor_tensor(over[:, :, :], count[:, :].unsqueeze(2).broadcast_to([P, n_exp, T]),
                                       con["steps"][:, 0:T].unsqueeze(1).broadcast_to([P, n_exp, T]), ALU.is_gt))
            chain.then(v.tensor_reduce(tiles[:, :], over[:, :, :], AX.X, ALU.add))
            chain.then(v.tensor_tensor(pairs[:, :, :], tiles[:, :].unsqueeze(1).broadcast_to([P, n_exp, n_exp]),
                                       con["lower"][:, 0:n_exp, 0:n_exp], ALU.mult))
            chain.then(v.tensor_reduce(base[:, :], pairs[:, :, :], AX.X, ALU.add))
            chain.then(v.scalar_tensor_tensor(slots[:, :, :], experts(base[:, :]), float(P), rank, ALU.mult, ALU.add))
            for c, h in enumerate(hot):
                chain.then(v.tensor_tensor(eq[:, :, :], h[:, :, :], slots[:, :, :], ALU.mult))
                chain.then(v.tensor_reduce(slot[:, :], eq[:, :, :], AX.X, ALU.add))
                chain.then(v.tensor_copy(R.slot[:, c, :], slot[:, :]))
            chain.then(v.tensor_tensor(begun[:, :, :], con["steps"][:, 0:n_tiles].unsqueeze(2)
                                       .broadcast_to([P, n_tiles, n_exp]),
                                       base[:, :].unsqueeze(1).broadcast_to([P, n_tiles, n_exp]), ALU.is_ge))
            chain.then(v.tensor_reduce(owner[:, :], begun[:, :, 1:], AX.X, ALU.add))
            chain.then(v.tensor_copy(R.expert[:, 0:n_tiles], owner[:, :]))
            count_of.steps += chain.n


def slot_tiles(n_exp, choices):
    return (T * P * choices + n_exp * (P - 1)) // P


def sparse_experts(nc, cx, name, X, XNT, XR, R, con, W, n_exp, choices, shared):
    ds = bass.ds
    sem = lambda k: cx.enter_context(nc.semaphore(f"{name}_{k}"))
    NT = slot_tiles(n_exp, choices)
    NC = len(CH)
    SU = NC * (T // 4) if shared else 0
    SB = T // 4 if shared else 0
    names = ("up_mm", "silu_done", "h_ready", "down_mm", "y_done", "x_turned", "x_copied", "scattered",
             "y_stored", "x_updated", "w_staged", "x_staged")
    s = {k: sem(k) for k in names}
    LOADS = ((0, 2), (2, 6), (6, NT))
    loaded = [sem(f"loaded{n}") for n in range(len(LOADS))]
    gathered = [sem(f"gathered{n}") for n in range(T // 4)]
    with ExitStack() as mem:
        sb = lambda k, sh, d=F32: mem.enter_context(nc.sbuf_tensor(f"{name}_{k}", sh, d))
        ps = lambda k, sh: mem.enter_context(nc.psum_tensor(f"{name}_{k}", sh, F32))
        w13, w2 = W["w13"], W["w2"]
        xs = [sb(f"xs{k}", [P, D]) for k in range(2)]
        rows = sb("rows", [P, NT, D])
        xT = [sb(f"xT{k}", [P, P]) for k in range(2)]
        wt = [sb(f"wt{k}", [P, 1, 2, NC * P]) for k in range(2)]
        g = [sb(f"g{k}", [P, 512]) for k in range(2)]
        h = [sb(f"h{k}", [P, NC, 512]) for k in range(2)]
        back = [XR] + [sb(f"back{c}", [P, T, D]) for c in range(1, choices)]
        u1 = [ps(f"u1{k}", [P, 512]) for k in range(2)]
        u3 = [ps(f"u3{k}", [P, 512]) for k in range(2)]
        xt_ps = [ps(f"xt{k}", [P, 512]) for k in range(2)]
        y = [ps(f"y{k}", [P, 4, P]) for k in range(2)]
        block = mem.enter_context(nc.Block())
        inbox, outbox = W["inbox"], W["outbox"]

        def tiles(eng, tile):
            tile(0, 0, True, False)
            tile(1, 1, False, False)
            with eng.Fori(1, NT // 2 - 1) as i:
                tile(2 * i, 0, False, False)
                tile(2 * i + 1, 1, False, False)
            tile(NT - 2, 0, False, False)
            tile(NT - 1, 1, False, True)

        @block.gpsimd
        def _(pool):
            W["wait_zeroed"](pool)
            for c in range(choices):
                for t in range(T):
                    pool.indirect_dma_start(inbox, bass.IndirectOffsetOnAxis(R.slot[:, c, t:t + 1], 0),
                                            XR[:, t, :], None).then_inc(s["scattered"], 16)
            pool.wait_ge(s["y_stored"], 16 * NT)
            for n in range(T // 4):
                for t in range(4 * n, 4 * n + 4):
                    for c in range(choices):
                        pool.indirect_dma_start(back[c][:, t, :], None, outbox,
                                                bass.IndirectOffsetOnAxis(R.slot[:, c, t:t + 1], 0)
                                                ).then_inc(gathered[n], 16)

        @block.sync
        def _(sp):
            sp.wait_ge(s["scattered"], 16 * T * choices)

            for (a, b), done in zip(LOADS, loaded):
                sp.dma_start(rows[:, a:b, :], inbox[P * a:P * b, :].rearrange("(t p) d -> p t d", p=P)).then_inc(done, 16)

            def tile(t, p, first, last):
                sp.wait_ge(s["y_done"], SB + t + 1)
                sp.dma_start(outbox[ds(P * t, P), :], at_tile(rows, t)).then_inc(s["y_stored"], 16)
            tiles(sp, tile)

        @block.tensor
        def _(pe):
            W["wait"](pe)

            def shared_up(k, c):
                m = NC * k + c
                wait(pe, s["h_ready"], m - 1)
                for j, u in ((0, u1), (1, u3)):
                    last = nc.tensor.matmul(u[m % 2][:, :], w13[:, n_exp, j, c * P:(c + 1) * P],
                                            XNT[:, k * 512:(k + 1) * 512], start=True, stop=True)
                last.then_inc(s["up_mm"], 1)

            def shared_down(k):
                wait(pe, s["y_done"], k - 1)
                pe.wait_ge(s["h_ready"], NC * (k + 1))
                for t in range(4):
                    for c in range(NC):
                        last = nc.tensor.matmul(y[k % 2][:, t, :], h[k % 2][:, c, t * P:(t + 1) * P],
                                                w2[:, n_exp, c, :], start=(c == 0), stop=(c == NC - 1))
                last.then_inc(s["down_mm"], 1)

            for k in range(SB):
                for c in range(NC):
                    shared_up(k, c)
                    if k and c == 1:
                        shared_down(k - 1)
            if shared:
                shared_down(SB - 1)

            def turn(t, p):
                pe.wait_ge(s["x_staged"], t + 1)
                wait(pe, s["x_copied"], t - 1)
                nc.tensor.transpose(xt_ps[p][:, 0:P], xs[p][:, :], con["ident"]).then_inc(s["x_turned"], 1)

            def up(t, p):
                pe.wait_ge(s["w_staged"], t + 1)
                pe.wait_ge(s["x_copied"], t + 1)
                wait(pe, s["h_ready"], SU + t - 1)
                for j, u in ((0, u1), (1, u3)):
                    for c in range(NC):
                        last = nc.tensor.matmul(u[p][:, c * P:(c + 1) * P], wt[p][:, 0, j, c * P:(c + 1) * P],
                                                xT[p][:, :], start=True, stop=True)
                last.then_inc(s["up_mm"], 1)

            def down(t, p):
                e = pe.value_load(R.expert[0:1, ds(t, 1)], min_val=0, max_val=n_exp - 1)
                wait(pe, s["y_done"], SB + t - 1)
                pe.wait_ge(s["h_ready"], SU + t + 1)
                for c in range(NC):
                    last = nc.tensor.matmul(y[p][:, 0, :], h[p][:, c, 0:P],
                                            w2[:, ds(e, 1), c, :].rearrange("p o n -> p (o n)"),
                                            start=(c == 0), stop=(c == NC - 1))
                last.then_inc(s["down_mm"], 1)

            def tile(t, p, first, last):
                if not last:
                    turn(t + 1, 1 - p)
                up(t, p)
                if not first:
                    down(t - 1, 1 - p)
            turn(0, 0)
            tiles(pe, tile)
            down(NT - 1, 1)

        @block.scalar
        def _(act):
            def silu(m, p, n):
                act.wait_ge(s["up_mm"], m + 1)
                wait(act, s["h_ready"], m - 1)
                nc.scalar.activation(g[p][:, 0:n], u1[p][:, 0:n], ACT.Silu).then_inc(s["silu_done"], 1)

            for m in range(SU):
                silu(m, m % 2, 512)

            def copy(t, p):
                act.wait_ge(s["x_turned"], t + 1)
                wait(act, s["up_mm"], SU + t - 1)
                nc.scalar.copy(xT[p][:, :], xt_ps[p][:, 0:P]).then_inc(s["x_copied"], 1)

            def place(t, p):
                wait(act, s["x_turned"], t - 1)
                nc.scalar.copy(xs[p][:, :], at_tile(rows, t)).then_inc(s["x_staged"], 1)

            def tile(t, p, first, last):
                if not (isinstance(t, int) and t + 2 >= NT):
                    place(t + 2, p)
                if not last:
                    copy(t + 1, 1 - p)
                silu(SU + t, p, NC * P)

            act.wait_ge(loaded[0], 16)
            place(0, 0)
            place(1, 1)
            copy(0, 0)
            act.wait_ge(loaded[1], 16)
            tile(0, 0, True, False)
            tile(1, 1, False, False)
            tile(2, 0, False, False)
            tile(3, 1, False, False)
            act.wait_ge(loaded[2], 16)
            with act.Fori(2, NT // 2 - 1) as i:
                tile(2 * i, 0, False, False)
                tile(2 * i + 1, 1, False, False)
            tile(NT - 2, 0, False, False)
            tile(NT - 1, 1, False, True)

        @block.vector
        def _(dve):
            def hidden(m, p, dst, n, shape):
                dve.wait_ge(s["silu_done"], m + 1)
                view = (lambda a: a) if shape is None else (lambda a: a.rearrange("p (c n) -> p c n", c=shape))
                nc.vector.tensor_tensor(dst, view(g[p][:, 0:n]), view(u3[p][:, 0:n]), ALU.mult).then_inc(s["h_ready"], 1)

            def shared_update(k):
                dve.wait_ge(s["down_mm"], k + 1)
                for t in range(4):
                    tt = 4 * k + t
                    last = nc.vector.scalar_tensor_tensor(X[:, tt, :], y[k % 2][:, t, :], R.shared[:, tt:tt + 1],
                                                          X[:, tt, :], ALU.mult, ALU.add)
                last.then_inc(s["y_done"], 1)

            for k in range(SB):
                for c in range(NC):
                    if c == 0 and k > 1:
                        dve.wait_ge(s["down_mm"], k - 1)
                    m = NC * k + c
                    hidden(m, m % 2, h[k % 2][:, c, :], 512, None)
                    if k and c == 1:
                        shared_update(k - 1)
            if shared:
                shared_update(SB - 1)

            def stage(t, p):
                e = dve.value_load(R.expert[0:1, ds(t, 1)], min_val=0, max_val=n_exp - 1)
                wait(dve, s["up_mm"], SU + t - 1)
                nc.vector.tensor_scalar(wt[p][:, :, :, :], w13[:, ds(e, 1), :, :], 1.0, None,
                                        ALU.mult).then_inc(s["w_staged"], 1)

            def take(t, p):
                dve.wait_ge(s["down_mm"], SB + t + 1)
                nc.vector.tensor_copy(at_tile(rows, t), y[p][:, 0, :]).then_inc(s["y_done"], 1)

            def tile(t, p, first, last):
                if not last:
                    stage(t + 1, 1 - p)
                wait(dve, s["down_mm"], SB + t - 1)
                hidden(SU + t, p, h[p][:, :, 0:P], NC * P, NC)
                if not first:
                    take(t - 1, 1 - p)
            stage(0, 0)
            tiles(dve, tile)
            take(NT - 1, 1)
            dve.wait_ge(s["y_done"], SB + NT)
            for n in range(T // 4):
                dve.wait_ge(gathered[n], 16 * 4 * choices)
                for c in range(choices):
                    if c:
                        dve.wait_ge(s["x_updated"], n + 1)
                    for t in range(4 * n, 4 * n + 4):
                        last = nc.vector.scalar_tensor_tensor(X[:, t, :], back[c][:, t, :], R.gate[:, c, t:t + 1],
                                                              X[:, t, :], ALU.mult, ALU.add)
                    if c == 0:
                        last.then_inc(s["x_updated"], 1)


def rope_attention(nc, cx, name, X, XNT, con, W):
    sem = lambda n: cx.enter_context(nc.semaphore(f"{name}_{n}"))
    names = ("xb_ready", "xs_ready", "qkv_mm", "qk_ready", "v_ready", "cos_done", "swap_done", "roped",
             "qkT_mm", "qkT_copied", "scored", "max_ready", "bias_ready", "exp_done", "rsum_ready", "probs_ready",
             "pT_ready", "spread", "o_mm", "o_copied", "out_mm", "x_updated")
    s = {n: sem(n) for n in names}
    TB = 4
    NBLK = T // TB
    HALF = D // 2
    with ExitStack() as mem:
        sb = lambda n, sh, d=F32: mem.enter_context(nc.sbuf_tensor(f"{name}_{n}", sh, d))
        ps = lambda n, sh: mem.enter_context(nc.psum_tensor(f"{name}_{n}", sh, F32))
        wqkv, wo, bqkv, bo = (W[n] for n in ("wqkv", "wo", "bqkv", "bo"))
        xs = sb("xs", [P, TB * P])
        qk = sb("qk", [P, TB * 2, 2, HALF])
        v = sb("v", [P, TB, D])
        qc, qs, qr = sb("qc", [P, TB * 2, 2, HALF]), sb("qs", [P, TB * 2, 2, HALF]), sb("qr", [P, TB * 2, 2, HALF])
        qkT = sb("qkT", [P, TB * 2, P])
        nmax, sums, rsum = sb("nmax", [P, TB]), sb("sums", [P, TB]), sb("rsum", [P, TB])
        pr, prn, prT = sb("pr", [P, TB, S]), sb("prn", [P, TB, S]), sb("prT", [P, TB, S])
        pbd = sb("pbd", [P, TB, BT, S])
        oT = sb("oT", [P, TB, P])
        qkv_ps = ps("qkv_ps", [P, TB, 512])
        tr_ps = ps("tr_ps", [P, 2, 4, P])
        sc_ps = ps("sc_ps", [P, 512])
        o_ps = ps("o_ps", [P, TB, P])
        block = mem.enter_context(nc.Block())

        def blocks(eng, work):
            work(0)
            with eng.Fori(1, NBLK) as i:
                work(i)

        @block.tensor
        def _(pe):
            W["wait"](pe)
            def work(i):
                pe.wait_ge(s["xs_ready"], i + 1)
                wait(pe, s["x_updated"], i)
                for t in range(TB):
                    last = nc.tensor.matmul(qkv_ps[:, t, 0:3 * D], xs[:, t * P:(t + 1) * P], wqkv[:, :],
                                            start=True, stop=True)
                last.then_inc(s["qkv_mm"], 1)
                pe.wait_ge(s["roped"], i + 1)
                for m in range(2 * TB):
                    last = nc.tensor.transpose(tr_ps[:, m // 4, m % 4, :],
                                               qr[:, m, :, :].rearrange("p h d -> p (h d)"), con["ident"])
                last.then_inc(s["qkT_mm"], 1)
                pe.wait_ge(s["qkT_copied"], i + 1)
                for t in range(TB):
                    for b in range(BT):
                        r = slice(S * b, S * b + S)
                        last = nc.tensor.matmul(sc_ps[r, S * t:S * t + S], qkT[:, 2 * t, r], qkT[:, 2 * t + 1, r],
                                                start=True, stop=True)
                last.then_inc(s["scored"], 1)
                pe.wait_ge(s["spread"], i + 1)
                for t in range(TB):
                    last = nc.tensor.matmul(o_ps[:, t, :], v[:, t, :], pbd[:, t, :, :], start=True, stop=True)
                last.then_inc(s["o_mm"], 1)
                pe.wait_ge(s["o_copied"], i + 1)
                for t in range(TB):
                    last = nc.tensor.matmul(qkv_ps[:, 0, t * P:(t + 1) * P], oT[:, t, :], wo[:, :], start=True, stop=True)
                last.then_inc(s["out_mm"], 1)
            blocks(pe, work)

        @block.scalar
        def _(act):
            def work(i):
                wait(act, s["qkv_mm"], i)
                nc.scalar.copy(xs[:, :], at_cols(XNT, i, TB * P)).then_inc(s["xs_ready"], 1)
                act.wait_ge(s["qkT_mm"], i + 1)
                nc.scalar.copy(qkT[:, :, :].rearrange("p m n -> p (m n)"),
                               tr_ps[:, :, :, :].rearrange("p a m n -> p (a m n)")).then_inc(s["qkT_copied"], 1)
                act.wait_ge(s["bias_ready"], i + 1)
                wait(act, s["probs_ready"], i)
                for t in range(TB):
                    nc.scalar.activation(pr[:, t, :], sc_ps[:, S * t:S * t + S], ACT.Exp, bias=nmax[:, t:t + 1],
                                         scale=D ** -0.5, accum_out=sums[:, t:t + 1]).then_inc(s["exp_done"], 1)
                act.wait_ge(s["o_mm"], i + 1)
                nc.scalar.copy(oT[:, :, :], o_ps[:, :, :]).then_inc(s["o_copied"], 1)
            blocks(act, work)

        @block.gpsimd
        def _(pool):
            def work(i):
                pool.wait_ge(s["qk_ready"], i + 1)
                wait(pool, s["spread"], i)
                nc.gpsimd.tensor_tensor(qc[:, :, :, :].rearrange("p m h d -> p m (h d)"),
                                        qk[:, :, :, :].rearrange("p m h d -> p m (h d)"),
                                        con["cos"].unsqueeze(1).broadcast_to([P, 2 * TB, D]), ALU.mult
                                        ).then_inc(s["cos_done"], 1)
                pool.wait_ge(s["pT_ready"], i + 1)
                pool.wait_ge(s["cos_done"], i + 1)
                nc.gpsimd.tensor_tensor(pbd[:, :, :, :], prT[:, :, :].unsqueeze(2).broadcast_to([P, TB, BT, S]),
                                        con["seqmask"].unsqueeze(1).unsqueeze(3).broadcast_to([P, TB, BT, S]),
                                        ALU.mult).then_inc(s["spread"], 1)
            blocks(pool, work)

        @block.vector
        def _(dve):
            W["wait"](dve)
            nc.vector.tensor_tensor(X[:, :, :], X[:, :, :], bo[:, :].unsqueeze(1).broadcast_to([P, T, D]),
                                    ALU.add).then_inc(s["xb_ready"], 1)
            dve.wait_ge(s["xb_ready"], 1)
            def work(i):
                dve.wait_ge(s["qkv_mm"], i + 1)
                nc.vector.tensor_tensor(
                    qk[:, :, :, :].rearrange("p (t m) h d -> p t (m h d)", t=TB), qkv_ps[:, :, 0:2 * D],
                    bqkv[:, 0:2 * D].unsqueeze(1).broadcast_to([P, TB, 2 * D]), ALU.add).then_inc(s["qk_ready"], 1)
                dve.wait_ge(s["qk_ready"], i + 1)
                for h in range(2):
                    nc.vector.tensor_tensor(qs[:, :, h, :], qk[:, :, 1 - h, :],
                                            con["sin"][:, h * HALF:(h + 1) * HALF].unsqueeze(1)
                                            .broadcast_to([P, 2 * TB, HALF]), ALU.mult).then_inc(s["swap_done"], 1)
                dve.wait_ge(s["cos_done"], i + 1)
                dve.wait_ge(s["swap_done"], 2 * i + 2)
                nc.vector.tensor_tensor(qr[:, :, :, :], qc[:, :, :, :], qs[:, :, :, :], ALU.add).then_inc(s["roped"], 1)
                nc.vector.tensor_tensor(v[:, :, :], qkv_ps[:, :, 2 * D:3 * D],
                                        bqkv[:, 2 * D:3 * D].unsqueeze(1).broadcast_to([P, TB, D]),
                                        ALU.add).then_inc(s["v_ready"], 1)
                dve.wait_ge(s["scored"], i + 1)
                wait(dve, s["exp_done"], 4 * i)
                nc.vector.tensor_reduce(nmax[:, :], sc_ps[:, 0:TB * S].rearrange("p (t k) -> p t k", k=S), AX.X,
                                        ALU.max, negate=True).then_inc(s["max_ready"], 1)
                dve.wait_ge(s["max_ready"], i + 1)
                nc.vector.tensor_scalar(nmax[:, :], nmax[:, :], D ** -0.5, None, ALU.mult).then_inc(s["bias_ready"], 1)
                dve.wait_ge(s["exp_done"], 4 * i + 4)
                nc.vector.reciprocal(rsum[:, :], sums[:, :]).then_inc(s["rsum_ready"], 1)
                dve.wait_ge(s["rsum_ready"], i + 1)
                nc.vector.tensor_tensor(prn[:, :, :], pr[:, :, :], rsum[:, :].unsqueeze(2).broadcast_to([P, TB, S]),
                                        ALU.mult).then_inc(s["probs_ready"], 1)
                dve.wait_ge(s["probs_ready"], i + 1)
                nc.vector.transpose(prT[:, :, :].rearrange("p t k -> p (t k)"),
                                    prn[:, :, :].rearrange("p t k -> p (t k)")).then_inc(s["pT_ready"], 1)
                dve.wait_ge(s["out_mm"], i + 1)
                xb = X[:, slice(0, TB) if isinstance(i, int) else bass.ds(i * TB, TB), :].rearrange("p t d -> p (t d)")
                nc.vector.tensor_tensor(xb, qkv_ps[:, 0, :], xb, ALU.add).then_inc(s["x_updated"], 1)
            blocks(dve, work)

CONSTS = (("ident", P), ("qmask", J * G), ("rowmask", P), ("eye4", S), ("causal", E_H * S), ("rank", 9), ("ones", P), ("before", P), ("lower", 81),
          ("steps", 40), ("scalars", 2),
          ("cos", D), ("sin", D), ("seqmask", BT))


class Routes:
    pass


def perceiver(nc, a, out):
    with ExitStack() as cx:
        sb = lambda n, s: cx.enter_context(nc.sbuf_tensor(n, s, F32))
        sem = lambda n: cx.enter_context(nc.semaphore(n))
        X = sb("x", [P, T, D])
        XNT = sb("xnt", [P, T * P])
        R = Routes()
        R.gate, R.shared = sb("gate", [P, 2, T]), sb("shared_gate", [P, T])
        R.slot = cx.enter_context(nc.sbuf_tensor("slot", [P, 2, T], I32))
        R.expert = cx.enter_context(nc.sbuf_tensor("tile_expert", [P, slot_tiles(9, 2)], I32))
        cs = sb("consts", [P, sum(w for _, w in CONSTS)])
        con, at = {}, 0
        for n, w in CONSTS:
            con[n] = cs[:, at:at + w]
            at += w
        con["eps"], con["power"] = con["scalars"][:, 0:1], con["scalars"][:, 1:2]
        con["lower"] = con["lower"].rearrange("p (f e) -> p f e", f=9)
        con["causal"] = con["causal"].rearrange("p (h k) -> p h k", k=S)
        loaded, stored = sem("loaded"), sem("stored")

        stages = {"x0_": ("wq", "wo", "wkvv", "bias", "bo"), "a0_": ("lnwb", "wqkv", "wo", "bqk", "bv", "bo"),
                  "r0_": ("rw", "rb"), "x1_": ("wq", "wo", "wkvv"), "a1_": ("wqkv", "wo", "bqkv", "bo"),
                  "r1_": ("rw", "rb")}
        first_loaded, later_loaded = sem("first_loaded"), sem("later_loaded")
        n_later = sum(len(names) for pre, names in stages.items() if pre != "x0_")
        W = {}
        for pre, names in stages.items():
            W[pre] = {n: sb(pre + n, list(a[pre + n].shape)) for n in names}
            W[pre]["wait"] = ((lambda eng: eng.wait_ge(first_loaded, 16 * len(stages["x0_"]))) if pre == "x0_" else
                              (lambda eng: eng.wait_ge(later_loaded, 16 * n_later)))

        wide = len(CH) * P
        w13, w2, zeros = sb("w13", [P, 9, 2, wide]), sb("w2", [P, 9, len(CH), D]), sb("zeros", [P, 1, D])
        zeros_ready, zeroed = sem("zeros_ready"), sem("zeroed")
        experts_loaded = sem("experts_loaded")
        routed = {"f0_": (7, 1), "f1_": (9, 2)}
        F = {}
        for pre, (n_exp, choices) in routed.items():
            n_rows = slot_tiles(n_exp, choices) * P
            F[pre] = dict(w13=w13, w2=w2, rows=n_rows,
                          inbox=nc.dram_tensor(pre + "inbox", (n_rows, D), F32, kind="Internal").ap(),
                          outbox=nc.dram_tensor(pre + "outbox", (n_rows, D), F32, kind="Internal").ap())
            F[pre]["wait"] = lambda eng, layer=len(F): eng.wait_ge(experts_loaded, 32 * layer)
        for pre in F:
            F[pre]["wait_zeroed"] = lambda eng: eng.wait_ge(zeroed, 16 * len(F))

        def load_experts(pre):
            def loads(sp):
                n = a[pre + "w13"].shape[1]
                sp.dma_start(w13[:, 0:n, :, :], a[pre + "w13"]).then_inc(experts_loaded, 16)
                sp.dma_start(w2[:, 0:n, :, :], a[pre + "w2"]).then_inc(experts_loaded, 16)
            return loads

        def first_loads(sp):
            load_experts("f0_")(sp)
            sp.wait_ge(zeros_ready, 1)
            for pre in F:
                k = F[pre]["rows"] // P
                sp.dma_start(F[pre]["inbox"].rearrange("(p k) d -> p k d", k=k),
                             zeros[:, :, :].broadcast_to([P, k, D])).then_inc(zeroed, 16)

        cross_zeroed = sem("cross_zeroed")
        cross = CrossBuffers(nc, cx)
        CS = {n: cross_semaphores(nc, cx, n) for n in ("x0", "x1")}
        CX = {n: dict(W[n + "_"], ctx=a["ctx"]) for n in CS}
        wait_x = lambda eng: eng.wait_ge(loaded, 32)

        with nc.Block() as block:
            @block.gpsimd
            def _(pool):
                nc.gpsimd.memset(zeros[:, :, :], 0.0).then_inc(zeros_ready, 1)

            @block.sync
            def _(sp):
                sp.dma_start(X[:, :, :], a["x"]).then_inc(loaded, 16)
                sp.dma_start(cs[:, :], a["consts"]).then_inc(loaded, 16)
                for pre, names in stages.items():
                    for n in names:
                        sp.dma_start(W[pre][n][tuple(slice(None) for _ in a[pre + n].shape)],
                                     a[pre + n]).then_inc(first_loaded if pre == "x0_" else later_loaded, 16)

        norms = LayernormCount(nc, cx)
        before, after, first_context = cross_start(nc, CS["x0"], cross, CX["x0"], cross_zeroed)
        layernorm_stage(nc, norms, "n0", X, XNT, con, loads=first_context, before=before, after=after, wait_x=wait_x)
        cross_attention(nc, cx, "x0", X, XNT, con, CX["x0"], CS["x0"], cross)

        lnwb = W["a0_"]["lnwb"]
        layernorm_stage(nc, norms, "n1", X, XNT, con, twice=(lnwb[:, 0:1], lnwb[:, 1:2]), wait_wb=W["a0_"]["wait"],
                        loads=first_loads)
        self_attention(nc, cx, "a0", X, XNT, con, W["a0_"])

        with nc.sbuf_tensor("rows0", [P, T, D], F32) as XR:
            layernorm_stage(nc, norms, "n2", X, XNT, con, rows=XR)
            counts = RouterCount(nc, cx)
            router(nc, counts, "r0", XNT, R, con, W["r0_"], 7, top2=False, shared=True)
            sparse_experts(nc, cx, "f0", X, XNT, XR, R, con, F["f0_"], 7, 1, shared=True)

        before, after, first_context = cross_start(nc, CS["x1"], cross, CX["x1"])

        def second_loads(sp):
            first_context(sp)
            load_experts("f1_")(sp)
        layernorm_stage(nc, norms, "n3", X, XNT, con, loads=second_loads, before=before, after=after)
        cross_attention(nc, cx, "x1", X, XNT, con, CX["x1"], CS["x1"], cross)

        layernorm_stage(nc, norms, "n4", X, XNT, con)
        rope_attention(nc, cx, "a1", X, XNT, con, W["a1_"])

        with nc.sbuf_tensor("rows1", [P, T, D], F32) as XR:
            layernorm_stage(nc, norms, "n5", X, XNT, con, rows=XR)
            router(nc, counts, "r1", XNT, R, con, W["r1_"], 9, top2=True, shared=False)
            sparse_experts(nc, cx, "f1", X, XNT, XR, R, con, F["f1_"], 9, 2, shared=False)

        with nc.Block() as block:
            @block.sync
            def _(sp):
                sp.dma_start(out, X[:, :, :]).then_inc(stored, 16)
                sp.wait_ge(stored, 16)


def kernel(**inputs):
    import numpy as np
    import concourse.bacc as bacc
    from concourse.bass_utils import run_bass_kernel_spmd

    i = {k: np.asarray(v) for k, v in inputs.items()}
    f32 = np.float32
    tile = lambda a: np.broadcast_to(a, (P, a.shape[-1]))
    twice = lambda w: np.concatenate([w, w], 0)
    r = np.arange(P)

    qmask = np.zeros((P, J * G), f32)
    qmask[r, G * (r // DH % J) + r // (J * DH)] = 1
    rowmask = (r[None, :] // DH % G == r[:, None] // S).astype(f32)
    causal = np.where(np.tril(np.ones((S, S))) > 0, 0, -3e38).astype(f32)
    half = D // 2
    inv = (1.0 / 10000.0 ** (np.arange(half, dtype=f32) / f32(half))).astype(f32)
    ang = np.arange(S, dtype=f32)[:, None] * inv[None]
    seqmask = (r[:, None] // S == np.arange(BT)[None]).astype(f32)
    consts = {
        "ident": np.eye(P, dtype=f32), "qmask": qmask, "rowmask": rowmask,
        "eye4": np.tile(np.eye(S, dtype=f32), (BT, 1)), "causal": np.tile(causal, (BT, E_H)),
        "rank": tile(np.arange(9, 0, -1).astype(f32)),
        "ones": np.ones((P, P), f32), "before": np.triu(np.ones((P, P), f32), 1),
        "lower": tile(np.tril(np.ones((9, 9), f32), -1).reshape(-1)), "steps": tile(np.arange(40).astype(f32)),
        "scalars": tile(np.array([EPS, -0.5], f32)), "cos": np.tile(np.cos(ang), (BT, 2)),
        "sin": np.tile(np.concatenate([-np.sin(ang), np.sin(ang)], 1), (BT, 1)), "seqmask": seqmask,
    }

    rows = np.array([(J * g + j) * DH + d for j in range(J) for g in range(G) for d in range(DH)])
    arrays = {
        "x": i["x"].reshape(T, P, D).transpose(1, 0, 2),
        "consts": np.concatenate([consts[n] for n, _ in CONSTS], 1),
        "ctx": np.pad(i["ctx_512"].transpose(2, 0, 1), ((0, 0), (0, 0), (0, KVP - KV))),
    }

    def cross(pre, wq, wk, wv, wo):
        arrays[pre + "wq"], arrays[pre + "wo"] = wq, wo[rows]
        arrays[pre + "wkvv"] = np.stack([twice(wk), twice(wv), twice(wv[:, rows])], 1)

    cross("x0_", *(i[f"L0_xattn_W{c}"] for c in "qkvo"))
    bq, bk, bv, bo = (i[f"L0_xattn_b{c}"] for c in "qkvo")
    arrays["x0_bias"], arrays["x0_bo"] = np.stack([bq, bk, bv, bv[rows]], 1), tile(bo)
    wkv = i["L1_xattn_Wkv"]
    cross("x1_", i["L1_xattn_Wq"].T, wkv[:D].T, wkv[D:].T, i["L1_xattn_Wo"].T)

    heads = lambda w: w.transpose(1, 0, 2).reshape(D, E_H * E_D)
    arrays["a0_lnwb"] = np.stack([i["L0_attn_ln_w"], i["L0_attn_ln_b"]], 1)
    arrays["a0_wqkv"] = np.stack([heads(i[f"L0_attn_W_{c}"]) for c in "qkv"], 1)
    arrays["a0_wo"] = i["L0_attn_W_o"].reshape(E_H // 2, P, D).transpose(1, 0, 2)
    arrays["a0_bqk"] = np.stack([i[f"L0_attn_b_{c}"].reshape(E_H // 2, P).T for c in "qk"], 1)
    arrays["a0_bv"] = tile(i["L0_attn_b_v"].reshape(-1))
    arrays["a0_bo"] = tile(i["L0_attn_b_o"])

    arrays["a1_wqkv"], arrays["a1_wo"] = i["L1_attn_w_qkv"].T, i["L1_attn_w_o"].T
    arrays["a1_bqkv"], arrays["a1_bo"] = tile(i["L1_attn_b_qkv"]), tile(i["L1_attn_b_o"])

    def experts(pre, w1, w2, w3, rw, rb):
        pad = P * len(CH) - I_FF
        up = np.stack([w1.transpose(2, 0, 1), w3.transpose(2, 0, 1)], 2)
        arrays[pre + "w13"] = np.pad(up, ((0, 0), (0, 0), (0, 0), (0, pad)))
        down = np.pad(w2.transpose(0, 2, 1), ((0, 0), (0, pad), (0, 0))).reshape(len(w2), len(CH), P, D)
        arrays[pre + "w2"] = down.transpose(2, 0, 1, 3)
        arrays[pre.replace("f", "r") + "rw"], arrays[pre.replace("f", "r") + "rb"] = rw.T, tile(rb)

    join = lambda *n: np.concatenate([i[k] if i[k].ndim != 2 or "gate" in k else i[k][None] for k in n])
    experts("f0_", *(join(f"L0_ffn_ew{m}", f"L0_ffn_sw{m}") for m in (1, 2, 3)),
            i["L0_ffn_router_w"], i["L0_ffn_routing_bias"])
    experts("f1_", *(join(f"L1_ffn_w{m}", f"L1_ffn_new_w{m}") for m in (1, 2, 3)),
            join("L1_ffn_gate_weight", "L1_ffn_new_gate_weight"), np.pad(i["L1_ffn_gate_bias"], (8, 0)))

    nc = bacc.Bacc("TRN2", target_bir_lowering=False, num_devices=1)
    arrays = {f"in_{n}": np.ascontiguousarray(v, dtype=f32) for n, v in arrays.items()}
    aps = {n[3:]: nc.dram_tensor(n, v.shape, F32, kind="ExternalInput").ap() for n, v in arrays.items()}
    out = nc.dram_tensor("out", (P, T, D), F32, kind="ExternalOutput").ap()
    perceiver(nc, aps, out)
    got = run_bass_kernel_spmd(nc, [arrays], core_ids=[0]).results[0]["out"]
    return got.transpose(1, 0, 2).reshape(B, S, D)
```

```python
import concourse.bass as bass
from concourse import mybir
from contextlib import ExitStack

F32 = mybir.dt.float32
F32R = mybir.dt.float32r
BF16 = mybir.dt.bfloat16
I32 = mybir.dt.int32
ALU = mybir.AluOpType
ACT = mybir.ActivationFunctionType
AX = mybir.AxisListType

P = 128
D = 128
B, S = 64, 32
T = B * S // P
BT = P // S
KV = 257
KVP = 258
CW = 64
H, DH = 16, 8
G, J = 4, 4
EPS = 1e-5
ACT_QUADS, POOL_QUADS = (0, 1, 2), (3,)


def wait(eng, sem, value):
    if not isinstance(value, int) or value > 0:
        eng.wait_ge(sem, value)


class Chain:

    def __init__(self, eng, sem, base=0):
        self.eng, self.sem, self.base, self.n = eng, sem, base, 0

    def then(self, ins):
        self.n += 1
        ins.then_inc(self.sem, 1)
        self.eng.wait_ge(self.sem, self.base + self.n)


class LayernormCount:

    def __init__(self, nc, cx):
        (self.stats_ready, self.mv_ready, self.rstd_ready, self.shift_ready, self.xn_dve, self.xn_act, self.xt_ready,
         self.step) = (cx.enter_context(nc.semaphore("norm_" + n)) for n in (
            "stats_ready", "mv_ready", "rstd_ready", "shift_ready", "xn_dve", "xn_act", "xt_ready", "step"))
        self.stages = self.steps = 0
        self.stats = cx.enter_context(nc.sbuf_tensor("norm_stats", [P, T, 6], F32))

    def take(self, nc, X, t):
        one = (lambda a: a[:, t, :]) if isinstance(t, int) else (
            lambda a: a[:, bass.ds(t, 1), :].rearrange("p o n -> p (o n)"))
        return nc.vector.bn_stats(one(self.stats), one(X))


def layernorm_stage(nc, count, name, X, XNT, con, twice=None, wait_wb=None, rows=None,
                    loads=None, before=None, after=None, wait_x=None):
    NB = 4
    NG = T // NB
    stage = count.stages
    count.stages += 1
    with ExitStack() as mem:
        sb = lambda n, s, d=F32: mem.enter_context(nc.sbuf_tensor(f"{name}_{n}", s, d))
        stats = count.stats
        mv = sb("mv", [P, T, 2])
        rvar, rstd, again = sb("rvar", [P, T]), sb("rstd", [P, T]), sb("again", [P, T])
        shift = sb("shift", [P, T])
        XN = rows or sb("rows", [P, T, D])
        xt_ps = [mem.enter_context(nc.psum_tensor(f"{name}_xt{n}", [P, NB * P], F32)) for n in range(NG)]
        block = mem.enter_context(nc.Block())
        w, b = twice or (1.0, 0.0)
        group = lambda n: slice(n * NB * P, (n + 1) * NB * P)

        @block.sync
        def _(sp):
            if loads:
                loads(sp)

        @block.vector
        def _(dve):
            if wait_x:
                for t in range(T):
                    if t % NB == 0:
                        wait_x(dve, t // NB)
                    last = count.take(nc, X, t)
                last.then_inc(count.stats_ready, 1)
                dve.wait_ge(count.stats_ready, 1)
            for t in range(T):
                last = nc.vector.bn_aggr(mv[:, t, :], stats[:, t, :])
            last.then_inc(count.mv_ready, 1)
            dve.wait_ge(count.rstd_ready, stage + 1)
            nc.vector.scalar_tensor_tensor(shift[:, :], mv[:, :, 0], -1.0, rstd[:, :], ALU.mult,
                                           ALU.mult).then_inc(count.shift_ready, 1)
            for n in range(NG):
                for t in range(NB * n, NB * n + NB - 1):
                    last = nc.vector.tensor_scalar(XN[:, t, :], X[:, t, :], mv[:, t, 0:1], rstd[:, t:t + 1],
                                                   ALU.subtract, ALU.mult)
                last.then_inc(count.xn_dve, 1)
            if wait_wb:
                wait_wb(dve)
            for n in (1, 3):
                dve.wait_ge(count.xt_ready, stage * NG + n + 1)
                nc.vector.tensor_scalar(XNT[:, group(n)], xt_ps[n][:, :], w, b, ALU.mult, ALU.add)

        @block.gpsimd
        def _(pool):
            if before:
                before(pool)
            if wait_x:
                wait_x(pool, None)
            pool.wait_ge(count.mv_ready, stage + 1)
            chain = Chain(pool, count.step, count.steps)
            mul = lambda out, a, b: nc.gpsimd.tensor_tensor(out[:, :], a, b[:, :], ALU.mult)
            add_eps = lambda out, a: nc.gpsimd.tensor_tensor(out[:, :], a, con["eps"].broadcast_to([P, T]), ALU.add)
            root = lambda out, a: nc.gpsimd.tensor_tensor(out[:, :], a[:, :], con["power"].broadcast_to([P, T]), ALU.pow)
            chain.then(add_eps(rvar, mv[:, :, 1]))
            if twice:
                chain.then(root(again, rvar))
                chain.then(mul(rvar, mv[:, :, 1], again))
                chain.then(mul(rvar, rvar[:, :], again))
                chain.then(add_eps(rvar, rvar[:, :]))
                chain.then(root(rvar, rvar))
                mul(rstd, rvar[:, :], again).then_inc(count.rstd_ready, 1)
            else:
                root(rstd, rvar).then_inc(count.rstd_ready, 1)
            count.steps += chain.n
            if after:
                pool.wait_ge(count.rstd_ready, stage + 1)
                after(pool)

        @block.scalar
        def _(act):
            if wait_x:
                wait_x(act, None)
            act.wait_ge(count.shift_ready, stage + 1)
            for n in range(NG):
                t = NB * n + NB - 1
                nc.scalar.activation(XN[:, t, :], X[:, t, :], ACT.Identity, bias=shift[:, t:t + 1],
                                     scale=rstd[:, t:t + 1]).then_inc(count.xn_act, 1)
            if wait_wb:
                wait_wb(act)
            for n in (0, 2):
                act.wait_ge(count.xt_ready, stage * NG + n + 1)
                nc.scalar.activation(XNT[:, group(n)], xt_ps[n][:, :], ACT.Identity, bias=b, scale=w)

        @block.tensor
        def _(pe):
            if wait_x:
                wait_x(pe, None)
            for n in range(NG):
                pe.wait_ge(count.xn_dve, stage * NG + n + 1)
                pe.wait_ge(count.xn_act, stage * NG + n + 1)
                for k in range(NB):
                    last = nc.tensor.transpose(xt_ps[n][:, k * P:(k + 1) * P], XN[:, n * NB + k, :], con["ident"])
                last.then_inc(count.xt_ready, 1)


class CrossBuffers:

    def __init__(self, nc, cx):
        sb = lambda n, sh, d=F32: cx.enter_context(nc.sbuf_tensor(f"cross_{n}", sh, d))
        self.whi, self.wlo = sb("whi", [P, 3, D], F32R), sb("wlo", [P, 3, D], F32R)
        self.ctx_raw = sb("ctx_raw", [P, BT, KVP])
        self.ctx_hl = [sb(f"ctx_hl{n}", [P, BT, KVP], F32R) for n in range(2)]
        self.VB = [sb(f"vb{n}", [P, BT * 256 // 32, J, G, DH]) for n in range(2)]
        self.zero = sb("zero", [P, 1])


def cross_semaphores(nc, cx, name):
    names = ("ctx_loaded", "w_split", "ctx_split", "q_mm", "q_ready", "qbd_ready", "pair_scored",
             "max_ready", "exp_done", "p_transposed", "rsum_ready", "spread_ready", "pv_done", "rl_done", "concat_step",
             "concat_ready", "out_mm", "x_updated", "k_mm", "k_ready", "v_mm", "v_copied", "v256_ready",
             "v_turned", "v_act", "v_pool", "xb_ready")
    return {n: cx.enter_context(nc.semaphore(f"{name}_{n}")) for n in names}


def load_context(sp, s, B, W, t):
    wait(sp, s["ctx_split"], 2 * t)
    for half in range(2):
        sp.dma_start(B.ctx_raw[half * CW:(half + 1) * CW, :, :],
                     W["ctx"][:, bass.ds(BT * t, BT), :]).then_inc(s["ctx_loaded"], 16)


def split_high(nc, pool, s, B, t, p):
    pool.wait_ge(s["ctx_loaded"], 32 * t + 32)
    wait(pool, s["k_mm"], 4 * (t - 1))
    nc.gpsimd.tensor_tensor(B.ctx_hl[p][:, :, :], B.ctx_raw[:, :, :],
                            B.zero[:, :].unsqueeze(2).broadcast_to([P, BT, KVP]), ALU.add).then_inc(s["ctx_split"], 1)


def split_low(nc, pool, s, B, t, p):
    pool.wait_ge(s["ctx_split"], 2 * t + 1)
    nc.gpsimd.tensor_tensor(B.ctx_hl[p][CW:P, :, :], B.ctx_raw[CW:P, :, :],
                            B.ctx_hl[p][CW:P, :, :].bitcast(F32), ALU.subtract).then_inc(s["ctx_split"], 1)


def cross_start(nc, s, B, W, zeroed=None):

    def before(pool):
        if zeroed:
            nc.gpsimd.memset(B.zero[:, :], 0.0).then_inc(zeroed, 1)
            for n in range(2):
                pool.wait_ge(zeroed, n + 1)
                nc.gpsimd.memset(B.VB[n][:, :, :, :, :], 0.0).then_inc(zeroed, 1)
            pool.wait_ge(zeroed, 3)
        else:
            split_weights(pool)

    def split_weights(pool):
        W["wait"](pool)
        nc.gpsimd.tensor_copy(B.whi[:, :, :], W["wkvv"][:, :, :]).then_inc(s["w_split"], 1)
        pool.wait_ge(s["w_split"], 1)
        nc.gpsimd.tensor_tensor(B.wlo[:, :, :], W["wkvv"][:, :, :], B.whi[:, :, :].bitcast(F32),
                                ALU.subtract).then_inc(s["w_split"], 1)
        pool.wait_ge(s["w_split"], 2)

    def after(pool):
        if zeroed:
            split_weights(pool)
        split_high(nc, pool, s, B, 0, 0)
        split_low(nc, pool, s, B, 0, 0)

    return before, after, lambda sp: load_context(sp, s, B, W, 0)


def cross_attention(nc, cx, norms, name, X, XNT, con, W, s, B):
    ds = bass.ds
    SCALE = DH ** -0.5
    biased = "bias" in W
    NA = len(ACT_QUADS)
    KB = 256 // 32
    with ExitStack() as mem:
        sb = lambda n, sh, d=F32: mem.enter_context(nc.sbuf_tensor(f"{name}_{n}", sh, d))
        ps = lambda n, sh: mem.enter_context(nc.psum_tensor(f"{name}_{n}", sh, F32))
        wq, wo, bo = (W.get(n) for n in ("wq", "wo", "bo"))
        bias = W.get("bias")
        whi, wlo, ctx_hl, VB, zero = B.whi, B.wlo, B.ctx_hl, B.VB, B.zero
        QT = sb("qt", [P, T * P])
        qbd = [sb(f"qbd{n}", [P, BT, J * G, S]) for n in range(2)]
        KT = [sb(f"kt{n}", [P, BT, KVP]) for n in range(2)]
        VT = sb("vt", [P, BT, 256])
        VS = sb("vs", [P, BT * KB, J * DH])
        v256 = [sb(f"v256{n}", [P, BT]) for n in range(2)]
        probs = [sb(f"probs{n}", [P, J, KV]) for n in range(2)]
        probsT = [sb(f"probsT{n}", [P, J, 256]) for n in range(2)]
        nmax = [sb(f"nmax{n}", [P, J]) for n in range(2)]
        sums = [sb(f"sums{n}", [P, J]) for n in range(2)]
        rsum = [sb(f"rsum{n}", [P, J]) for n in range(2)]
        spread = [sb(f"spread{n}", [P, 2, J, G, DH]) for n in range(2)]
        cc = sb("cc", [P, 3, P])
        sc = [ps(f"sc{n}", [P, 2, 512]) for n in range(2)]
        pj = [ps(f"pj{n}", [P, 512]) for n in range(2)]
        oacc = [ps(f"oacc{n}", [P, 512]) for n in range(2)]
        oacc_v, oacc_last, oacc_rsum, xo = ([o[:, k * P:(k + 1) * P] for o in oacc] for k in range(4))
        block = mem.enter_context(nc.Block())

        def tiles(eng, tile):
            tile(0, 0, True, False)
            tile(1, 1, False, False)
            with eng.Fori(1, T // 2 - 1) as i:
                tile(2 * i, 0, False, False)
                tile(2 * i + 1, 1, False, False)
            tile(T - 2, 0, False, False)
            tile(T - 1, 1, False, True)

        @block.sync
        def _(sp):
            load_context(sp, s, B, W, 1)
            with sp.Fori(2, T) as t:
                load_context(sp, s, B, W, t)

        @block.gpsimd
        def _(pool):
            def spread_values(t, p, h, quadrants=POOL_QUADS):
                wait(pool, s["pv_done"], 4 * (t - 1))
                for g in quadrants:
                    r = slice(32 * g, 32 * g + 32)
                    pool.wait_ge(s["v_turned"], 2 * t + h + 1)
                    nc.gpsimd.tensor_tensor(VB[p][r, 2 * h * KB:2 * (h + 1) * KB, :, g, :].rearrange("p k j d -> p (k j) d"),
                                            VS[r, 2 * h * KB:2 * (h + 1) * KB, :].rearrange("p k (j d) -> p (k j) d", j=J),
                                            zero[r, :].unsqueeze(2).broadcast_to([32, 2 * KB * J, DH]),
                                            ALU.add).then_inc(s["v_pool"], 1)

            def queries(t, p, b):
                wait(pool, s["pair_scored"], 8 * (t - 1))
                nc.gpsimd.tensor_tensor(
                    qbd[p][:, b, :, :],
                    QT[:, ds(P * t + S * b, S)].unsqueeze(1).broadcast_to([P, J * G, S]),
                    con["qmask"].unsqueeze(2).broadcast_to([P, J * G, S]), ALU.mult).then_inc(s["qbd_ready"], 1)

            pool.wait_ge(s["q_ready"], 4)
            for b in range(BT):
                wait(pool, s["qbd_ready"], b)
                queries(0, 0, b)
            pool.wait_ge(s["qbd_ready"], 4)
            split_high(nc, pool, s, B, 1, 1)
            split_low(nc, pool, s, B, 1, 1)
            pool.wait_ge(s["ctx_split"], 4)
            for h in range(2):
                wait(pool, s["v_pool"], h)
                spread_values(0, 0, h)

            def tile(t, p, first, last):
                splits = not (isinstance(t, int) and t + 2 >= T)
                for b in range(BT):
                    n = 4 * t + b
                    q = b % 2
                    wait(pool, s["rl_done"], n - 1)
                    if b == 0 and first:
                        pool.wait_ge(s["v_pool"], 2)
                    elif b == 0:
                        pool.wait_ge(s["qbd_ready"], 4 * t + 4)
                    elif b == 1 and not last:
                        pool.wait_ge(s["qbd_ready"], 4 * t + 6)
                    elif b == 1:
                        pool.wait_ge(s["v_pool"], 2 * t + 2)
                    elif b == 2 and splits:
                        pool.wait_ge(s["ctx_split"], 2 * t + 5)
                    elif b == 3 and not last:
                        pool.wait_ge(s["v_pool"], 2 * t + 3)
                    else:
                        pool.wait_ge(s["spread_ready"], 2 * n)
                    pool.wait_ge(s["exp_done"], 4 * n + 4)
                    nc.gpsimd.tensor_tensor(
                        spread[q][:, 0], con["rowmask"].rearrange("p (j g d) -> p j (g d)", j=J, g=G),
                        probs[q][:, :, KV - 1:KV].broadcast_to([P, J, G * DH]), ALU.mult).then_inc(s["spread_ready"], 1)
                    pool.wait_ge(s["rsum_ready"], n + 1)
                    pool.wait_ge(s["spread_ready"], 2 * n + 1)
                    nc.gpsimd.tensor_tensor(
                        spread[q][:, 1], con["rowmask"].rearrange("p (j g d) -> p j (g d)", j=J, g=G),
                        rsum[q][:, :].unsqueeze(2).broadcast_to([P, J, G * DH]), ALU.mult).then_inc(s["spread_ready"], 1)
                    if b == 0 and not first:
                        pool.wait_ge(s["spread_ready"], 2 * n + 2)
                        spread_values(t, p, 1)
                        if not last:
                            pool.wait_ge(s["v_pool"], 2 * t + 2)
                    if b in (0, 3) and not last:
                        c = 0 if b == 0 else 2
                        pool.wait_ge(s["spread_ready"], 2 * n + 2)
                        queries(t + 1, 1 - p, c)
                        pool.wait_ge(s["qbd_ready"], 4 * t + 5 + c)
                        queries(t + 1, 1 - p, c + 1)
                    if b in (1, 2) and splits:
                        pool.wait_ge(s["spread_ready"], 2 * n + 2)
                        if b == 1:
                            split_high(nc, pool, s, B, t + 2, p)
                        else:
                            split_low(nc, pool, s, B, t + 2, p)
                            pool.wait_ge(s["ctx_split"], 2 * t + 6)
                    if b == 2 and not last:
                        if not splits:
                            pool.wait_ge(s["spread_ready"], 2 * n + 2)
                        spread_values(t + 1, 1 - p, 0)
            tiles(pool, tile)

        @block.scalar
        def _(act):
            W["wait"](act)

            def key_copies(t, p, h):
                wait(act, s["pair_scored"], 8 * (t - 1))
                for c in (2 * h, 2 * h + 1):
                    act.wait_ge(s["k_mm"], 4 * t + c + 1)
                    nc.scalar.activation(KT[p][:, c, :], pj[c % 2][:, 0:KVP], ACT.Identity,
                                         bias=bias[:, 1:2] if biased else 0.0).then_inc(s["k_ready"], 1)

            def value_copies(t, p, h):
                wait(act, s["v_turned"], 2 * (t - 1) + h + 1)
                for c in (2 * h, 2 * h + 1):
                    act.wait_ge(s["v_mm"], 4 * t + c + 1)
                    nc.scalar.activation(VT[:, c, :], pj[c % 2][:, 0:256], ACT.Identity,
                                         bias=bias[:, 2:3] if biased else 0.0).then_inc(s["v_copied"], 1)
                if h == 1:
                    wait(act, s["concat_ready"], t - 1)
                    nc.scalar.activation(v256[p][:, :], pj[1][:, 300:300 + BT], ACT.Identity,
                                         bias=bias[:, 3:4] if biased else 0.0).then_inc(s["v256_ready"], 1)

            def spread_values(t, p, h, quadrants=ACT_QUADS):
                wait(act, s["pv_done"], 4 * (t - 1))
                act.wait_ge(s["v_turned"], 2 * t + h + 1)
                for g in quadrants:
                    r = slice(32 * g, 32 * g + 32)
                    nc.scalar.copy(VB[p][r, 2 * h * KB:2 * (h + 1) * KB, :, g, :].rearrange("p k j d -> p (k j) d"),
                                          VS[r, 2 * h * KB:2 * (h + 1) * KB, :].rearrange("p k (j d) -> p (k j) d", j=J)
                                   ).then_inc(s["v_act"], 1)

            for h in range(2):
                value_copies(0, 0, h)
                key_copies(0, 0, h)
            for h in range(2):
                spread_values(0, 0, h)

            def tile(t, p, first, last):
                for b in range(BT):
                    n = 4 * t + b
                    q = b % 2
                    wait(act, s["p_transposed"], 2 * (n - 1))
                    wait(act, s["spread_ready"], 2 * (n - 1))
                    for j in range(J):
                        act.wait_ge(s["max_ready"], 2 * n + j // 2 + 1)
                        nc.scalar.activation(probs[q][:, j, :], sc[j // 2][:, j % 2, 0:KV], ACT.Exp,
                                             bias=nmax[q][:, j:j + 1],
                                             accum_out=sums[q][:, j:j + 1]).then_inc(s["exp_done"], 1)
                    if not last:
                        (key_copies if b % 2 else value_copies)(t + 1, 1 - p, b // 2)
                    quadrants = ACT_QUADS[2:] if b % 2 else ACT_QUADS[:2]
                    if b >= 2 and not last:
                        spread_values(t + 1, 1 - p, 0, quadrants)
                    if b < 2 and not first:
                        spread_values(t, p, 1, quadrants)
            tiles(act, tile)

        @block.vector
        def _(dve):
            for c in range(4):
                dve.wait_ge(s["q_mm"], c + 1)
                if c == 0:
                    W["wait"](dve)
                src = [sc[0][:, 0, :], sc[0][:, 1, :], sc[1][:, 0, :], sc[1][:, 1, :]][c]
                if biased:
                    nc.vector.tensor_scalar(QT[:, 512 * c:512 * (c + 1)], src, bias[:, 0:1], SCALE,
                                            ALU.add, ALU.mult).then_inc(s["q_ready"], 1)
                else:
                    nc.vector.tensor_scalar(QT[:, 512 * c:512 * (c + 1)], src, SCALE, None,
                                            ALU.mult).then_inc(s["q_ready"], 1)
            if biased:
                add_bias = lambda: nc.vector.tensor_tensor(
                    X[:, :, :], X[:, :, :], bo[:, :].unsqueeze(1).broadcast_to([P, T, D]),
                    ALU.add).then_inc(s["xb_ready"], 1)

            def values(t, h):
                dve.wait_ge(s["v_copied"], 4 * t + 2 * h + 2)
                wait(dve, s["v_act"], NA * (2 * (t - 1) + h + 1))
                wait(dve, s["v_pool"], 2 * (t - 1) + h + 1)
                nc.vector.transpose(VS[:, 2 * h * KB:2 * (h + 1) * KB, :].rearrange("p k d -> p (k d)"),
                                    VT[:, 2 * h:2 * h + 2, :].rearrange("p c k -> p (c k)")).then_inc(s["v_turned"], 1)

            def finish(t, p):
                dve.wait_ge(s["rl_done"], 4 * t + 4)
                dve.wait_ge(s["v256_ready"], t + 1)
                wait(dve, s["out_mm"], t)
                chain = Chain(dve, s["concat_step"], 2 * t)
                chain.then(nc.vector.tensor_tensor(
                    cc[:, 0, :].rearrange("p (b q) -> p b q", b=BT), oacc_last[p].rearrange("p (b q) -> p b q", b=BT),
                    v256[p][:, :].unsqueeze(2).broadcast_to([P, BT, S]), ALU.mult))
                chain.then(nc.vector.tensor_tensor(cc[:, 1, :], oacc_v[p], cc[:, 0, :], ALU.add))
                nc.vector.tensor_tensor(cc[:, 2, :], oacc_rsum[p], cc[:, 1, :], ALU.mult).then_inc(s["concat_ready"], 1)

            def update(t, p):
                dve.wait_ge(s["out_mm"], t + 1)
                if biased:
                    dve.wait_ge(s["xb_ready"], 1)
                row = X[:, ds(t, 1), :].rearrange("p o d -> p (o d)")
                nc.vector.tensor_tensor(row, xo[p], row, ALU.add).then_inc(s["x_updated"], 1)

            values(0, 0)
            values(0, 1)
            if biased:
                add_bias()

            def maximum(n, q, h):
                dve.wait_ge(s["pair_scored"], 2 * n + h + 1)
                if h == 0:
                    wait(dve, s["exp_done"], 4 * (n - 1))
                nc.vector.tensor_reduce(nmax[q][:, 2 * h:2 * h + 2], sc[h][:, :, 0:KV], AX.X, ALU.max,
                                        negate=True).then_inc(s["max_ready"], 1)

            def turn(n, q, h):
                dve.wait_ge(s["exp_done"], 4 * n + 2 * h + 2)
                if h == 0:
                    wait(dve, s["pv_done"], n - 1)
                nc.vector.transpose(probsT[q][:, 2 * h:2 * h + 2, :],
                                    probs[q][:, 2 * h:2 * h + 2, 0:256]).then_inc(s["p_transposed"], 1)

            def second_half(n, q):
                turn(n, q, 1)
                wait(dve, s["spread_ready"], 2 * (n - 1))
                nc.vector.reciprocal(rsum[q][:, :], sums[q][:, :]).then_inc(s["rsum_ready"], 1)

            def tile(t, p, first, last):
                for b in range(BT):
                    n = 4 * t + b
                    if b == 0:
                        wait(dve, s["x_updated"], t - 1)
                    if not (b == 0 and first):
                        second_half(n - 1, 1 - b % 2)
                    maximum(n, b % 2, 0)
                    maximum(n, b % 2, 1)
                    turn(n, b % 2, 0)
                    if b == 1 and not first:
                        finish(t - 1, 1 - p)
                    if b == 2 and not first:
                        update(t - 1, 1 - p)
                    if b == 0 and not (isinstance(t, int) and t < 2):
                        norms.take(nc, X, t - 2)
                    if b == 1 and not last:
                        values(t + 1, 0)
                    if b == 3 and not last:
                        values(t + 1, 1)
            tiles(dve, tile)
            second_half(4 * T - 1, 1)
            finish(T - 1, 1)
            update(T - 1, 1)
            dve.wait_ge(s["x_updated"], T)
            for t in (T - 2, T - 1):
                norms.take(nc, X, t)

        @block.tensor
        def _(pe):
            W["wait"](pe)
            for c in range(4):
                nc.tensor.matmul([sc[0][:, 0, :], sc[0][:, 1, :], sc[1][:, 0, :], sc[1][:, 1, :]][c],
                                 wq[:, :], XNT[:, 512 * c:512 * (c + 1)], start=True, stop=True).then_inc(s["q_mm"], 1)
            pe.wait_ge(s["w_split"], 2)

            def project(t, p, h, what):
                pe.wait_ge(s["ctx_split"], 2 * t + 2)
                for c in (2 * h, 2 * h + 1):
                    if what == 0:
                        pe.wait_ge(s["v_copied"], 4 * t + c + 1)
                        if c == 3:
                            pe.wait_ge(s["v256_ready"], t + 1)
                    else:
                        wait(pe, s["k_ready"], 4 * t + c - 1)
                    nc.tensor.matmul(pj[c % 2][:, 0:KVP], whi[:, what, :], ctx_hl[p][:, c, :], start=True, stop=False)
                    last = nc.tensor.matmul(pj[c % 2][:, 0:KVP], wlo[:, what, :], ctx_hl[p][:, c, :], start=False, stop=True)
                    if what == 1 and c == BT - 1:
                        lk = ctx_hl[p][:, :, KV - 1]
                        nc.tensor.matmul(pj[1][:, 300:300 + BT], whi[:, 2, :], lk, start=True, stop=False)
                        last = nc.tensor.matmul(pj[1][:, 300:300 + BT], wlo[:, 2, :], lk, start=False, stop=True)
                    last.then_inc(s["v_mm"] if what else s["k_mm"], 1)

            def score(t, p, b):
                n = 4 * t + b
                pe.wait_ge(s["qbd_ready"], n + 1)
                pe.wait_ge(s["k_ready"], n + 1)
                for j in range(J):
                    wait(pe, s["exp_done"], 4 * (n - 1) + j + 1)
                    last = nc.tensor.matmul(sc[j // 2][:, j % 2, 0:KV],
                                            qbd[p][:, b, G * j:G * (j + 1), :], KT[p][:, b, 0:KV],
                                            start=True, stop=True)
                    if j % 2:
                        last.then_inc(s["pair_scored"], 1)

            def weigh(t, p, b):
                n = 4 * t + b
                q = b % 2
                pe.wait_ge(s["p_transposed"], 2 * n + 2)
                pe.wait_ge(s["v_act"], NA * (2 * t + b // 2 + 1))
                pe.wait_ge(s["v_pool"], 2 * t + b // 2 + 1)
                if b == 0:
                    wait(pe, s["concat_ready"], t - 1)
                    wait(pe, s["x_updated"], t - 1)
                cols = slice(S * b, S * (b + 1))
                for kb in range(KB):
                    for j in range(J):
                        last = nc.tensor.matmul(oacc_v[p][32 * j:32 * j + 32, cols], VB[p][:, KB * b + kb, j, :, :],
                                         probsT[q][:, j, 32 * kb:32 * kb + 32], start=(kb == 0),
                                         stop=(kb == KB - 1))
                last.then_inc(s["pv_done"], 1)

            def spread_rows(t, p, b):
                n = 4 * t + b
                q = b % 2
                cols = slice(S * b, S * (b + 1))
                pe.wait_ge(s["spread_ready"], 2 * n + 2)
                nc.tensor.matmul(oacc_last[p][:, cols], spread[q][:, 0], con["eye4"], start=True, stop=True)
                nc.tensor.matmul(oacc_rsum[p][:, cols], spread[q][:, 1], con["eye4"], start=True,
                                 stop=True).then_inc(s["rl_done"], 1)

            def output(t, p):
                pe.wait_ge(s["concat_ready"], t + 1)
                nc.tensor.matmul(xo[p], cc[:, 2, :], wo[:, :], start=True, stop=True).then_inc(s["out_mm"], 1)

            for h in range(2):
                project(0, 0, h, 1)
                project(0, 0, h, 0)
            pe.wait_ge(s["q_ready"], 4)

            def tile(t, p, first, last):
                for b in range(BT):
                    score(t, p, b)
                    if b >= 2:
                        spread_rows(t, p, b - 2)
                    elif not first:
                        spread_rows(t - 1, 1 - p, b + 2)
                    if b == 2 and not first:
                        output(t - 1, 1 - p)
                    if b > 0:
                        weigh(t, p, b - 1)
                    elif not first:
                        weigh(t - 1, 1 - p, 3)
                    if not last:
                        project(t + 1, 1 - p, b // 2, 1 - b % 2)
            tiles(pe, tile)
            spread_rows(T - 1, 1, 2)
            weigh(T - 1, 1, 3)
            spread_rows(T - 1, 1, 3)
            output(T - 1, 1)


E_H, E_D = 16, 64


def at_tile(ap3, t):
    if isinstance(t, int):
        return ap3[:, t, :]
    return ap3[:, bass.ds(t, 1), :].rearrange("p o n -> p (o n)")


def at_cols(ap2, t, n):
    return ap2[:, t * n:(t + 1) * n] if isinstance(t, int) else ap2[:, bass.ds(t * n, n)]


def self_attention(nc, cx, norms, name, X, XNT, con, W):
    sem = lambda n: cx.enter_context(nc.semaphore(f"{name}_{n}"))
    names = ("zeroed", "xb_ready", "proj_mm", "q_copied", "k_copied", "v_copied", "scored", "masked",
             "max_ready", "shifted", "exp_done", "sum_ready", "rsum_ready", "probs_ready", "p_transposed",
             "z_mm", "z_copied", "out_mm", "x_updated", "xts_ready")
    s = {n: sem(n) for n in names}
    HC = E_H // 2
    HE = E_H * E_D
    NPR = 6
    with ExitStack() as mem:
        sb = lambda n, sh, d=F32: mem.enter_context(nc.sbuf_tensor(f"{name}_{n}", sh, d))
        ps = lambda n, sh: mem.enter_context(nc.psum_tensor(f"{name}_{n}", sh, F32))
        wqkv, wo, bqk, bv, bo = (W[n] for n in ("wqkv", "wo", "bqk", "bv", "bo"))
        QT = [sb(f"q{n}", [P, HC, P]) for n in range(2)]
        KE = [sb(f"k{n}", [P, HC, 2, P]) for n in range(2)]
        V = [sb(f"v{n}", [P, HE]) for n in range(2)]
        sm = sb("sm", [P, E_H, S])
        pr = sb("pr", [P, E_H, S])
        PT = sb("pT", [P, E_H, P])
        nmax, sums, rsum = sb("nmax", [P, E_H]), sb("sums", [P, E_H]), sb("rsum", [P, E_H])
        zT = sb("zT", [P, HC, P])
        xts = sb("xts", [P, P])
        pj = [ps(f"pj{n}", [P, 512]) for n in range(2)]
        sc = ps("sc", [P, E_H, P])
        z = ps("z", [P, HC, P])
        block = mem.enter_context(nc.Block())
        heads = lambda a: a[:, :].unsqueeze(2).broadcast_to([P, E_H, S])
        quads = [slice(S * b, S * b + S) for b in range(BT)]

        def tiles(eng, tile):
            tile(0, 0, True, False)
            tile(1, 1, False, False)
            with eng.Fori(1, T // 2 - 1) as i:
                tile(2 * i, 0, False, False)
                tile(2 * i + 1, 1, False, False)
            tile(T - 2, 0, False, False)
            tile(T - 1, 1, False, True)

        @block.tensor
        def _(pe):
            W["wait"](pe)

            def project(t, m):
                if m < 2:
                    wait(pe, s["v_copied"], 2 * (t - 1) + m + 1)
                elif m < 4:
                    pe.wait_ge(s["q_copied"], HC * t + 4 * (m - 1))
                else:
                    pe.wait_ge(s["k_copied"], 4 * t + 2 * (m - 3))
                if m < 4:
                    xt = at_cols(XNT, t, P)
                    for c in range(4):
                        w = 4 * (m % 2) + c
                        last = nc.tensor.matmul(pj[m % 2][:, c * P:(c + 1) * P], wqkv[:, m // 2, w * P:(w + 1) * P],
                                                xt, start=True, stop=True)
                else:
                    if m == 4:
                        pe.wait_ge(s["xts_ready"], t + 1)
                    w = (m - 4) * 512
                    last = nc.tensor.matmul(pj[m % 2][:, :], xts[:, :], wqkv[:, 2, w:w + 512], start=True, stop=True)
                last.then_inc(s["proj_mm"], 1)

            def score(t, p):
                pe.wait_ge(s["q_copied"], HC * t + HC)
                pe.wait_ge(s["k_copied"], 4 * t + 4)
                wait(pe, s["masked"], BT * t)
                for c in range(HC):
                    last = nc.tensor.matmul(sc[:, 2 * c:2 * c + 2, :], QT[p][:, c, :], KE[p][:, c, :, :],
                                            start=True, stop=True)
                last.then_inc(s["scored"], 1)

            def weigh(t, p):
                pe.wait_ge(s["p_transposed"], BT * t + BT)
                pe.wait_ge(s["v_copied"], 2 * t + 2)
                wait(pe, s["x_updated"], t)
                for h in range(E_H):
                    r = slice(E_D * (h % 2), E_D * (h % 2) + E_D)
                    last = nc.tensor.matmul(z[r, h // 2, :], V[p][:, E_D * h:E_D * h + E_D], PT[:, h, :],
                                            start=True, stop=True)
                last.then_inc(s["z_mm"], 1)

            def output(t):
                pe.wait_ge(s["z_copied"], t + 1)
                for c in range(HC):
                    last = nc.tensor.matmul(z[:, 0, :], zT[:, c, :], wo[:, c, :], start=(c == 0), stop=(c == HC - 1))
                last.then_inc(s["out_mm"], 1)

            def tile(t, p, first, last):
                score(t, p)
                if not last:
                    for m in range(4):
                        project(t + 1, m)
                if not first:
                    weigh(t - 1, 1 - p)
                if not last:
                    project(t + 1, 4)
                    project(t + 1, 5)
                if not first:
                    output(t - 1)
            for m in range(NPR):
                project(0, m)
            tiles(pe, tile)
            weigh(T - 1, 1)
            output(T - 1)

        @block.vector
        def _(dve):
            W["wait"](dve)
            nc.vector.tensor_tensor(X[:, :, :], X[:, :, :], bo[:, :].unsqueeze(1).broadcast_to([P, T, D]),
                                    ALU.add).then_inc(s["xb_ready"], 1)

            def key_copies(t, p):
                if isinstance(t, int) and t < 2:
                    dve.wait_ge(s["zeroed"], 3)
                wait(dve, s["scored"], t - 1)
                for m in range(2):
                    dve.wait_ge(s["proj_mm"], NPR * t + m + 3)
                    for h in range(2):
                        r = slice(E_D * h, E_D * h + E_D)
                        nc.vector.tensor_tensor(
                            KE[p][r, 4 * m:4 * m + 4, h, :], pj[m][r, :].rearrange("p (c n) -> p c n", c=4),
                            bqk[r, 1, 4 * m:4 * m + 4].unsqueeze(2).broadcast_to([E_D, 4, P]),
                            ALU.add).then_inc(s["k_copied"], 1)

            def value_copies(t, p):
                wait(dve, s["z_mm"], t - 1)
                for m in range(2):
                    dve.wait_ge(s["proj_mm"], NPR * t + m + 5)
                    nc.vector.tensor_tensor(V[p][:, 512 * m:512 * (m + 1)], pj[m][:, :], bv[:, 512 * m:512 * (m + 1)],
                                            ALU.add).then_inc(s["v_copied"], 1)

            def update(t):
                dve.wait_ge(s["out_mm"], t + 1)
                dve.wait_ge(s["xb_ready"], 1)
                nc.vector.tensor_tensor(at_tile(X, t), z[:, 0, :], at_tile(X, t), ALU.add).then_inc(s["x_updated"], 1)

            key_copies(0, 0)
            value_copies(0, 0)

            def tile(t, p, first, last):
                dve.wait_ge(s["scored"], t + 1)
                wait(dve, s["exp_done"], t)
                wait(dve, s["x_updated"], t - 1)
                for b, r in enumerate(quads):
                    nc.vector.scalar_tensor_tensor(sm[r, :, :], sc[r, :, S * b:S * b + S], E_D ** -0.5,
                                                   con["causal"][r, :, :], ALU.mult, ALU.add).then_inc(s["masked"], 1)
                dve.wait_ge(s["masked"], BT * t + BT)
                nc.vector.tensor_reduce(nmax[:, :], sm[:, :, :], AX.X, ALU.max).then_inc(s["max_ready"], 1)
                if not last:
                    key_copies(t + 1, 1 - p)
                if not (isinstance(t, int) and t < 2):
                    norms.take(nc, X, t - 2)
                dve.wait_ge(s["exp_done"], t + 1)
                nc.vector.reduce_sum(sums[:, :], pr[:, :, :], AX.X).then_inc(s["sum_ready"], 1)
                dve.wait_ge(s["sum_ready"], t + 1)
                nc.vector.reciprocal(rsum[:, :], sums[:, :]).then_inc(s["rsum_ready"], 1)
                if not last:
                    value_copies(t + 1, 1 - p)
                if isinstance(t, int) and t == 0:
                    dve.wait_ge(s["zeroed"], 3)
                dve.wait_ge(s["probs_ready"], t + 1)
                wait(dve, s["z_mm"], t)
                for b, r in enumerate(quads):
                    nc.vector.transpose(PT[r, :, S * b:S * b + S], pr[r, :, :]).then_inc(s["p_transposed"], 1)
                if not first:
                    update(t - 1)
            tiles(dve, tile)
            update(T - 1)
            dve.wait_ge(s["x_updated"], T)
            for t in (T - 2, T - 1):
                norms.take(nc, X, t)

        @block.gpsimd
        def _(pool):
            for n, a in enumerate((KE[0], KE[1])):
                nc.gpsimd.memset(a[:, :, :, :], 0.0).then_inc(s["zeroed"], 1)
            nc.gpsimd.memset(PT[:, :, :], 0.0).then_inc(s["zeroed"], 1)
            pool.wait_ge(s["zeroed"], 3)

            def tile(t, p, first, last):
                pool.wait_ge(s["max_ready"], t + 1)
                wait(pool, s["probs_ready"], t)
                nc.gpsimd.tensor_tensor(sm[:, :, :], sm[:, :, :], heads(nmax), ALU.subtract).then_inc(s["shifted"], 1)
                pool.wait_ge(s["rsum_ready"], t + 1)
                pool.wait_ge(s["shifted"], t + 1)
                nc.gpsimd.tensor_tensor(pr[:, :, :], pr[:, :, :], heads(rsum), ALU.mult).then_inc(s["probs_ready"], 1)
            tiles(pool, tile)

        @block.scalar
        def _(act):
            W["wait"](act)

            def stage(t):
                wait(act, s["proj_mm"], NPR * t)
                nc.scalar.copy(xts[:, :], at_cols(XNT, t, P)).then_inc(s["xts_ready"], 1)

            def query_copies(t, p):
                wait(act, s["scored"], t - 1)
                for m in range(2):
                    act.wait_ge(s["proj_mm"], NPR * t + m + 1)
                    for c in range(4):
                        w = 4 * m + c
                        nc.scalar.activation(QT[p][:, w, :], pj[m][:, c * P:(c + 1) * P], ACT.Identity,
                                             bias=bqk[:, 0, w:w + 1]).then_inc(s["q_copied"], 1)
            stage(0)
            query_copies(0, 0)

            def heads_out(t):
                act.wait_ge(s["z_mm"], t + 1)
                wait(act, s["out_mm"], t)
                nc.scalar.copy(zT[:, :, :], z[:, :, :]).then_inc(s["z_copied"], 1)

            def tile(t, p, first, last):
                if not last:
                    stage(t + 1)
                    query_copies(t + 1, 1 - p)
                act.wait_ge(s["shifted"], t + 1)
                wait(act, s["p_transposed"], BT * t)
                nc.scalar.activation(pr[:, :, :], sm[:, :, :], ACT.Exp).then_inc(s["exp_done"], 1)
                if not first:
                    heads_out(t - 1)
            tiles(act, tile)
            heads_out(T - 1)


I_FF = 352
CH = (128, 128, 96)


class RouterCount:

    def __init__(self, nc, cx):
        (self.logits_mm, self.neg_ready, self.exp_done, self.mask_ready, self.counters_ready, self.ranks_mm,
         self.step, self.marks_ready, self.codes_mm, self.rows_sent) = (cx.enter_context(nc.semaphore("router_" + n)) for n in (
            "logits_mm", "neg_ready", "exp_done", "mask_ready", "counters_ready", "ranks_mm", "step",
            "marks_ready", "codes_mm", "rows_sent"))
        self.calls = self.steps = self.marks = 0
        self.returned = [cx.enter_context(nc.semaphore(f"returned{n}")) for n in range(T // 4)]
        self.returns = 0


def router(nc, count_of, name, XNT, XR, R, con, W, n_exp, top2, shared):
    call = count_of.calls
    count_of.calls = call + 1
    call_marks = count_of.marks
    count_of.marks += T * (2 if top2 else 1)
    choices = 2 if top2 else 1
    n_tiles = slot_tiles(n_exp, choices)
    with ExitStack() as mem:
        sb = lambda n, sh, d=F32: mem.enter_context(nc.sbuf_tensor(f"{name}_{n}", sh, d))
        rw, rb = W["rw"], W["rb"]
        pr, eq, pr2, slots = (sb(n, [P, T, n_exp]) for n in ("pr", "eq", "pr2", "slots"))
        hot = [sb(f"hot{c}", [P, T, n_exp]) for c in range(2 if top2 else 1)]
        mask = sb("mask", [P, T, n_exp], BF16)
        ones, before, places = (sb(n, [P, P], BF16) for n in ("ones", "before", "places"))
        best, first, total, second = (sb(n, [P, T]) for n in ("best", "first", "total", "second"))
        slot, quotient, remainder = (sb(n, [P, choices, T]) for n in ("slot", "quotient", "remainder"))
        slot_i, quotient_i, remainder_i = (sb(n, [P, choices, T], I32) for n in ("slot_i", "quotient_i", "remainder_i"))
        place = sb("place", [P, choices, T, P], BF16)
        tile_of = sb("tile_of", [P, choices, T, n_tiles], BF16)
        carried = sb("carried", [P, choices, T, 2, n_tiles], BF16)
        code, empty, spare, source, target = (sb(n, [P, n_tiles]) for n in ("code", "empty", "spare", "source", "target"))
        count, tiles, base = (sb(n, [P, n_exp]) for n in ("count", "tiles", "base"))
        over = sb("over", [P, n_exp, T])
        pairs = sb("pairs", [P, n_exp, n_exp])
        begun = sb("begun", [P, n_tiles, n_exp])
        owner = sb("owner", [P, n_tiles])
        banks = [mem.enter_context(nc.psum_tensor(f"{name}_{n}", [P, 512], F32)) for n in ("lg", "rank", "tot", "codes")]
        lgv, rank, tot = (k[:, 0:T * n_exp].rearrange("p (t e) -> p t e", e=n_exp) for k in banks[:3])
        codes = banks[3][:, 0:2 * n_tiles].rearrange("p (k n) -> p k n", k=2)
        block = mem.enter_context(nc.Block())
        wide = lambda a: a[:, :].unsqueeze(2).broadcast_to([P, T, n_exp])
        experts = lambda a: a.unsqueeze(1).broadcast_to([P, T, n_exp])

        @block.sync
        def _(sp):
            sp.dma_start(R.inbox.rearrange("(t p) d -> p t d", p=P), XR[:, :, :]).then_inc(count_of.rows_sent, 16)

        @block.tensor
        def _(pe):
            W["wait"](pe)
            for t in range(T):
                last = nc.tensor.matmul(lgv[:, t, :], XNT[:, t * P:(t + 1) * P], rw[:, :], start=True, stop=True)
            last.then_inc(count_of.logits_mm, 1)
            pe.wait_ge(count_of.counters_ready, 3 * call + 3)
            pe.wait_ge(count_of.mask_ready, call + 1)
            nc.tensor.matmul(tot, ones[:, :], mask[:, :, :], start=True, stop=True)
            nc.tensor.matmul(rank, before[:, :], mask[:, :, :], start=True, stop=False)
            for t in range(T - 1):
                last = nc.tensor.matmul(rank[:, t + 1:, :], ones[:, :],
                                        mask[:, t:t + 1, :].broadcast_to([P, T - 1 - t, n_exp]),
                                        start=False, stop=(t == T - 2))
            last.then_inc(count_of.ranks_mm, 1)
            for n in range(choices * T):
                c, t = n // T, n % T
                pe.wait_ge(count_of.marks_ready, call_marks + n + 1)
                last = nc.tensor.matmul(codes, place[:, c, t, :], carried[:, c, t, :, :],
                                        start=(n == 0), stop=(n == choices * T - 1))
            last.then_inc(count_of.codes_mm, 1)

        @block.scalar
        def _(act):
            nc.scalar.copy(ones[:, :], con["ones"]).then_inc(count_of.counters_ready, 1)
            nc.scalar.copy(before[:, :], con["before"]).then_inc(count_of.counters_ready, 1)
            nc.scalar.copy(places[:, :], con["places"]).then_inc(count_of.counters_ready, 1)
            act.wait_ge(count_of.neg_ready, call + 1)
            nc.scalar.activation(pr[:, :, :], pr[:, :, :], ACT.Exp, scale=-1.0).then_inc(count_of.exp_done, 1)

        @block.vector
        def _(dve):
            chain = Chain(dve, count_of.step, count_of.steps)
            v = nc.vector
            W["wait"](dve)
            dve.wait_ge(count_of.logits_mm, call + 1)
            if shared:
                chain.then(v.tensor_tensor(pr[:, :, :], lgv, experts(rb[:, :]), ALU.add))
                v.tensor_scalar(pr[:, :, :], pr[:, :, :], 50.0, -50.0, ALU.min, ALU.max).then_inc(count_of.neg_ready, 1)
            else:
                v.tensor_tensor(pr[:, :, :], lgv, experts(rb[:, :]), ALU.add).then_inc(count_of.neg_ready, 1)
            dve.wait_ge(count_of.exp_done, call + 1)
            chain.then(v.tensor_scalar_add(pr[:, :, :], pr[:, :, :], 1.0))
            chain.then(v.reciprocal(pr[:, :, :], pr[:, :, :]))

            def pick(src, best, hot):
                chain.then(v.tensor_reduce(best[:, :], src[:, :, :], AX.X, ALU.max))
                chain.then(v.tensor_tensor(eq[:, :, :], src[:, :, :], wide(best), ALU.is_equal))
                chain.then(v.tensor_tensor(eq[:, :, :], eq[:, :, :], experts(con["rank"][:, 0:n_exp]), ALU.mult))
                chain.then(v.tensor_reduce(first[:, :], eq[:, :, :], AX.X, ALU.max))
                chain.then(v.tensor_tensor(hot[:, :, :], eq[:, :, :], wide(first), ALU.is_equal))

            pick(pr, best, hot[0])
            if top2:
                chain.then(v.scalar_tensor_tensor(pr2[:, :, :], hot[0][:, :, :], -2.0, pr[:, :, :], ALU.mult, ALU.add))
                pick(pr2, second, hot[1])
                v.tensor_tensor(mask[:, :, :], hot[0][:, :, :], hot[1][:, :, :], ALU.add).then_inc(count_of.mask_ready, 1)
            else:
                v.tensor_copy(mask[:, :, :], hot[0][:, :, :]).then_inc(count_of.mask_ready, 1)
            if not top2:
                chain.then(v.tensor_scalar(best[:, :], best[:, :], 1e-8, 1.0 - 1e-8, ALU.max, ALU.min))
                chain.then(v.tensor_scalar(total[:, :], best[:, :], 0.5, 1e-8, ALU.add, ALU.add))
                chain.then(v.tensor_scalar(total[:, :], total[:, :], 0.5, 2.0, ALU.max, ALU.min))
                chain.then(v.reciprocal(total[:, :], total[:, :]))
                chain.then(v.tensor_scalar(R.shared[:, :], total[:, :], 0.5, None, ALU.mult))
                chain.then(v.tensor_tensor(R.gate[:, 0, :], best[:, :], total[:, :], ALU.mult))
            else:
                chain.then(v.tensor_tensor(total[:, :], best[:, :], second[:, :], ALU.add))
                chain.then(v.tensor_scalar_add(total[:, :], total[:, :], 1e-20))
                chain.then(v.reciprocal(total[:, :], total[:, :]))
                chain.then(v.tensor_tensor(R.gate[:, 0, :], best[:, :], total[:, :], ALU.mult))
                chain.then(v.tensor_tensor(R.gate[:, 1, :], second[:, :], total[:, :], ALU.mult))

            dve.wait_ge(count_of.ranks_mm, call + 1)
            chain.then(v.tensor_reduce(count[:, :], tot.rearrange("p t e -> p e t"), AX.X, ALU.add))
            chain.then(v.tensor_scalar(count[:, :], count[:, :], 1.0 / P, None, ALU.mult))
            chain.then(v.tensor_tensor(over[:, :, :], count[:, :].unsqueeze(2).broadcast_to([P, n_exp, T]),
                                       con["steps"][:, 0:T].unsqueeze(1).broadcast_to([P, n_exp, T]), ALU.is_gt))
            chain.then(v.tensor_reduce(tiles[:, :], over[:, :, :], AX.X, ALU.add))
            chain.then(v.tensor_tensor(pairs[:, :, :], tiles[:, :].unsqueeze(1).broadcast_to([P, n_exp, n_exp]),
                                       con["lower"][:, 0:n_exp, 0:n_exp], ALU.mult))
            chain.then(v.tensor_reduce(base[:, :], pairs[:, :, :], AX.X, ALU.add))
            chain.then(v.scalar_tensor_tensor(slots[:, :, :], experts(base[:, :]), float(P), rank, ALU.mult, ALU.add))
            for c, h in enumerate(hot):
                chain.then(v.tensor_tensor(eq[:, :, :], h[:, :, :], slots[:, :, :], ALU.mult))
                chain.then(v.tensor_reduce(slot[:, c, :], eq[:, :, :], AX.X, ALU.add))
            chain.then(v.tensor_copy(slot_i[:, :, :], slot[:, :, :]))
            v.tensor_scalar(quotient_i[:, :, :], slot_i[:, :, :], 7, None, ALU.arith_shift_right)
            chain.then(v.tensor_scalar(remainder_i[:, :, :], slot_i[:, :, :], P - 1, None, ALU.bitwise_and))
            v.tensor_copy(quotient[:, :, :], quotient_i[:, :, :])
            chain.then(v.tensor_copy(remainder[:, :, :], remainder_i[:, :, :]))
            dve.wait_ge(count_of.counters_ready, 3 * call + 3)
            for c in range(choices):
                chain.then(v.tensor_tensor(tile_of[:, c, :, :],
                                           con["steps"][:, 0:n_tiles].unsqueeze(1).broadcast_to([P, T, n_tiles]),
                                           quotient[:, c, :].unsqueeze(2).broadcast_to([P, T, n_tiles]), ALU.is_equal))
                v.tensor_scalar(carried[:, c, :, 0, :], tile_of[:, c, :, :], con["place"], None, ALU.mult)
                chain.then(v.tensor_tensor(carried[:, c, :, 1, :], tile_of[:, c, :, :],
                                           con["steps"][:, c * T:(c + 1) * T].unsqueeze(2).broadcast_to([P, T, n_tiles]),
                                           ALU.mult))
                for t in range(T):
                    v.tensor_scalar(place[:, c, t, :], places[:, :], remainder[:, c, t:t + 1], None,
                                    ALU.is_equal).then_inc(count_of.marks_ready, 1)
            chain.then(v.tensor_tensor(begun[:, :, :], con["steps"][:, 0:n_tiles].unsqueeze(2)
                                       .broadcast_to([P, n_tiles, n_exp]),
                                       base[:, :].unsqueeze(1).broadcast_to([P, n_tiles, n_exp]), ALU.is_ge))
            chain.then(v.tensor_reduce(owner[:, :], begun[:, :, 1:], AX.X, ALU.add))
            chain.then(v.tensor_copy(R.expert[:, 0:n_tiles], owner[:, :]))
            dve.wait_ge(count_of.codes_mm, call + 1)
            chain.then(v.tensor_copy(code[:, :], codes[:, 0, :]))
            chain.then(v.scalar_tensor_tensor(code[:, :], codes[:, 1, :], float(P), code[:, :], ALU.mult, ALU.add))
            v.tensor_scalar(empty[:, :], code[:, :], 0.5, None, ALU.is_lt)
            chain.then(v.tensor_scalar(spare[:, :], con["slots"][:, 0:n_tiles], choices * T * P + 1.0, None, ALU.add))
            chain.then(v.tensor_tensor(spare[:, :], spare[:, :], empty[:, :], ALU.mult))
            v.scalar_tensor_tensor(target[:, :], code[:, :], -1.0, spare[:, :], ALU.add, ALU.add)
            chain.then(v.tensor_scalar(source[:, :], code[:, :], T * P + 0.5, -float(T * P), ALU.is_gt, ALU.mult))
            chain.then(v.tensor_tensor(source[:, :], source[:, :], code[:, :], ALU.add))
            chain.then(v.tensor_scalar(source[:, :], source[:, :], -1.0, 0.0, ALU.add, ALU.max))
            v.tensor_copy(R.target[:, 0:n_tiles], target[:, :])
            chain.then(v.tensor_copy(R.source[:, 0:n_tiles], source[:, :]))
            count_of.steps += chain.n


def slot_tiles(n_exp, choices):
    return (T * P * choices + n_exp * (P - 1)) // P


def sparse_experts(nc, cx, counts, norms, name, X, XNT, XR, R, con, W, n_exp, choices, shared, store=None):
    ds = bass.ds
    sem = lambda k: cx.enter_context(nc.semaphore(f"{name}_{k}"))
    NT = slot_tiles(n_exp, choices)
    NC = len(CH)
    SU = NC * (T // 4) if shared else 0
    SB = T // 4 if shared else 0
    names = ("up_mm", "silu_done", "h_ready", "down_mm", "y_done", "x_turned", "x_copied", "scattered",
             "x_updated", "x_done", "w_staged", "x_staged")
    s = {k: sem(k) for k in names}
    AHEAD = 8
    loaded = [sem(f"loaded{n}") for n in range(2)]
    returned, returns = counts.returned, counts.returns
    counts.returns += 16 * choices
    with ExitStack() as mem:
        sb = lambda k, sh, d=F32: mem.enter_context(nc.sbuf_tensor(f"{name}_{k}", sh, d))
        ps = lambda k, sh: mem.enter_context(nc.psum_tensor(f"{name}_{k}", sh, F32))
        w13, w2 = W["w13"], W["w2"]
        xs = [sb(f"xs{k}", [P, D]) for k in range(2)]
        rows = sb("rows", [P, NT, D])
        xT = [sb(f"xT{k}", [P, P]) for k in range(2)]
        wt = [sb(f"wt{k}", [P, 1, 2, NC * P]) for k in range(2)]
        g = [sb(f"g{k}", [P, 512]) for k in range(2)]
        h = [sb(f"h{k}", [P, NC, 512]) for k in range(2)]
        back = [XR] + [sb(f"back{c}", [P, T, D]) for c in range(1, choices)]
        u1 = [ps(f"u1{k}", [P, 512]) for k in range(2)]
        u3 = [ps(f"u3{k}", [P, 512]) for k in range(2)]
        xt_ps = [ps(f"xt{k}", [P, 512]) for k in range(2)]
        y = [ps(f"y{k}", [P, 4, P]) for k in range(2)]
        block = mem.enter_context(nc.Block())
        inbox, outbox = R.inbox, W["outbox"]

        def tiles(eng, tile):
            tile(0, 0, True, False)
            tile(1, 1, False, False)
            with eng.Fori(1, NT // 2 - 1) as i:
                tile(2 * i, 0, False, False)
                tile(2 * i + 1, 1, False, False)
            tile(NT - 2, 0, False, False)
            tile(NT - 1, 1, False, True)

        @block.gpsimd
        def _(pool):
            W["wait_rows"](pool)
            for t in range(NT + AHEAD):
                if t < NT:
                    wait(pool, loaded[t % 2], 16 * (t // 2))
                    pool.indirect_dma_start(rows[:, t, :], None, inbox,
                                            bass.IndirectOffsetOnAxis(R.source[:, t:t + 1], 0)
                                            ).then_inc(loaded[t % 2], 16)
                if t >= AHEAD:
                    pool.wait_ge(s["y_done"], SB + t - AHEAD + 1)
                    pool.indirect_dma_start(outbox, bass.IndirectOffsetOnAxis(R.target[:, t - AHEAD:t - AHEAD + 1], 0),
                                            rows[:, t - AHEAD, :], None).then_inc(s["scattered"], 16)

        @block.sync
        def _(sp):
            sp.wait_ge(s["scattered"], 16 * NT)
            for n in range(T // 4):
                for c in range(choices):
                    at = (c * T + 4 * n) * P
                    sp.dma_start(back[c][:, 4 * n:4 * n + 4, :],
                                 outbox[at:at + 4 * P, :].rearrange("(t p) d -> p t d", p=P)).then_inc(returned[n], 16)
            if store:
                for n in range(T // 4):
                    sp.wait_ge(s["x_done"], n + 1)
                    store(sp, slice(4 * n, 4 * n + 4))

        @block.tensor
        def _(pe):
            W["wait"](pe)

            def shared_up(k, c):
                m = NC * k + c
                wait(pe, s["h_ready"], m - 1)
                for j, u in ((0, u1), (1, u3)):
                    last = nc.tensor.matmul(u[m % 2][:, :], w13[:, n_exp, j, c * P:(c + 1) * P],
                                            XNT[:, k * 512:(k + 1) * 512], start=True, stop=True)
                last.then_inc(s["up_mm"], 1)

            def shared_down(k):
                wait(pe, s["y_done"], k - 1)
                pe.wait_ge(s["h_ready"], NC * (k + 1))
                for t in range(4):
                    for c in range(NC):
                        last = nc.tensor.matmul(y[k % 2][:, t, :], h[k % 2][:, c, t * P:(t + 1) * P],
                                                w2[:, n_exp, c, :], start=(c == 0), stop=(c == NC - 1))
                last.then_inc(s["down_mm"], 1)

            for k in range(SB):
                for c in range(NC):
                    shared_up(k, c)
                    if k and c == 1:
                        shared_down(k - 1)
            if shared:
                shared_down(SB - 1)

            def turn(t, p):
                pe.wait_ge(s["x_staged"], t + 1)
                wait(pe, s["x_copied"], t - 1)
                nc.tensor.transpose(xt_ps[p][:, 0:P], xs[p][:, :], con["ident"]).then_inc(s["x_turned"], 1)

            def up(t, p):
                pe.wait_ge(s["w_staged"], t + 1)
                pe.wait_ge(s["x_copied"], t + 1)
                wait(pe, s["h_ready"], SU + t - 1)
                for j, u in ((0, u1), (1, u3)):
                    for c in range(NC):
                        last = nc.tensor.matmul(u[p][:, c * P:(c + 1) * P], wt[p][:, 0, j, c * P:(c + 1) * P],
                                                xT[p][:, :], start=True, stop=True)
                last.then_inc(s["up_mm"], 1)

            def down(t, p):
                e = pe.value_load(R.expert[0:1, ds(t, 1)], min_val=0, max_val=n_exp - 1)
                wait(pe, s["y_done"], SB + t - 1)
                pe.wait_ge(s["h_ready"], SU + t + 1)
                for c in range(NC):
                    last = nc.tensor.matmul(y[p][:, 0, :], h[p][:, c, 0:P],
                                            w2[:, ds(e, 1), c, :].rearrange("p o n -> p (o n)"),
                                            start=(c == 0), stop=(c == NC - 1))
                last.then_inc(s["down_mm"], 1)

            def tile(t, p, first, last):
                if not last:
                    turn(t + 1, 1 - p)
                up(t, p)
                if not first:
                    down(t - 1, 1 - p)
            turn(0, 0)
            tiles(pe, tile)
            down(NT - 1, 1)

        @block.scalar
        def _(act):
            def silu(m, p, n):
                act.wait_ge(s["up_mm"], m + 1)
                wait(act, s["h_ready"], m - 1)
                nc.scalar.activation(g[p][:, 0:n], u1[p][:, 0:n], ACT.Silu).then_inc(s["silu_done"], 1)

            for m in range(SU):
                silu(m, m % 2, 512)

            def copy(t, p):
                act.wait_ge(s["x_turned"], t + 1)
                wait(act, s["up_mm"], SU + t - 1)
                nc.scalar.copy(xT[p][:, :], xt_ps[p][:, 0:P]).then_inc(s["x_copied"], 1)

            def place(t, p, pair):
                act.wait_ge(loaded[p], 16 * pair + 16)
                wait(act, s["x_turned"], t - 1)
                nc.scalar.copy(xs[p][:, :], at_tile(rows, t)).then_inc(s["x_staged"], 1)

            def tile(t, p, pair, last_pair, last):
                if not last_pair:
                    place(t + 2, p, pair + 1)
                if not last:
                    copy(t + 1, 1 - p)
                silu(SU + t, p, NC * P)

            place(0, 0, 0)
            place(1, 1, 0)
            copy(0, 0)
            tile(0, 0, 0, False, False)
            tile(1, 1, 0, False, False)
            with act.Fori(1, NT // 2 - 1) as i:
                tile(2 * i, 0, i, False, False)
                tile(2 * i + 1, 1, i, False, False)
            tile(NT - 2, 0, NT // 2 - 1, True, False)
            tile(NT - 1, 1, NT // 2 - 1, True, True)

        @block.vector
        def _(dve):
            def hidden(m, p, dst, n, shape):
                dve.wait_ge(s["silu_done"], m + 1)
                view = (lambda a: a) if shape is None else (lambda a: a.rearrange("p (c n) -> p c n", c=shape))
                nc.vector.tensor_tensor(dst, view(g[p][:, 0:n]), view(u3[p][:, 0:n]), ALU.mult).then_inc(s["h_ready"], 1)

            def shared_update(k):
                dve.wait_ge(s["down_mm"], k + 1)
                for t in range(4):
                    tt = 4 * k + t
                    last = nc.vector.scalar_tensor_tensor(X[:, tt, :], y[k % 2][:, t, :], R.shared[:, tt:tt + 1],
                                                          X[:, tt, :], ALU.mult, ALU.add)
                last.then_inc(s["y_done"], 1)

            for k in range(SB):
                for c in range(NC):
                    if c == 0 and k > 1:
                        dve.wait_ge(s["down_mm"], k - 1)
                    m = NC * k + c
                    hidden(m, m % 2, h[k % 2][:, c, :], 512, None)
                    if k and c == 1:
                        shared_update(k - 1)
            if shared:
                shared_update(SB - 1)

            def stage(t, p):
                e = dve.value_load(R.expert[0:1, ds(t, 1)], min_val=0, max_val=n_exp - 1)
                wait(dve, s["up_mm"], SU + t - 1)
                nc.vector.tensor_scalar(wt[p][:, :, :, :], w13[:, ds(e, 1), :, :], 1.0, None,
                                        ALU.mult).then_inc(s["w_staged"], 1)

            def take(t, p):
                dve.wait_ge(s["down_mm"], SB + t + 1)
                nc.vector.tensor_copy(at_tile(rows, t), y[p][:, 0, :]).then_inc(s["y_done"], 1)

            def tile(t, p, first, last):
                if not last:
                    stage(t + 1, 1 - p)
                wait(dve, s["down_mm"], SB + t - 1)
                hidden(SU + t, p, h[p][:, :, 0:P], NC * P, NC)
                if not first:
                    take(t - 1, 1 - p)
            stage(0, 0)
            tiles(dve, tile)
            take(NT - 1, 1)
            dve.wait_ge(s["y_done"], SB + NT)
            for n in range(T // 4):
                dve.wait_ge(returned[n], returns + 16 * choices)
                for c in range(choices):
                    if c:
                        dve.wait_ge(s["x_updated"], n + 1)
                    for t in range(4 * n, 4 * n + 4):
                        last = nc.vector.scalar_tensor_tensor(X[:, t, :], back[c][:, t, :], R.gate[:, c, t:t + 1],
                                                              X[:, t, :], ALU.mult, ALU.add)
                    if c < choices - 1:
                        last.then_inc(s["x_updated"], 1)
                last.then_inc(s["x_done"], 1)
                if not store:
                    dve.wait_ge(s["x_done"], n + 1)
                    for t in range(4 * n, 4 * n + 4):
                        norms.take(nc, X, t)


def rope_attention(nc, cx, norms, name, X, XNT, con, W):
    sem = lambda n: cx.enter_context(nc.semaphore(f"{name}_{n}"))
    names = ("xb_ready", "xs_ready", "qkv_mm", "qk_ready", "v_ready", "cos_done", "swap_done", "roped",
             "qkT_mm", "qkT_copied", "scored", "max_ready", "bias_ready", "exp_done", "rsum_ready", "probs_ready",
             "pT_ready", "spread", "o_mm", "o_copied", "out_mm", "x_updated")
    s = {n: sem(n) for n in names}
    TB = 4
    NBLK = T // TB
    HALF = D // 2
    with ExitStack() as mem:
        sb = lambda n, sh, d=F32: mem.enter_context(nc.sbuf_tensor(f"{name}_{n}", sh, d))
        ps = lambda n, sh: mem.enter_context(nc.psum_tensor(f"{name}_{n}", sh, F32))
        wqkv, wo, bqkv, bo = (W[n] for n in ("wqkv", "wo", "bqkv", "bo"))
        xs = sb("xs", [P, TB * P])
        qk = sb("qk", [P, TB * 2, 2, HALF])
        v = sb("v", [P, TB, D])
        qc, qs, qr = sb("qc", [P, TB * 2, 2, HALF]), sb("qs", [P, TB * 2, 2, HALF]), sb("qr", [P, TB * 2, 2, HALF])
        qkT = sb("qkT", [P, TB * 2, P])
        nmax, sums, rsum = sb("nmax", [P, TB]), sb("sums", [P, TB]), sb("rsum", [P, TB])
        pr, prn, prT = sb("pr", [P, TB, S]), sb("prn", [P, TB, S]), sb("prT", [P, TB, S])
        pbd = sb("pbd", [P, TB, BT, S])
        oT = sb("oT", [P, TB, P])
        qkv_ps = ps("qkv_ps", [P, TB, 512])
        tr_ps = ps("tr_ps", [P, 2, 4, P])
        sc_ps = ps("sc_ps", [P, 512])
        o_ps = ps("o_ps", [P, TB, P])
        block = mem.enter_context(nc.Block())


        @block.tensor
        def _(pe):
            W["wait"](pe)

            def project(i):
                pe.wait_ge(s["xs_ready"], i + 1)
                wait(pe, s["v_ready"], i)
                for t in range(TB):
                    last = nc.tensor.matmul(qkv_ps[:, t, 0:3 * D], xs[:, t * P:(t + 1) * P], wqkv[:, :],
                                            start=True, stop=True)
                last.then_inc(s["qkv_mm"], 1)

            def turn(i):
                pe.wait_ge(s["roped"], i + 1)
                wait(pe, s["qkT_copied"], i)
                for m in range(2 * TB):
                    last = nc.tensor.transpose(tr_ps[:, m // 4, m % 4, :],
                                               qr[:, m, :, :].rearrange("p h d -> p (h d)"), con["ident"])
                last.then_inc(s["qkT_mm"], 1)

            def score(i):
                pe.wait_ge(s["qkT_copied"], i + 1)
                wait(pe, s["exp_done"], TB * i)
                for t in range(TB):
                    for b in range(BT):
                        r = slice(S * b, S * b + S)
                        last = nc.tensor.matmul(sc_ps[r, S * t:S * t + S], qkT[:, 2 * t, r], qkT[:, 2 * t + 1, r],
                                                start=True, stop=True)
                last.then_inc(s["scored"], 1)

            def weigh(i):
                pe.wait_ge(s["spread"], i + 1)
                pe.wait_ge(s["v_ready"], i + 1)
                wait(pe, s["x_updated"], i)
                for t in range(TB):
                    last = nc.tensor.matmul(o_ps[:, t, :], v[:, t, :], pbd[:, t, :, :], start=True, stop=True)
                last.then_inc(s["o_mm"], 1)

            def output(i):
                pe.wait_ge(s["o_copied"], i + 1)
                for t in range(TB):
                    last = nc.tensor.matmul(o_ps[:, t, :], oT[:, t, :], wo[:, :], start=True, stop=True)
                last.then_inc(s["out_mm"], 1)

            project(0)
            turn(0)
            project(1)
            for i in range(NBLK):
                score(i)
                weigh(i)
                if i + 1 < NBLK:
                    turn(i + 1)
                output(i)
                if i + 2 < NBLK:
                    project(i + 2)

        @block.scalar
        def _(act):
            def place(i):
                wait(act, s["qkv_mm"], i)
                nc.scalar.copy(xs[:, :], at_cols(XNT, i, TB * P)).then_inc(s["xs_ready"], 1)

            def turned(i):
                act.wait_ge(s["qkT_mm"], i + 1)
                wait(act, s["scored"], i)
                nc.scalar.copy(qkT[:, :, :].rearrange("p m n -> p (m n)"),
                               tr_ps[:, :, :, :].rearrange("p a m n -> p (a m n)")).then_inc(s["qkT_copied"], 1)

            def exponentials(i):
                act.wait_ge(s["bias_ready"], i + 1)
                wait(act, s["probs_ready"], i)
                for t in range(TB):
                    nc.scalar.activation(pr[:, t, :], sc_ps[:, S * t:S * t + S], ACT.Exp, bias=nmax[:, t:t + 1],
                                         scale=D ** -0.5, accum_out=sums[:, t:t + 1]).then_inc(s["exp_done"], 1)

            def heads(i):
                act.wait_ge(s["o_mm"], i + 1)
                wait(act, s["out_mm"], i)
                nc.scalar.copy(oT[:, :, :], o_ps[:, :, :]).then_inc(s["o_copied"], 1)

            place(0)
            place(1)
            turned(0)
            for i in range(NBLK):
                exponentials(i)
                if i + 2 < NBLK:
                    place(i + 2)
                heads(i)
                if i + 1 < NBLK:
                    turned(i + 1)

        @block.gpsimd
        def _(pool):
            def by_cosine(i):
                pool.wait_ge(s["qk_ready"], i + 1)
                wait(pool, s["roped"], i)
                wait(pool, s["spread"], i - 1)
                nc.gpsimd.tensor_tensor(qc[:, :, :, :].rearrange("p m h d -> p m (h d)"),
                                        qk[:, :, :, :].rearrange("p m h d -> p m (h d)"),
                                        con["cos"].unsqueeze(1).broadcast_to([P, 2 * TB, D]), ALU.mult
                                        ).then_inc(s["cos_done"], 1)

            def spread(i):
                pool.wait_ge(s["pT_ready"], i + 1)
                wait(pool, s["o_mm"], i)
                pool.wait_ge(s["cos_done"], min(i + 2, NBLK))
                nc.gpsimd.tensor_tensor(pbd[:, :, :, :], prT[:, :, :].unsqueeze(2).broadcast_to([P, TB, BT, S]),
                                        con["seqmask"].unsqueeze(1).unsqueeze(3).broadcast_to([P, TB, BT, S]),
                                        ALU.mult).then_inc(s["spread"], 1)
            by_cosine(0)
            for i in range(NBLK):
                if i + 1 < NBLK:
                    by_cosine(i + 1)
                spread(i)

        @block.vector
        def _(dve):
            W["wait"](dve)

            def biases(i):
                dve.wait_ge(s["qkv_mm"], i + 1)
                wait(dve, s["cos_done"], i)
                nc.vector.tensor_tensor(
                    qk[:, :, :, :].rearrange("p (t m) h d -> p t (m h d)", t=TB), qkv_ps[:, :, 0:2 * D],
                    bqkv[:, 0:2 * D].unsqueeze(1).broadcast_to([P, TB, 2 * D]), ALU.add).then_inc(s["qk_ready"], 1)
                dve.wait_ge(s["qk_ready"], i + 1)
                for h in range(2):
                    nc.vector.tensor_tensor(qs[:, :, h, :], qk[:, :, 1 - h, :],
                                            con["sin"][:, h * HALF:(h + 1) * HALF].unsqueeze(1)
                                            .broadcast_to([P, 2 * TB, HALF]), ALU.mult).then_inc(s["swap_done"], 1)

            def rope(i):
                dve.wait_ge(s["cos_done"], i + 1)
                dve.wait_ge(s["swap_done"], 2 * i + 2)
                wait(dve, s["qkT_mm"], i)
                nc.vector.tensor_tensor(qr[:, :, :, :], qc[:, :, :, :], qs[:, :, :, :], ALU.add).then_inc(s["roped"], 1)

            def values(i):
                wait(dve, s["o_mm"], i)
                nc.vector.tensor_tensor(v[:, :, :], qkv_ps[:, :, 2 * D:3 * D],
                                        bqkv[:, 2 * D:3 * D].unsqueeze(1).broadcast_to([P, TB, D]),
                                        ALU.add).then_inc(s["v_ready"], 1)

            def maximum(i):
                dve.wait_ge(s["scored"], i + 1)
                wait(dve, s["exp_done"], TB * i)
                nc.vector.tensor_reduce(nmax[:, :], sc_ps[:, 0:TB * S].rearrange("p (t k) -> p t k", k=S), AX.X,
                                        ALU.max, negate=True).then_inc(s["max_ready"], 1)
                dve.wait_ge(s["max_ready"], i + 1)
                nc.vector.tensor_scalar(nmax[:, :], nmax[:, :], D ** -0.5, None, ALU.mult).then_inc(s["bias_ready"], 1)

            def probabilities(i):
                dve.wait_ge(s["exp_done"], TB * i + TB)
                nc.vector.reciprocal(rsum[:, :], sums[:, :]).then_inc(s["rsum_ready"], 1)
                dve.wait_ge(s["rsum_ready"], i + 1)
                nc.vector.tensor_tensor(prn[:, :, :], pr[:, :, :], rsum[:, :].unsqueeze(2).broadcast_to([P, TB, S]),
                                        ALU.mult).then_inc(s["probs_ready"], 1)
                dve.wait_ge(s["probs_ready"], i + 1)
                wait(dve, s["spread"], i)
                nc.vector.transpose(prT[:, :, :].rearrange("p t k -> p (t k)"),
                                    prn[:, :, :].rearrange("p t k -> p (t k)")).then_inc(s["pT_ready"], 1)

            def update(i):
                dve.wait_ge(s["out_mm"], i + 1)
                if i == 0:
                    dve.wait_ge(s["xb_ready"], 1)
                xb = X[:, i * TB:(i + 1) * TB, :].rearrange("p t d -> p (t d)")
                nc.vector.tensor_tensor(xb, o_ps[:, :, :].rearrange("p t d -> p (t d)"), xb,
                                        ALU.add).then_inc(s["x_updated"], 1)

            biases(0)
            rope(0)
            values(0)
            nc.vector.tensor_tensor(X[:, :, :], X[:, :, :], bo[:, :].unsqueeze(1).broadcast_to([P, T, D]),
                                    ALU.add).then_inc(s["xb_ready"], 1)
            for i in range(NBLK):
                maximum(i)
                if i + 1 < NBLK:
                    biases(i + 1)
                probabilities(i)
                if i + 1 < NBLK:
                    rope(i + 1)
                    values(i + 1)
                update(i)
                dve.wait_ge(s["x_updated"], i + 1)
                for t in range(TB * i, TB * i + TB):
                    norms.take(nc, X, t)

CONSTS = (("ident", P), ("qmask", J * G), ("rowmask", P), ("eye4", S), ("causal", E_H * S), ("rank", 9), ("ones", P), ("before", P), ("lower", 81),
          ("steps", 40), ("places", P), ("place", 1), ("slots", 40), ("scalars", 2),
          ("cos", D), ("sin", D), ("seqmask", BT))


class Routes:
    pass


def perceiver(nc, a, out):
    with ExitStack() as cx:
        sb = lambda n, s: cx.enter_context(nc.sbuf_tensor(n, s, F32))
        sem = lambda n: cx.enter_context(nc.semaphore(n))
        X = sb("x", [P, T, D])
        XNT = sb("xnt", [P, T * P])
        R = Routes()
        R.gate, R.shared = sb("gate", [P, 2, T]), sb("shared_gate", [P, T])
        R.expert, R.source, R.target = (cx.enter_context(nc.sbuf_tensor(n, [P, slot_tiles(9, 2)], I32))
                                        for n in ("tile_expert", "source", "target"))
        R.inbox = nc.dram_tensor("inbox", (T * P, D), F32, kind="Internal").ap()
        cs = sb("consts", [P, sum(w for _, w in CONSTS)])
        con, at = {}, 0
        for n, w in CONSTS:
            con[n] = cs[:, at:at + w]
            at += w
        con["eps"], con["power"] = con["scalars"][:, 0:1], con["scalars"][:, 1:2]
        con["lower"] = con["lower"].rearrange("p (f e) -> p f e", f=9)
        con["causal"] = con["causal"].rearrange("p (h k) -> p h k", k=S)
        loaded, stored = sem("loaded"), sem("stored")
        x_loaded = [sem(f"x_loaded{n}") for n in range(T // 4)]

        stages = {"x0_": ("wq", "wo", "wkvv", "bias", "bo"), "a0_": ("lnwb", "wqkv", "wo", "bqk", "bv", "bo"),
                  "r0_": ("rw", "rb"), "x1_": ("wq", "wo", "wkvv"), "a1_": ("wqkv", "wo", "bqkv", "bo"),
                  "r1_": ("rw", "rb")}
        first_loaded, later_loaded = sem("first_loaded"), sem("later_loaded")
        n_later = sum(len(names) for pre, names in stages.items() if pre != "x0_")
        W = {}
        for pre, names in stages.items():
            W[pre] = {n: sb(pre + n, list(a[pre + n].shape)) for n in names}
            W[pre]["wait"] = ((lambda eng: eng.wait_ge(first_loaded, 16 * len(stages["x0_"]))) if pre == "x0_" else
                              (lambda eng: eng.wait_ge(later_loaded, 16 * n_later)))

        wide = len(CH) * P
        w13, w2 = sb("w13", [P, 9, 2, wide]), sb("w2", [P, 9, len(CH), D])
        experts_loaded = sem("experts_loaded")
        routed = {"f0_": (7, 1), "f1_": (9, 2)}
        F = {}
        for pre, (n_exp, choices) in routed.items():
            n_rows = (T * choices + slot_tiles(n_exp, choices)) * P
            F[pre] = dict(w13=w13, w2=w2, outbox=nc.dram_tensor(pre + "outbox", (n_rows, D), F32, kind="Internal").ap())
            F[pre]["wait"] = lambda eng, layer=len(F): eng.wait_ge(experts_loaded, 32 * layer)
            F[pre]["wait_rows"] = lambda eng, layer=len(F): eng.wait_ge(counts.rows_sent, 16 * layer)

        def load_experts(pre):
            def loads(sp):
                n = a[pre + "w13"].shape[1]
                sp.dma_start(w13[:, 0:n, :, :], a[pre + "w13"]).then_inc(experts_loaded, 16)
                sp.dma_start(w2[:, 0:n, :, :], a[pre + "w2"]).then_inc(experts_loaded, 16)
            return loads

        cross_zeroed = sem("cross_zeroed")
        cross = CrossBuffers(nc, cx)
        CS = {n: cross_semaphores(nc, cx, n) for n in ("x0", "x1")}
        CX = {n: dict(W[n + "_"], ctx=a["ctx"]) for n in CS}

        def wait_x(eng, group):
            for n in range(T // 4) if group is None else (group,):
                eng.wait_ge(x_loaded[n], 16)
            if group is None:
                eng.wait_ge(loaded, 16)

        def load_weights(sp, pre):
            for n in stages[pre]:
                sp.dma_start(W[pre][n][tuple(slice(None) for _ in a[pre + n].shape)],
                             a[pre + n]).then_inc(first_loaded if pre == "x0_" else later_loaded, 16)

        with nc.Block() as block:
            @block.sync
            def _(sp):
                for n, done in enumerate(x_loaded):
                    sp.dma_start(X[:, 4 * n:4 * n + 4, :], a["x"][:, 4 * n:4 * n + 4, :]).then_inc(done, 16)
                sp.dma_start(cs[:, :], a["consts"]).then_inc(loaded, 16)
                load_weights(sp, "x0_")

        norms, counts = LayernormCount(nc, cx), RouterCount(nc, cx)
        before, after, first_context = cross_start(nc, CS["x0"], cross, CX["x0"], cross_zeroed)

        def early_loads(sp):
            first_context(sp)
            for pre in stages:
                if pre != "x0_":
                    load_weights(sp, pre)
        layernorm_stage(nc, norms, "n0", X, XNT, con, loads=early_loads, before=before, after=after, wait_x=wait_x)
        cross_attention(nc, cx, norms, "x0", X, XNT, con, CX["x0"], CS["x0"], cross)

        lnwb = W["a0_"]["lnwb"]
        layernorm_stage(nc, norms, "n1", X, XNT, con, twice=(lnwb[:, 0:1], lnwb[:, 1:2]), wait_wb=W["a0_"]["wait"],
                        loads=load_experts("f0_"))
        self_attention(nc, cx, norms, "a0", X, XNT, con, W["a0_"])

        with nc.sbuf_tensor("rows0", [P, T, D], F32) as XR:
            layernorm_stage(nc, norms, "n2", X, XNT, con, rows=XR)
            router(nc, counts, "r0", XNT, XR, R, con, W["r0_"], 7, top2=False, shared=True)
            sparse_experts(nc, cx, counts, norms, "f0", X, XNT, XR, R, con, F["f0_"], 7, 1, shared=True)

        before, after, first_context = cross_start(nc, CS["x1"], cross, CX["x1"])

        def second_loads(sp):
            first_context(sp)
            load_experts("f1_")(sp)
        layernorm_stage(nc, norms, "n3", X, XNT, con, loads=second_loads, before=before, after=after)
        cross_attention(nc, cx, norms, "x1", X, XNT, con, CX["x1"], CS["x1"], cross)

        layernorm_stage(nc, norms, "n4", X, XNT, con)
        rope_attention(nc, cx, norms, "a1", X, XNT, con, W["a1_"])

        with nc.sbuf_tensor("rows1", [P, T, D], F32) as XR:
            def store(sp, tiles):
                sp.dma_start(out[:, tiles, :], X[:, tiles, :]).then_inc(stored, 16)
                if tiles.stop == T:
                    sp.wait_ge(stored, 16 * (T // 4))

            layernorm_stage(nc, norms, "n5", X, XNT, con, rows=XR)
            router(nc, counts, "r1", XNT, XR, R, con, W["r1_"], 9, top2=True, shared=False)
            sparse_experts(nc, cx, counts, norms, "f1", X, XNT, XR, R, con, F["f1_"], 9, 2, shared=False, store=store)


def kernel(**inputs):
    import numpy as np
    import concourse.bacc as bacc
    from concourse.bass_utils import run_bass_kernel_spmd

    i = {k: np.asarray(v) for k, v in inputs.items()}
    f32 = np.float32
    tile = lambda a: np.broadcast_to(a, (P, a.shape[-1]))
    twice = lambda w: np.concatenate([w, w], 0)
    r = np.arange(P)

    qmask = np.zeros((P, J * G), f32)
    qmask[r, G * (r // DH % J) + r // (J * DH)] = 1
    rowmask = (r[None, :] // DH % G == r[:, None] // S).astype(f32)
    causal = np.where(np.tril(np.ones((S, S))) > 0, 0, -3e38).astype(f32)
    half = D // 2
    inv = (1.0 / 10000.0 ** (np.arange(half, dtype=f32) / f32(half))).astype(f32)
    ang = np.arange(S, dtype=f32)[:, None] * inv[None]
    seqmask = (r[:, None] // S == np.arange(BT)[None]).astype(f32)
    consts = {
        "ident": np.eye(P, dtype=f32), "qmask": qmask, "rowmask": rowmask,
        "eye4": np.tile(np.eye(S, dtype=f32), (BT, 1)), "causal": np.tile(causal, (BT, E_H)),
        "rank": tile(np.arange(9, 0, -1).astype(f32)),
        "ones": np.ones((P, P), f32), "before": np.triu(np.ones((P, P), f32), 1),
        "lower": tile(np.tril(np.ones((9, 9), f32), -1).reshape(-1)), "steps": tile(np.arange(40).astype(f32)),
        "places": tile(np.arange(P).astype(f32)), "place": np.arange(1, P + 1, dtype=f32)[:, None],
        "slots": (np.arange(40)[None] * P + r[:, None]).astype(f32), "scalars": tile(np.array([EPS, -0.5], f32)), "cos": np.tile(np.cos(ang), (BT, 2)),
        "sin": np.tile(np.concatenate([-np.sin(ang), np.sin(ang)], 1), (BT, 1)), "seqmask": seqmask,
    }

    rows = np.array([(J * g + j) * DH + d for j in range(J) for g in range(G) for d in range(DH)])
    arrays = {
        "x": i["x"].reshape(T, P, D).transpose(1, 0, 2),
        "consts": np.concatenate([consts[n] for n, _ in CONSTS], 1),
        "ctx": np.pad(i["ctx_512"].transpose(2, 0, 1), ((0, 0), (0, 0), (0, KVP - KV))),
    }

    def cross(pre, wq, wk, wv, wo):
        arrays[pre + "wq"], arrays[pre + "wo"] = wq, wo[rows]
        arrays[pre + "wkvv"] = np.stack([twice(wk), twice(wv), twice(wv[:, rows])], 1)

    cross("x0_", *(i[f"L0_xattn_W{c}"] for c in "qkvo"))
    bq, bk, bv, bo = (i[f"L0_xattn_b{c}"] for c in "qkvo")
    arrays["x0_bias"], arrays["x0_bo"] = np.stack([bq, bk, bv, bv[rows]], 1), tile(bo)
    wkv = i["L1_xattn_Wkv"]
    cross("x1_", i["L1_xattn_Wq"].T, wkv[:D].T, wkv[D:].T, i["L1_xattn_Wo"].T)

    heads = lambda w: w.transpose(1, 0, 2).reshape(D, E_H * E_D)
    arrays["a0_lnwb"] = np.stack([i["L0_attn_ln_w"], i["L0_attn_ln_b"]], 1)
    arrays["a0_wqkv"] = np.stack([heads(i[f"L0_attn_W_{c}"]) for c in "qkv"], 1)
    arrays["a0_wo"] = i["L0_attn_W_o"].reshape(E_H // 2, P, D).transpose(1, 0, 2)
    arrays["a0_bqk"] = np.stack([i[f"L0_attn_b_{c}"].reshape(E_H // 2, P).T for c in "qk"], 1)
    arrays["a0_bv"] = tile(i["L0_attn_b_v"].reshape(-1))
    arrays["a0_bo"] = tile(i["L0_attn_b_o"])

    arrays["a1_wqkv"], arrays["a1_wo"] = i["L1_attn_w_qkv"].T, i["L1_attn_w_o"].T
    arrays["a1_bqkv"], arrays["a1_bo"] = tile(i["L1_attn_b_qkv"]), tile(i["L1_attn_b_o"])

    def experts(pre, w1, w2, w3, rw, rb):
        pad = P * len(CH) - I_FF
        up = np.stack([w1.transpose(2, 0, 1), w3.transpose(2, 0, 1)], 2)
        arrays[pre + "w13"] = np.pad(up, ((0, 0), (0, 0), (0, 0), (0, pad)))
        down = np.pad(w2.transpose(0, 2, 1), ((0, 0), (0, pad), (0, 0))).reshape(len(w2), len(CH), P, D)
        arrays[pre + "w2"] = down.transpose(2, 0, 1, 3)
        arrays[pre.replace("f", "r") + "rw"], arrays[pre.replace("f", "r") + "rb"] = rw.T, tile(rb)

    join = lambda *n: np.concatenate([i[k] if i[k].ndim != 2 or "gate" in k else i[k][None] for k in n])
    experts("f0_", *(join(f"L0_ffn_ew{m}", f"L0_ffn_sw{m}") for m in (1, 2, 3)),
            i["L0_ffn_router_w"], i["L0_ffn_routing_bias"])
    experts("f1_", *(join(f"L1_ffn_w{m}", f"L1_ffn_new_w{m}") for m in (1, 2, 3)),
            join("L1_ffn_gate_weight", "L1_ffn_new_gate_weight"), np.pad(i["L1_ffn_gate_bias"], (8, 0)))

    nc = bacc.Bacc("TRN2", target_bir_lowering=False, num_devices=1)
    arrays = {f"in_{n}": np.ascontiguousarray(v, dtype=f32) for n, v in arrays.items()}
    aps = {n[3:]: nc.dram_tensor(n, v.shape, F32, kind="ExternalInput").ap() for n, v in arrays.items()}
    out = nc.dram_tensor("out", (P, T, D), F32, kind="ExternalOutput").ap()
    perceiver(nc, aps, out)
    got = run_bass_kernel_spmd(nc, [arrays], core_ids=[0]).results[0]["out"]
    return got.transpose(1, 0, 2).reshape(B, S, D)
```
